# Optimizing a Trainium2 kernel written in Bass

```python
import numpy as np
import jax
import jax.numpy as jnp

def _softmax(x, axis=-1):
    return jax.nn.softmax(x, axis=axis)

def _gelu(x):
    return jax.nn.gelu(x, approximate=True)

def _silu(x):
    return jax.nn.silu(x)

def _sigmoid(x):
    return jax.nn.sigmoid(x)

def _layernorm(x, axis=-1, eps=1e-05):
    m = jnp.mean(x, axis=axis, keepdims=True)
    v = jnp.var(x, axis=axis, keepdims=True)
    return (x - m) / jnp.sqrt(v + eps)

def _scatter_add(tgt, idx, src, axis=0):
    return tgt.at[idx].add(src)

def _segment_sum(src, seg, n):
    return jax.ops.segment_sum(src, seg, n)
kernel_name = 'mk_gnn_preln_d4_gnn_r32_a25cd8'

def setup_inputs(seed: int=0):
    np.random.seed(seed)
    _w = jnp.asarray

    def _rec_inputs():
        import jax
        import jax.numpy as jnp
        _gk = jax.random.key(seed)
        x = -0.000202 + 1 * jax.random.normal(jax.random.fold_in(_gk, 1), (3125, 128), jnp.float32)
        src = jax.random.randint(jax.random.fold_in(_gk, 2), (100000,), 0, 3125, jnp.int32)
        dst = jnp.minimum((3125 * jax.random.uniform(jax.random.fold_in(_gk, 3), (100000,)) ** 2.0).astype(jnp.int32), 99999)
        _o = jnp.argsort(dst, stable=True)
        src = src[_o]
        dst = dst[_o]
        edge_attr_50 = 0.000152336 + 1.00009 * jax.random.normal(jax.random.fold_in(_gk, 12), (100000, 50), jnp.float32)
        edge_type_8 = jax.random.randint(jax.random.fold_in(_gk, 14), (100000,), 0, 8, jnp.int32)
        edge_weight = jax.random.uniform(jax.random.fold_in(_gk, 15), (100000,), jnp.float32, 0.0, 0.999998)
        return (x, src, dst, edge_attr_50, edge_type_8, edge_weight)
    x, src, dst, edge_attr_50, edge_type_8, edge_weight = _rec_inputs()

    def _L0_gnn_setup():
        import jax, jax.numpy as jnp
        import numpy as np
        N, E, IN, H, OUT = (50000, 25000, 128, 256, 128)
        BN_EPS = 1e-05

        def _sage_conv(x, edge_index, Wl, bl, Wr):
            src, dst = (edge_index[0], edge_index[1])
            n = x.shape[0]
            agg = jax.ops.segment_sum(x[src], dst, num_segments=n)
            cnt = jax.ops.segment_sum(jnp.ones((src.shape[0],), x.dtype), dst, num_segments=n)
            mean = agg / jnp.maximum(cnt, 1.0)[:, None]
            return mean @ Wl + bl + x @ Wr

        def _batchnorm(x, gamma, beta):
            m = jnp.mean(x, axis=0)
            v = jnp.var(x, axis=0)
            return (x - m) * jax.lax.rsqrt(v + BN_EPS) * gamma + beta
        key = jax.random.key(seed)
        ks = jax.random.split(key, 10)
        x = jax.random.normal(ks[0], (N, IN), dtype=jnp.float32)
        edge_index = jax.random.randint(ks[1], (2, E), 0, N, dtype=jnp.int64)
        s1 = 1.0 / np.sqrt(IN)
        s2 = 1.0 / np.sqrt(H)
        return {'x': x, 'edge_index': edge_index, 'W1l': jax.random.normal(ks[2], (IN, H), dtype=jnp.float32) * s1, 'b1': jax.random.normal(ks[3], (H,), dtype=jnp.float32) * s1, 'W1r': jax.random.normal(ks[4], (IN, H), dtype=jnp.float32) * s1, 'gamma': jnp.ones((H,), dtype=jnp.float32), 'beta': jnp.zeros((H,), dtype=jnp.float32), 'W2l': jax.random.normal(ks[5], (H, OUT), dtype=jnp.float32) * s2, 'b2': jax.random.normal(ks[6], (OUT,), dtype=jnp.float32) * s2, 'W2r': jax.random.normal(ks[7], (H, OUT), dtype=jnp.float32) * s2}
    _L0_gnn_all = _L0_gnn_setup()
    _L0_gnn_in = {k: v for k, v in _L0_gnn_all.items() if k in ('W1l', 'b1', 'W1r', 'gamma', 'beta', 'W2l', 'b2', 'W2r')}
    del _L0_gnn_all

    def _L1_gnn_setup():
        import jax, jax.numpy as jnp
        import numpy as np
        PI = float(np.pi)
        SHIFT = float(np.log(2.0))
        CUTOFF = 10.0
        N_NODES = 3125
        N_EDGES = 20000
        HIDDEN = 128
        NFILT = 128
        NGAUSS = 50

        def ssp(x):
            return jax.nn.softplus(x) - SHIFT
        key = jax.random.key(seed)
        ks = jax.random.split(key, 12)
        x = jax.random.normal(ks[0], (N_NODES, HIDDEN), dtype=jnp.float32)
        edge_index = jax.random.randint(ks[1], (2, N_EDGES), 0, N_NODES, dtype=jnp.int64)
        edge_weight = jax.random.uniform(ks[2], (N_EDGES,), dtype=jnp.float32)
        edge_attr = jax.random.normal(ks[3], (N_EDGES, NGAUSS), dtype=jnp.float32)

        def xav(k, shape):
            fan_in, fan_out = (shape[0], shape[1])
            lim = np.sqrt(6.0 / (fan_in + fan_out))
            return jax.random.uniform(k, shape, dtype=jnp.float32, minval=-lim, maxval=lim)
        mlp_w1 = xav(ks[4], (NGAUSS, NFILT))
        mlp_b1 = jnp.zeros((NFILT,), dtype=jnp.float32)
        mlp_w2 = xav(ks[5], (NFILT, NFILT))
        mlp_b2 = jnp.zeros((NFILT,), dtype=jnp.float32)
        lin1_w = xav(ks[6], (HIDDEN, NFILT))
        lin2_w = xav(ks[7], (NFILT, HIDDEN))
        lin2_b = jnp.zeros((HIDDEN,), dtype=jnp.float32)
        lin_w = xav(ks[8], (HIDDEN, HIDDEN))
        lin_b = jnp.zeros((HIDDEN,), dtype=jnp.float32)
        return {'x': x, 'edge_index': edge_index, 'edge_weight': edge_weight, 'edge_attr': edge_attr, 'mlp_w1': mlp_w1, 'mlp_b1': mlp_b1, 'mlp_w2': mlp_w2, 'mlp_b2': mlp_b2, 'lin1_w': lin1_w, 'lin2_w': lin2_w, 'lin2_b': lin2_b, 'lin_w': lin_w, 'lin_b': lin_b}
    _L1_gnn_all = _L1_gnn_setup()
    _L1_gnn_in = {k: v for k, v in _L1_gnn_all.items() if k in ('mlp_w1', 'mlp_b1', 'mlp_w2', 'mlp_b2', 'lin1_w', 'lin2_w', 'lin2_b', 'lin_w', 'lin_b')}
    del _L1_gnn_all

    def _L2_gnn_setup():
        import jax, jax.numpy as jnp
        import numpy as np
        N_ENT = 3125

        def _rgcn_layer(x, W, SW, b, src, dst, rel):
            xt = jnp.einsum('nd,rde->rne', x, W)
            msg = xt[rel, src]
            agg = jax.ops.segment_sum(msg, dst, num_segments=x.shape[0])
            return jax.nn.relu(agg + x @ SW + b)
        key = jax.random.key(seed)
        ks = jax.random.split(key, 8)
        d, R, E = (128, 8, 18750)
        scale = 1.0 / np.sqrt(d)
        return {'entity_emb': jax.random.normal(ks[0], (N_ENT, d), dtype=jnp.float32), 'w1': jax.random.normal(ks[1], (R, d, d), dtype=jnp.float32) * scale, 'sl1': jax.random.normal(ks[2], (d, d), dtype=jnp.float32) * scale, 'b1': jnp.zeros((d,), dtype=jnp.float32), 'w2': jax.random.normal(ks[3], (R, d, d), dtype=jnp.float32) * scale, 'sl2': jax.random.normal(ks[4], (d, d), dtype=jnp.float32) * scale, 'b2': jnp.zeros((d,), dtype=jnp.float32), 'edge_index': jax.random.randint(ks[5], (2, E), 0, N_ENT, dtype=jnp.int64), 'edge_type': jax.random.randint(ks[6], (E,), 0, R, dtype=jnp.int64)}
    _L2_gnn_all = _L2_gnn_setup()
    _L2_gnn_in = {k: v for k, v in _L2_gnn_all.items() if k in ('w1', 'sl1', 'b1', 'w2', 'sl2', 'b2')}
    del _L2_gnn_all

    def _L3_gnn_setup():
        import jax, jax.numpy as jnp
        import numpy as np
        N_NODES = 3125
        N_EDGES = 50000
        N_FEAT = 128
        N_CH = 128
        key = jax.random.key(seed)
        k1, k2, k3, k4, k5, k6, k7 = jax.random.split(key, 7)
        features = jax.random.normal(k1, (N_NODES, N_FEAT), dtype=jnp.float32)
        kernel = jax.random.normal(k2, (N_FEAT, N_CH), dtype=jnp.float32) * (1.0 / np.sqrt(N_FEAT))
        bias = jax.random.normal(k3, (N_CH,), dtype=jnp.float32) * 0.02
        skip_weight = jax.random.normal(k4, (N_CH,), dtype=jnp.float32)
        edge_weight = jax.random.uniform(k5, (N_EDGES,), dtype=jnp.float32)
        edge_src = jax.random.randint(k6, (N_EDGES,), 0, N_NODES, dtype=jnp.int64 if jax.config.jax_enable_x64 else jnp.int32)
        edge_dst = jax.random.randint(k7, (N_EDGES,), 0, N_NODES, dtype=jnp.int64 if jax.config.jax_enable_x64 else jnp.int32)
        return {'features': features, 'kernel': kernel, 'bias': bias, 'skip_weight': skip_weight, 'edge_weight': edge_weight, 'edge_src': edge_src, 'edge_dst': edge_dst}
    _L3_gnn_all = _L3_gnn_setup()
    _L3_gnn_in = {k: v for k, v in _L3_gnn_all.items() if k in ('kernel', 'bias', 'skip_weight')}
    del _L3_gnn_all
    return {'x': x, 'src': src, 'dst': dst, 'edge_attr_50': edge_attr_50, 'edge_type_8': edge_type_8, 'edge_weight': edge_weight, 'L0_gnn_W1l': _L0_gnn_in['W1l'], 'L0_gnn_b1': _L0_gnn_in['b1'], 'L0_gnn_W1r': _L0_gnn_in['W1r'], 'L0_gnn_gamma': _L0_gnn_in['gamma'], 'L0_gnn_beta': _L0_gnn_in['beta'], 'L0_gnn_W2l': _L0_gnn_in['W2l'], 'L0_gnn_b2': _L0_gnn_in['b2'], 'L0_gnn_W2r': _L0_gnn_in['W2r'], 'L1_gnn_mlp_w1': _L1_gnn_in['mlp_w1'], 'L1_gnn_mlp_b1': _L1_gnn_in['mlp_b1'], 'L1_gnn_mlp_w2': _L1_gnn_in['mlp_w2'], 'L1_gnn_mlp_b2': _L1_gnn_in['mlp_b2'], 'L1_gnn_lin1_w': _L1_gnn_in['lin1_w'], 'L1_gnn_lin2_w': _L1_gnn_in['lin2_w'], 'L1_gnn_lin2_b': _L1_gnn_in['lin2_b'], 'L1_gnn_lin_w': _L1_gnn_in['lin_w'], 'L1_gnn_lin_b': _L1_gnn_in['lin_b'], 'L2_gnn_w1': _L2_gnn_in['w1'], 'L2_gnn_sl1': _L2_gnn_in['sl1'], 'L2_gnn_b1': _L2_gnn_in['b1'], 'L2_gnn_w2': _L2_gnn_in['w2'], 'L2_gnn_sl2': _L2_gnn_in['sl2'], 'L2_gnn_b2': _L2_gnn_in['b2'], 'L3_gnn_kernel': _L3_gnn_in['kernel'], 'L3_gnn_bias': _L3_gnn_in['bias'], 'L3_gnn_skip_weight': _L3_gnn_in['skip_weight']}

def reference(x, src, dst, edge_attr_50, edge_type_8, edge_weight, L0_gnn_W1l, L0_gnn_b1, L0_gnn_W1r, L0_gnn_gamma, L0_gnn_beta, L0_gnn_W2l, L0_gnn_b2, L0_gnn_W2r, L1_gnn_mlp_w1, L1_gnn_mlp_b1, L1_gnn_mlp_w2, L1_gnn_mlp_b2, L1_gnn_lin1_w, L1_gnn_lin2_w, L1_gnn_lin2_b, L1_gnn_lin_w, L1_gnn_lin_b, L2_gnn_w1, L2_gnn_sl1, L2_gnn_b1, L2_gnn_w2, L2_gnn_sl2, L2_gnn_b2, L3_gnn_kernel, L3_gnn_bias, L3_gnn_skip_weight):
    import jax
    import jax.numpy as jnp

    def _L0_gnn_ref(x, edge_index, W1l, b1, W1r, gamma, beta, W2l, b2, W2r):
        import jax, jax.numpy as jnp
        import numpy as np
        N, E, IN, H, OUT = (50000, 25000, 128, 256, 128)
        BN_EPS = 1e-05

        def _sage_conv(x, edge_index, Wl, bl, Wr):
            src, dst = (edge_index[0], edge_index[1])
            n = x.shape[0]
            agg = jax.ops.segment_sum(x[src], dst, num_segments=n)
            cnt = jax.ops.segment_sum(jnp.ones((src.shape[0],), x.dtype), dst, num_segments=n)
            mean = agg / jnp.maximum(cnt, 1.0)[:, None]
            return mean @ Wl + bl + x @ Wr

        def _batchnorm(x, gamma, beta):
            m = jnp.mean(x, axis=0)
            v = jnp.var(x, axis=0)
            return (x - m) * jax.lax.rsqrt(v + BN_EPS) * gamma + beta
        h = _sage_conv(x, edge_index, W1l, b1, W1r)
        h = jax.nn.relu(_batchnorm(h, gamma, beta))
        out = _sage_conv(h, edge_index, W2l, b2, W2r)
        return out

    def _L1_gnn_ref(x, edge_index, edge_weight, edge_attr, mlp_w1, mlp_b1, mlp_w2, mlp_b2, lin1_w, lin2_w, lin2_b, lin_w, lin_b):
        import jax, jax.numpy as jnp
        import numpy as np
        PI = float(np.pi)
        SHIFT = float(np.log(2.0))
        CUTOFF = 10.0
        N_NODES = 3125
        N_EDGES = 20000
        HIDDEN = 128
        NFILT = 128
        NGAUSS = 50

        def ssp(x):
            return jax.nn.softplus(x) - SHIFT
        C = 0.5 * (jnp.cos(edge_weight * PI / CUTOFF) + 1.0)
        h = ssp(edge_attr @ mlp_w1 + mlp_b1)
        W = (h @ mlp_w2 + mlp_b2) * C[:, None]
        xp = x @ lin1_w
        src, dst = (edge_index[0], edge_index[1])
        msg = xp[src] * W
        agg = jax.ops.segment_sum(msg, dst, num_segments=x.shape[0])
        out = agg @ lin2_w + lin2_b
        out = ssp(out)
        out = out @ lin_w + lin_b
        return out

    def _L2_gnn_ref(entity_emb, w1, sl1, b1, w2, sl2, b2, edge_index, edge_type):
        import jax, jax.numpy as jnp
        import numpy as np
        N_ENT = 3125

        def _rgcn_layer(x, W, SW, b, src, dst, rel):
            xt = jnp.einsum('nd,rde->rne', x, W)
            msg = xt[rel, src]
            agg = jax.ops.segment_sum(msg, dst, num_segments=x.shape[0])
            return jax.nn.relu(agg + x @ SW + b)
        src, dst = (edge_index[0], edge_index[1])
        x = _rgcn_layer(entity_emb, w1, sl1, b1, src, dst, edge_type)
        x = _rgcn_layer(x, w2, sl2, b2, src, dst, edge_type)
        return x

    def _L3_gnn_ref(features, kernel, bias, skip_weight, edge_weight, edge_src, edge_dst):
        import jax, jax.numpy as jnp
        import numpy as np
        N_NODES = 3125
        N_EDGES = 50000
        N_FEAT = 128
        N_CH = 128
        h = jnp.matmul(features, kernel)
        msg = h[edge_src] * edge_weight[:, None]
        agg = jax.ops.segment_sum(msg, edge_dst, num_segments=features.shape[0])
        out = h * skip_weight + agg + bias
        return jax.nn.selu(out)
    edge_index = jnp.stack([src, dst])
    h = jnp.maximum(_layernorm(x, axis=-1), 0.0)
    x = x + _L0_gnn_ref(h, edge_index, L0_gnn_W1l, L0_gnn_b1, L0_gnn_W1r, L0_gnn_gamma, L0_gnn_beta, L0_gnn_W2l, L0_gnn_b2, L0_gnn_W2r)
    h = jnp.maximum(_layernorm(x, axis=-1), 0.0)
    x = x + _L1_gnn_ref(h, edge_index, edge_weight, edge_attr_50, L1_gnn_mlp_w1, L1_gnn_mlp_b1, L1_gnn_mlp_w2, L1_gnn_mlp_b2, L1_gnn_lin1_w, L1_gnn_lin2_w, L1_gnn_lin2_b, L1_gnn_lin_w, L1_gnn_lin_b)
    h = jnp.maximum(_layernorm(x, axis=-1), 0.0)
    x = x + _L2_gnn_ref(h, L2_gnn_w1, L2_gnn_sl1, L2_gnn_b1, L2_gnn_w2, L2_gnn_sl2, L2_gnn_b2, edge_index, edge_type_8)
    h = jnp.maximum(_layernorm(x, axis=-1), 0.0)
    x = x + _L3_gnn_ref(h, L3_gnn_kernel, L3_gnn_bias, L3_gnn_skip_weight, edge_weight, src, dst)
    return x

_drawn_inputs = setup_inputs


def setup_inputs(seed=0):
    import zlib

    import numpy as np

    out = dict(_drawn_inputs(seed))
    spreads = {'L0_gnn_gamma': (1.0, 0.2),
     'L0_gnn_beta': (0.0, 0.1),
     'L1_gnn_mlp_b1': (0.0, 0.1),
     'L1_gnn_mlp_b2': (0.0, 0.1),
     'L1_gnn_lin2_b': (0.0, 0.354),
     'L1_gnn_lin_b': (0.0, 0.1),
     'L2_gnn_b1': (0.0, 0.658),
     'L2_gnn_b2': (0.0, 2.0)}
    factors = {'edge_weight': 3.791,
     'L0_gnn_W1l': 3.691,
     'L0_gnn_b1': 200.0,
     'L3_gnn_bias': 200.0,
     'L3_gnn_skip_weight': 5.327}
    for name, (base, spread) in spreads.items():
        noise = np.random.default_rng([zlib.crc32(name.encode()), seed]).standard_normal(out[name].shape)
        drawn = base * np.exp(spread * noise) if base else spread * noise
        out[name] = jnp.asarray(drawn.astype(out[name].dtype))
    for name, factor in factors.items():
        out[name] = (out[name] * factor).astype(out[name].dtype)
    return out
```

```python
import concourse.bass as bass
from concourse import mybir
from contextlib import ExitStack
import numpy as np

fp32 = mybir.dt.float32
bf16 = mybir.dt.bfloat16
i32 = mybir.dt.int32
ALU = mybir.AluOpType
ACT = mybir.ActivationFunctionType
AX = mybir.AxisListType

N_NODES = 3125
N_EDGES = 100000
D = 128
H2 = 2
N_GAUSS = 50
N_REL = 8
P = 128
N_TILES = -(-N_NODES // P)
NODES = N_TILES * P
CHUNK = P
GROUP = 4
G_EDGES = CHUNK * GROUP
SLOTS = 4
N_GROUPS = -(-N_EDGES // G_EDGES)
TURNS = N_GROUPS // SLOTS
EDGES = N_GROUPS * G_EDGES
AHEAD = N_GROUPS + SLOTS
WIN = 64
AGG = NODES + WIN
BANK = 512
COLS = [(c, min(BANK, NODES - c)) for c in range(0, NODES, BANK)]
QUADS = [(t, min(4, N_TILES - t)) for t in range(0, N_TILES, 4)]
MIN_ROWS = N_GROUPS // 2
LN_EPS = 1e-5
LN2 = float(np.log(2.0))
EXP_CAP = 30.0
SELU_SCALE = 1.0507009873554805
SELU_ALPHA = 1.6732632423543772
assert N_GROUPS % SLOTS == 0 and N_GROUPS % 2 == 0


class Tally:

    def __init__(self, sem):
        self.sem, self.value = sem, 0

    def at(self, n):
        return self.value + n

    def passed(self, n):
        self.value += n


def build_gnn(nc, a, out):
    with ExitStack() as ctx:
        def sb(name, shape, dt=fp32):
            return ctx.enter_context(nc.sbuf_tensor(name, shape, dt))

        def tally(name):
            return Tally(ctx.enter_context(nc.semaphore(name)))

        def scratch(name, shape, dt=fp32):
            return nc.dram_tensor(name, shape, dt, kind="Internal").ap()

        table = scratch("table", (NODES, D))
        rel_table = scratch("rel_table", (NODES * N_REL, D))
        min_dram = scratch("min_dram", (2, N_GROUPS))

        x_rows = sb("x_rows", [P, N_TILES, D])
        h_rows = sb("h_rows", [P, N_TILES, D])
        h_cols = sb("h_cols", [P, H2, NODES])
        m_cols = sb("m_cols", [P, NODES])
        agg = sb("agg", [P, 2, AGG])
        src_idx = sb("src_idx", [P, AHEAD * GROUP], i32)
        rel_idx = sb("rel_idx", [P, AHEAD * GROUP], i32)
        dst_rel = sb("dst_rel", [P, N_GROUPS * GROUP])
        e_weight = sb("e_weight", [P, N_GROUPS * GROUP])
        e_cut = sb("e_cut", [P, N_GROUPS * GROUP])
        base_row = sb("base_row", [P, N_GROUPS])
        base_i = sb("base_i", [1, N_GROUPS], i32)
        passes_i = sb("passes_i", [1, 1], i32)
        iota_f = sb("iota_f", [P, NODES])
        cur_idx = sb("cur_idx", [P, SLOTS, GROUP], i32)
        rows = sb("rows", [P, SLOTS, GROUP, D])
        onehot = sb("onehot", [P, GROUP, WIN])
        attr = sb("attr", [N_GAUSS, SLOTS, G_EDGES])
        soft = sb("soft", [P, 2, G_EDGES])
        filt = sb("filt", [P, 2, G_EDGES])
        ident = sb("ident", [P, P])
        ones = sb("ones", [P, P])
        eps_t = sb("eps_t", [P, 1])
        w1lr = sb("w1lr", [P, 2, H2 * D])
        w2lr = sb("w2lr", [P, H2, 2 * D])
        bn_vec = sb("bn_vec", [P, 3, H2])
        mlp_w1 = sb("mlp_w1", [N_GAUSS, D])
        sq_w = sb("sq_w", [P, 7, D])
        MLP2, LIN1, LIN2, LIN, SL1, SL2, KER = range(7)
        rel_w = sb("rel_w", [P, 2, N_REL * D])
        vecs = sb("vecs", [P, 6])
        MLP_B1, LIN2_B, R_B1, R_B2, BIAS, SKIP = range(6)
        row_vecs = sb("row_vecs", [P, 3, D])
        L0_B2, LIN_B, MLP_B2 = range(3)
        b2_parts = sb("b2_parts", [P, 3, D])
        b2_left = sb("b2_left", [P, 2, D])
        b2_split = sb("b2_split", [P, GROUP, D], bf16)
        three_ones = sb("three_ones", [P, P], bf16)
        stats = sb("stats", [P, N_TILES, 6])
        mean_var = sb("mean_var", [P, N_TILES, 2])
        ln_std = sb("ln_std", [P, N_TILES])
        ln_scale = sb("ln_scale", [P, N_TILES])
        ln_shift = sb("ln_shift", [P, N_TILES])
        dst_raw = agg[:, 0, 0:N_GROUPS * GROUP].bitcast(i32)
        dst_f = agg[:, 1, 0:N_GROUPS * GROUP]
        dst_groups_i = m_cols[0:MIN_ROWS, 0:2 * G_EDGES].rearrange("p (j e) -> p j e", j=2).bitcast(i32)
        dst_groups = m_cols[0:MIN_ROWS, 2 * G_EDGES:4 * G_EDGES].rearrange("p (j e) -> p j e", j=2)
        dst_lift = h_cols[0:MIN_ROWS, 0, 0:2 * G_EDGES].rearrange("p (j e) -> p j e", j=2)
        span = sb("span", [MIN_ROWS, 2, 2])
        span_row = sb("span_row", [1, N_GROUPS])
        span_max = sb("span_max", [1, 1])
        max_row = sb("max_row", [1, N_GROUPS])
        type_i = h_cols[:, 0, 1024:1024 + AHEAD * GROUP].bitcast(i32)
        cyc = h_cols[:, 1, 0:N_GROUPS * GROUP]
        cyc_round = h_cols[:, 1, 1024:1024 + N_GROUPS * GROUP]
        iota_i = h_rows[:, :, :].rearrange("p t f -> p (t f)").bitcast(i32)

        ps = [ctx.enter_context(nc.psum_tensor(f"ps{i}", [P, BANK], fp32)) for i in range(8)]

        loaded = tally("loaded")
        edges_in = tally("edges_in")
        chain_v = tally("chain_v")
        chain_s = tally("chain_s")
        chain_g = tally("chain_g")
        made_t = tally("made_t")
        taken_v = tally("taken_v")
        taken_s = tally("taken_s")
        rows_done = tally("rows_done")
        stored = tally("stored")
        stage_out = [tally(f"stage_out{i}") for i in range(3)]
        prepared = tally("prepared")
        wanted = tally("wanted")
        input_v = tally("input_v")
        idx_ready = tally("idx_ready")
        turn_begun = tally("turn_begun")
        gathered = [tally(f"gathered{i}") for i in range(SLOTS)]
        onehot_ready = tally("onehot_ready")
        scattered = tally("scattered")
        summed = tally("summed")
        attr_in = [tally(f"attr_in{i}") for i in range(SLOTS)]
        z_ready = tally("z_ready")
        z_capped = tally("z_capped")
        ln_ready = tally("ln_ready")
        filt_ready = tally("filt_ready")
        w_ready = tally("w_ready")
        weighed = tally("weighed")

        def link(ins, t, eng):
            ins.then_inc(t.sem, 1)
            t.passed(1)
            eng.wait_ge(t.sem, t.value)

        def prepare():
            with nc.Block() as block:
                @block.sync
                def _(sp):
                    sp.dma_start(dst_groups_i, a["dst"].rearrange("(p j e) -> p j e", j=2, e=G_EDGES)).then_inc(edges_in.sem, 16)
                    sp.dma_start(dst_raw, a["dst_cols"]).then_inc(edges_in.sem, 16)
                    sp.dma_start(x_rows[:, :, :], a["x"].rearrange("(t p) f -> p t f", p=P)).then_inc(loaded.sem, 16)
                    sp.dma_start(src_idx[:, :], a["src_cols"]).then_inc(edges_in.sem, 16)
                    sp.dma_start(type_i, a["type_cols"]).then_inc(edges_in.sem, 16)
                    sp.dma_start(e_weight[:, :], a["weight_cols"]).then_inc(edges_in.sem, 16)
                    n = 1
                    for dst, src in (
                        (w1lr[:, 0, :], a["L0_gnn_W1l"]), (w1lr[:, 1, :], a["L0_gnn_W1r"]),
                        (w2lr[:, :, 0:D], a["L0_gnn_W2l"].rearrange("(c p) m -> p c m", p=P)),
                        (w2lr[:, :, D:2 * D], a["L0_gnn_W2r"].rearrange("(c p) m -> p c m", p=P)),
                        (mlp_w1[:, :], a["L1_gnn_mlp_w1"]), (sq_w[:, MLP2, :], a["L1_gnn_mlp_w2"]),
                        (sq_w[:, LIN1, :], a["L1_gnn_lin1_w"]), (sq_w[:, LIN2, :], a["L1_gnn_lin2_w"]),
                        (sq_w[:, LIN, :], a["L1_gnn_lin_w"]), (sq_w[:, SL1, :], a["L2_gnn_sl1"]),
                        (sq_w[:, SL2, :], a["L2_gnn_sl2"]), (sq_w[:, KER, :], a["L3_gnn_kernel"]),
                        (rel_w[:, 0, :].rearrange("p (r m) -> p r m", r=N_REL), a["L2_gnn_w1"].rearrange("r p m -> p r m")),
                        (rel_w[:, 1, :].rearrange("p (r m) -> p r m", r=N_REL), a["L2_gnn_w2"].rearrange("r p m -> p r m")),
                        (vecs[:, MLP_B1:MLP_B1 + 1], a["L1_gnn_mlp_b1"][:, None]),
                        (vecs[:, LIN2_B:LIN2_B + 1], a["L1_gnn_lin2_b"][:, None]),
                        (vecs[:, R_B1:R_B1 + 1], a["L2_gnn_b1"][:, None]), (vecs[:, R_B2:R_B2 + 1], a["L2_gnn_b2"][:, None]),
                        (vecs[:, BIAS:BIAS + 1], a["L3_gnn_bias"][:, None]), (vecs[:, SKIP:SKIP + 1], a["L3_gnn_skip_weight"][:, None]),
                        (row_vecs[:, L0_B2, :], a["L0_gnn_b2"][None, :].broadcast_to([P, D])),
                        (row_vecs[:, LIN_B, :], a["L1_gnn_lin_b"][None, :].broadcast_to([P, D])),
                        (row_vecs[:, MLP_B2, :], a["L1_gnn_mlp_b2"][None, :].broadcast_to([P, D])),
                    ):
                        sp.dma_start(dst, src).then_inc(loaded.sem, 16)
                        n += 1
                    for i, name in enumerate(("L0_gnn_b1", "L0_gnn_gamma", "L0_gnn_beta")):
                        for c in range(H2):
                            sp.dma_start(bn_vec[:, i, c:c + 1], a[name][c * P:(c + 1) * P, None]).then_inc(loaded.sem, 16)
                            n += 1
                    sp.wait_ge(prepared.sem, 1)
                    sp.dma_start(min_dram[0, :].rearrange("(p j) -> p j", j=2), span[:, 0, :]).then_inc(stored.sem, 16)
                    sp.dma_start(min_dram[1, :].rearrange("(p j) -> p j", j=2), span[:, 1, :]).then_inc(stored.sem, 16)
                    sp.wait_ge(stored.sem, 32)
                    sp.dma_start(base_row[:, :], min_dram[0:1, :].broadcast_to([P, N_GROUPS])).then_inc(stage_out[0].sem, 16)
                    sp.dma_start(max_row[:, :], min_dram[1:2, :]).then_inc(stage_out[0].sem, 16)
                    sp.wait_ge(loaded.sem, 16 * n)
                    loaded.passed(16 * n)

                @block.gpsimd
                def _(pool):
                    link(nc.gpsimd.memset(ident[:, :], 0.0), chain_g, pool)
                    link(nc.gpsimd.affine_select(out=ident[:, :], in_=ident[:, :], compare_op=ALU.not_equal, fill=1.0,
                                                 base=0, pattern=[[-1, P]], channel_multiplier=1), chain_g, pool)
                    link(nc.gpsimd.memset(ones[:, :], 1.0), chain_g, pool)
                    link(nc.gpsimd.memset(eps_t[:, :], LN_EPS), chain_g, pool)
                    link(nc.gpsimd.memset(b2_split[:, :, :], 0.0), chain_g, pool)
                    link(nc.gpsimd.memset(three_ones[:, :], 1.0), chain_g, pool)
                    link(nc.gpsimd.affine_select(out=three_ones[:, :], in_=three_ones[:, :], compare_op=ALU.is_gt, fill=0.0,
                                                 base=3, pattern=[[0, P]], channel_multiplier=-1), chain_g, pool)
                    nc.gpsimd.iota(iota_i, pattern=[[1, NODES]], base=0, channel_multiplier=0).then_inc(wanted.sem, 1)

                @block.scalar
                def _(act):
                    act.wait_ge(input_v.sem, 1)
                    nc.scalar.activation(cyc, cyc, ACT.Sin, scale=float(np.pi)).then_inc(taken_s.sem, 1)

                @block.vector
                def _(dve):
                    dve.wait_ge(edges_in.sem, 80)
                    link(nc.vector.tensor_copy(dst_groups, dst_groups_i), chain_v, dve)
                    link(nc.vector.tensor_scalar(dst_lift, dst_groups, 0.0, float(NODES), ALU.is_lt, ALU.mult), chain_v, dve)
                    link(nc.vector.tensor_tensor(dst_lift, dst_lift, dst_groups, ALU.add), chain_v, dve)
                    link(nc.vector.tensor_reduce(span[:, 0, :], dst_lift, AX.X, ALU.min), chain_v, dve)
                    nc.vector.tensor_reduce(span[:, 1, :], dst_groups, AX.X, ALU.max).then_inc(prepared.sem, 1)
                    link(nc.vector.tensor_scalar(cyc, e_weight[:, :], 1.0 / 20.0, None, ALU.mult), chain_v, dve)
                    link(nc.vector.tensor_scalar(cyc_round, cyc, 12582912.0, None, ALU.add), chain_v, dve)
                    link(nc.vector.tensor_scalar(cyc_round, cyc_round, 12582912.0, None, ALU.subtract), chain_v, dve)
                    nc.vector.tensor_tensor(cyc, cyc, cyc_round, ALU.subtract).then_inc(input_v.sem, 1)
                    link(nc.vector.tensor_scalar(rel_idx[:, :], src_idx[:, :], float(N_REL), None, ALU.mult), chain_v, dve)
                    link(nc.vector.tensor_tensor(rel_idx[:, :], rel_idx[:, :], type_i, ALU.add), chain_v, dve)
                    link(nc.vector.tensor_copy(dst_f, dst_raw), chain_v, dve)
                    dve.wait_ge(wanted.sem, 1)
                    link(nc.vector.tensor_copy(iota_f[:, :], iota_i), chain_v, dve)
                    dve.wait_ge(taken_s.sem, 1)
                    link(nc.vector.tensor_tensor(cyc, cyc, cyc, ALU.mult), chain_v, dve)
                    link(nc.vector.tensor_scalar(e_cut[:, :], cyc, -1.0, 1.0, ALU.mult, ALU.add), chain_v, dve)
                    dve.wait_ge(stage_out[0].sem, 32)
                    link(nc.vector.tensor_tensor(dst_rel[:, :].rearrange("p (g j) -> p g j", j=GROUP),
                                                 dst_f.rearrange("p (g j) -> p g j", j=GROUP),
                                                 base_row[:, :].rearrange("p (g o) -> p g o", o=1).broadcast_to([P, N_GROUPS, GROUP]),
                                                 ALU.subtract), chain_v, dve)
                    link(nc.vector.tensor_copy(base_i[:, :], base_row[0:1, :]), chain_v, dve)
                    link(nc.vector.tensor_tensor(span_row[:, :], max_row[:, :], base_row[0:1, :], ALU.subtract), chain_v, dve)
                    link(nc.vector.tensor_reduce(span_max[:, :], span_row[:, :], AX.X, ALU.max), chain_v, dve)
                    link(nc.vector.tensor_copy(passes_i[:, :], span_max[:, :]), chain_v, dve)
                    link(nc.vector.tensor_scalar(passes_i[:, :], passes_i[:, :], WIN.bit_length() - 1, None,
                                                 ALU.arith_shift_right), chain_v, dve)
                    link(nc.vector.tensor_scalar(passes_i[:, :], passes_i[:, :], 1.0, None, ALU.add), chain_v, dve)

            for t, n in ((edges_in, 80), (prepared, 1), (wanted, 1), (input_v, 1), (taken_s, 1), (stored, 32), (stage_out[0], 32)):
                t.passed(n)

        def fold_biases():
            with nc.Block() as block:
                @block.tensor
                def _(pe):
                    nc.tensor.matmul(ps[0][:, 0:D], ones[:, :], sq_w[:, MLP2, :], start=True, stop=True)
                    nc.tensor.matmul(ps[0][:, D:2 * D], ones[:, :], sq_w[:, LIN, :], start=True, stop=True).then_inc(made_t.sem, 1)

                @block.gpsimd
                def _(pool):
                    nc.gpsimd.memset(agg[:, :, :], 0.0)

                @block.vector
                def _(dve):
                    dve.wait_ge(made_t.sem, made_t.at(1))
                    link(nc.vector.scalar_tensor_tensor(row_vecs[:, MLP_B2, :], ps[0][:, 0:D], -LN2, row_vecs[:, MLP_B2, :],
                                                        ALU.mult, ALU.add), chain_v, dve)
                    link(nc.vector.scalar_tensor_tensor(row_vecs[:, LIN_B, :], ps[0][:, D:2 * D], -LN2, row_vecs[:, LIN_B, :],
                                                        ALU.mult, ALU.add), chain_v, dve)
                    rest = row_vecs[:, MLP_B2, :]
                    for k in range(3):
                        link(nc.vector.tensor_copy(b2_split[:, k, :], rest), chain_v, dve)
                        link(nc.vector.tensor_copy(b2_parts[:, k, :], b2_split[:, k, :]), chain_v, dve)
                        if k < 2:
                            link(nc.vector.tensor_tensor(b2_left[:, k, :], rest, b2_parts[:, k, :], ALU.subtract), chain_v, dve)
                            rest = b2_left[:, k, :]
                    link(nc.vector.tensor_scalar(b2_left[:, 0, :], b2_parts[:, 0, :], ident[:, 0:1], None, ALU.mult), chain_v, dve)
                    for k in (1, 2):
                        link(nc.vector.scalar_tensor_tensor(b2_left[:, k % 2, :], b2_parts[:, k, :], ident[:, k:k + 1],
                                                            b2_left[:, (k - 1) % 2, :], ALU.mult, ALU.add), chain_v, dve)
                    for j in range(GROUP):
                        last = nc.vector.tensor_copy(b2_split[:, j, :], b2_left[:, 0, :])
                    link(last, chain_v, dve)
            made_t.passed(1)

        def normalise(to_table=False):
            with nc.Block() as block:
                @block.vector
                def _(dve):
                    for t in range(N_TILES):
                        last = nc.vector.bn_stats(stats[:, t, :], x_rows[:, t, :])
                    link(last, chain_v, dve)
                    for t in range(N_TILES):
                        last = nc.vector.bn_aggr(mean_var[:, t, :], stats[:, t, :])
                    last.then_inc(input_v.sem, 1)
                    dve.wait_ge(prepared.sem, prepared.at(1))
                    link(nc.vector.reciprocal(ln_scale[:, :], ln_std[:, :]), chain_v, dve)
                    nc.vector.scalar_tensor_tensor(ln_shift[:, :], mean_var[:, :, 0], -1.0, ln_scale[:, :],
                                                   ALU.mult, ALU.mult).then_inc(input_v.sem, 1)
                    for g, (t, n) in enumerate(QUADS):
                        dve.wait_ge(made_t.sem, made_t.at(g + 1))
                        nc.vector.tensor_copy(h_cols[:, 0, t * P:(t + n) * P], ps[g % 4][:, 0:n * P]).then_inc(taken_v.sem, 1)

                @block.scalar
                def _(act):
                    act.wait_ge(input_v.sem, input_v.at(1))
                    nc.scalar.activation(ln_std[:, :], mean_var[:, :, 1], ACT.Sqrt, bias=eps_t[:, :]).then_inc(prepared.sem, 1)
                    act.wait_ge(input_v.sem, input_v.at(2))
                    for t in range(N_TILES):
                        nc.scalar.activation(h_rows[:, t, :], x_rows[:, t, :], ACT.Relu, bias=ln_shift[:, t:t + 1],
                                             scale=ln_scale[:, t:t + 1]).then_inc(rows_done.sem, 1)

                @block.tensor
                def _(pe):
                    for g, (t, n) in enumerate(QUADS):
                        pe.wait_ge(rows_done.sem, rows_done.at(t + n))
                        if g >= 4:
                            pe.wait_ge(taken_v.sem, taken_v.at(g - 3))
                        for i in range(n):
                            last = nc.tensor.transpose(ps[g % 4][:, i * P:(i + 1) * P], h_rows[:, t + i, :], ident[:, :])
                        last.then_inc(made_t.sem, 1)

                @block.sync
                def _(sp):
                    if to_table:
                        sp.wait_ge(rows_done.sem, rows_done.at(N_TILES))
                        sp.dma_start(table.rearrange("(t p) f -> p t f", p=P), h_rows[:, :, :]).then_inc(stored.sem, 16)
                        sp.wait_ge(stored.sem, stored.at(16))
            for t, n in ((input_v, 2), (prepared, 1), (made_t, len(QUADS)), (taken_v, len(QUADS)), (rows_done, N_TILES),
                         (stored, 16 if to_table else 0)):
                t.passed(n)

        def project(lhs, weights, residual=None):
            pairs = [(t, min(2, N_TILES - t)) for t in range(0, N_TILES, 2)]
            with nc.Block() as block:
                @block.tensor
                def _(pe):
                    for g, (t, n) in enumerate(pairs):
                        if g >= 4:
                            pe.wait_ge(taken_s.sem, taken_s.at(g - 3))
                            if residual:
                                pe.wait_ge(taken_v.sem, taken_v.at(g - 3))
                        for bank, ws in ((g % 4, weights), (4 + g % 4, residual or [])):
                            for i in range(n):
                                for k, w in enumerate(ws):
                                    last = nc.tensor.matmul(ps[bank][:, i * P:(i + 1) * P], lhs[k][:, (t + i) * P:(t + i + 1) * P], w,
                                                            start=(k == 0), stop=(k == len(ws) - 1))
                        last.then_inc(made_t.sem, 1)

                @block.scalar
                def _(act):
                    for g, (t, n) in enumerate(pairs):
                        act.wait_ge(made_t.sem, made_t.at(g + 1))
                        nc.scalar.copy(h_rows[:, t:t + n, :].rearrange("p t f -> p (t f)"), ps[g % 4][:, 0:n * P]).then_inc(taken_s.sem, 1)

                @block.vector
                def _(dve):
                    if residual:
                        for g, (t, n) in enumerate(pairs):
                            dve.wait_ge(made_t.sem, made_t.at(g + 1))
                            xs = x_rows[:, t:t + n, :].rearrange("p t f -> p (t f)")
                            nc.vector.tensor_tensor(xs, xs, ps[4 + g % 4][:, 0:n * P], ALU.add).then_inc(taken_v.sem, 1)

                @block.sync
                def _(sp):
                    for t0, t1, g in ((0, 12, 6), (12, N_TILES, len(pairs))):
                        sp.wait_ge(taken_s.sem, taken_s.at(g))
                        sp.dma_start(table.rearrange("(t p) f -> p t f", p=P)[:, t0:t1, :], h_rows[:, t0:t1, :]).then_inc(stored.sem, 16)
                    sp.wait_ge(stored.sem, stored.at(32))
            for t, n in ((made_t, len(pairs)), (taken_s, len(pairs)), (taken_v, len(pairs) if residual else 0), (stored, 32)):
                t.passed(n)

        def project_relations(layer):
            half = N_REL * D // 2
            stage = h_rows[:, :, :].rearrange("p t f -> p (t f)")
            with nc.Block() as block:
                @block.tensor
                def _(pe):
                    for t in range(N_TILES):
                        if t >= 4:
                            pe.wait_ge(taken_v.sem, taken_v.at(t - 3))
                            pe.wait_ge(taken_s.sem, taken_s.at(t - 3))
                        for s in range(2):
                            last = nc.tensor.matmul(ps[2 * (t % 4) + s][:, :], h_cols[:, 0, t * P:(t + 1) * P],
                                                    rel_w[:, layer, s * half:(s + 1) * half], start=True, stop=True)
                        last.then_inc(made_t.sem, 1)

                @block.vector
                def _(dve):
                    for t in range(N_TILES):
                        if t >= 3:
                            dve.wait_ge(stage_out[t % 3].sem, stage_out[t % 3].at(16 * (t // 3)))
                        dve.wait_ge(made_t.sem, made_t.at(t + 1))
                        o = (t % 3) * N_REL * D
                        nc.vector.tensor_copy(stage[:, o:o + half], ps[2 * (t % 4)][:, :]).then_inc(taken_v.sem, 1)

                @block.scalar
                def _(act):
                    for t in range(N_TILES):
                        if t >= 3:
                            act.wait_ge(stage_out[t % 3].sem, stage_out[t % 3].at(16 * (t // 3)))
                        act.wait_ge(made_t.sem, made_t.at(t + 1))
                        o = (t % 3) * N_REL * D + half
                        nc.scalar.copy(stage[:, o:o + half], ps[2 * (t % 4) + 1][:, :]).then_inc(taken_s.sem, 1)

                @block.sync
                def _(sp):
                    for t in range(N_TILES):
                        sp.wait_ge(taken_v.sem, taken_v.at(t + 1))
                        sp.wait_ge(taken_s.sem, taken_s.at(t + 1))
                        o = (t % 3) * N_REL * D
                        sp.dma_start(rel_table[t * P * N_REL:(t + 1) * P * N_REL, :].rearrange("(p r) f -> p (r f)", r=N_REL),
                                     stage[:, o:o + N_REL * D]).then_inc(stage_out[t % 3].sem, 16)
                    for i in range(3):
                        uses = len(range(i, N_TILES, 3))
                        sp.wait_ge(stage_out[i].sem, stage_out[i].at(16 * uses))
            for t in (made_t, taken_v, taken_s):
                t.passed(N_TILES)
            for i in range(3):
                stage_out[i].passed(16 * len(range(i, N_TILES, 3)))

        def by_columns(weights, inputs, takes):
            with nc.Block() as block:
                @block.tensor
                def _(pe):
                    for g, (c, n) in enumerate(COLS):
                        if g >= 4:
                            pe.wait_ge(taken_s.sem, taken_s.at(g - 3))
                        for k, (w, h) in enumerate(zip(weights, inputs)):
                            last = nc.tensor.matmul(ps[g % 4][:, 0:n], w, h[:, c:c + n], start=(k == 0), stop=(k == len(weights) - 1))
                        last.then_inc(made_t.sem, 1)

                @block.scalar
                def _(act):
                    for g, (c, n) in enumerate(COLS):
                        act.wait_ge(made_t.sem, made_t.at(g + 1))
                        takes(ps[g % 4][:, 0:n], c, n).then_inc(taken_s.sem, 1)
            for t in (made_t, taken_s):
                t.passed(len(COLS))

        def add_transposed(to_out=False):
            with nc.Block() as block:
                @block.tensor
                def _(pe):
                    for g, (t, n) in enumerate(QUADS):
                        if g >= 4:
                            pe.wait_ge(taken_v.sem, taken_v.at(g - 3))
                        for i in range(n):
                            last = nc.tensor.transpose(ps[g % 4][:, i * P:(i + 1) * P], m_cols[:, (t + i) * P:(t + i + 1) * P], ident[:, :])
                        last.then_inc(made_t.sem, 1)

                @block.vector
                def _(dve):
                    for g, (t, n) in enumerate(QUADS):
                        dve.wait_ge(made_t.sem, made_t.at(g + 1))
                        xs = x_rows[:, t:t + n, :].rearrange("p t f -> p (t f)")
                        nc.vector.tensor_tensor(xs, xs, ps[g % 4][:, 0:n * P], ALU.add).then_inc(taken_v.sem, 1)

                @block.sync
                def _(sp):
                    if to_out:
                        whole = N_NODES // P
                        for n, (t, k) in enumerate(QUADS):
                            sp.wait_ge(taken_v.sem, taken_v.at(n + 1))
                            full = min(t + k, whole) - t
                            if full:
                                sp.dma_start(out[t * P:(t + full) * P, :].rearrange("(t p) f -> p t f", p=P),
                                             x_rows[:, t:t + full, :]).then_inc(stored.sem, 16)
                            else:
                                sp.dma_start(out[whole * P:N_NODES, :], x_rows[0:N_NODES - whole * P, whole, :]).then_inc(stored.sem, 16)
                        sp.wait_ge(stored.sem, stored.at(16 * len(QUADS)))
            for t in (made_t, taken_v):
                t.passed(len(QUADS))

        rounds = [0]
        column = nc.vector.alloc_register("column")

        def edge_round(source, indices, weights=None, counts=False, filters=False, add_rows=None):
            r = rounds[0]
            rounds[0] += 1
            first_group, first_idx = r * N_GROUPS, r * AHEAD
            first_turn = r * TURNS
            SUMS, W_BANK, Z_BANK = ps[0], ps[1], (ps[2], ps[3])
            planes = 2 if counts else 1
            sums = SUMS[:, 0:planes * WIN].rearrange("p (a w) -> p a w", w=WIN)
            with nc.Block() as block:
                @block.gpsimd
                def _(pool):
                    with pool.Fori(0, TURNS) as turn:
                        for s in range(SLOTS):
                            pool.wait_ge(idx_ready.sem, turn * SLOTS + (first_idx + s + 1))
                            pool.sem_inc(turn_begun.sem, 1)
                            for j in range(GROUP):
                                nc.gpsimd.indirect_dma_start(rows[:, s, j, :], None, source,
                                                             bass.IndirectOffsetOnAxis(ap=cur_idx[:, s, j:j + 1], axis=0)
                                                             ).then_inc(gathered[s].sem, 16)

                @block.sync
                def _(sp):
                    if filters:
                        cols = a["attr_cols"]
                        for s in range(SLOTS):
                            sp.dma_start(attr[:, s, :], cols[:, s * G_EDGES:(s + 1) * G_EDGES]).then_inc(attr_in[s].sem, 16)
                        with sp.Fori(1, TURNS) as turn:
                            for s in range(SLOTS):
                                sp.wait_ge(z_ready.sem, turn * SLOTS + (s + 1 - SLOTS))
                                sp.dma_start(attr[:, s, :], cols[:, bass.ds(turn * (SLOTS * G_EDGES) + s * G_EDGES, G_EDGES)]
                                             ).then_inc(attr_in[s].sem, 16)
                        sp.wait_ge(z_ready.sem, N_GROUPS - SLOTS + 1)
                        sp.dma_start(attr[:, 0, :], cols[:, EDGES:EDGES + G_EDGES]).then_inc(attr_in[0].sem, 16)

                @block.tensor
                def _(pe):
                    passes = pe.value_load(passes_i[0:1, 0:1], min_val=1, max_val=NODES // WIN)

                    def first_layer(slot, parity):
                        nc.tensor.matmul(Z_BANK[parity][:, :], mlp_w1[:, :], attr[:, slot, :], start=True, stop=True
                                         ).then_inc(z_ready.sem, 1)

                    if filters:
                        pe.wait_ge(attr_in[0].sem, 16)
                        first_layer(0, 0)
                    with pe.Fori(0, TURNS) as turn:
                        for s in range(SLOTS):
                            if filters:
                                pe.wait_ge(attr_in[(s + 1) % SLOTS].sem, (turn + (1 if s + 1 < SLOTS else 2)) * 16)
                                first_layer((s + 1) % SLOTS, (s + 1) % 2)
                                pe.wait_ge(filt_ready.sem, turn * SLOTS + (s + 1))
                                for j in range(GROUP):
                                    wj = W_BANK[:, j * D:(j + 1) * D]
                                    nc.tensor.matmul(wj, filt[:, s % 2, j * P:(j + 1) * P], sq_w[:, MLP2, :], start=True, stop=False)
                                    last = nc.tensor.matmul(wj, three_ones[:, :], b2_split[:, j, :], start=False, stop=True)
                                last.then_inc(w_ready.sem, 1)
                            with pe.Fori(0, passes) as w:
                                n = (turn * SLOTS + (first_group + s)) * passes + w
                                if filters:
                                    pe.wait_ge(weighed.sem, turn * SLOTS + (s + 1))
                                else:
                                    pe.wait_ge(gathered[s].sem, (turn + (first_turn + 1)) * (16 * GROUP))
                                pe.wait_ge(onehot_ready.sem, n + 1)
                                for j in range(GROUP):
                                    last = nc.tensor.matmul(SUMS[:, 0:WIN], rows[:, s, j, :], onehot[:, j, :],
                                                            start=(j == 0), stop=(j == GROUP - 1))
                                if counts:
                                    for j in range(GROUP):
                                        last = nc.tensor.matmul(SUMS[:, WIN:2 * WIN], ones[:, :], onehot[:, j, :],
                                                                start=(j == 0), stop=(j == GROUP - 1))
                                last.then_inc(scattered.sem, 1)

                if filters:
                    @block.scalar
                    def _(act):
                        def logs(parity, count):
                            act.wait_ge(z_capped.sem, count)
                            link_s = nc.scalar.activation(soft[:, parity, :], soft[:, parity, :], ACT.Exp)
                            link_s.then_inc(prepared.sem, 1)
                            act.wait_ge(prepared.sem, count + exp_base)
                            nc.scalar.activation(soft[:, parity, :], soft[:, parity, :], ACT.Ln, bias=ones[:, 0:1]).then_inc(ln_ready.sem, 1)

                        exp_base = prepared.value
                        logs(0, 1)
                        with act.Fori(0, TURNS) as turn:
                            for s in range(SLOTS):
                                logs((s + 1) % 2, turn * SLOTS + (s + 2))

                @block.vector
                def _(dve):
                    passes = dve.value_load(passes_i[0:1, 0:1], min_val=1, max_val=NODES // WIN)
                    if add_rows is not None:
                        row = row_vecs[:, add_rows, :].rearrange("p (o f) -> p o f", o=1).broadcast_to([P, N_TILES, D])
                        nc.vector.tensor_tensor(x_rows[:, :, :], x_rows[:, :, :], row, ALU.add)
                    for s in range(SLOTS):
                        nc.vector.tensor_copy(cur_idx[:, s, :], indices[:, s * GROUP:(s + 1) * GROUP]).then_inc(idx_ready.sem, 1)

                    def cap(parity, count):
                        dve.wait_ge(z_ready.sem, count)
                        nc.vector.tensor_scalar(soft[:, parity, :], Z_BANK[parity][:, :], vecs[:, MLP_B1:MLP_B1 + 1], EXP_CAP,
                                                ALU.add, ALU.min).then_inc(z_capped.sem, 1)

                    def softplus(parity, count):
                        dve.wait_ge(ln_ready.sem, count)
                        nc.vector.scalar_tensor_tensor(filt[:, parity, :], Z_BANK[parity][:, :], vecs[:, MLP_B1:MLP_B1 + 1],
                                                       soft[:, parity, :], ALU.add, ALU.max).then_inc(filt_ready.sem, 1)

                    if filters:
                        cap(0, 1)
                        softplus(0, 1)
                    with dve.Fori(0, TURNS) as turn:
                        for s in range(SLOTS):
                            if filters:
                                cap((s + 1) % 2, turn * SLOTS + (s + 2))
                                dve.wait_ge(w_ready.sem, turn * SLOTS + (s + 1))
                                dve.wait_ge(gathered[s].sem, (turn + (first_turn + 1)) * (16 * GROUP))
                                msg = rows[:, s, :, :].rearrange("p j f -> p (j f)")
                                nc.vector.tensor_tensor(msg, msg, W_BANK[:, :], ALU.mult).then_inc(weighed.sem, 1)
                            base = dve.value_load(base_i[0:1, bass.ds(turn * SLOTS + s, 1)], min_val=0, max_val=N_NODES)
                            with dve.Fori(0, passes) as w:
                                n = (turn * SLOTS + (first_group + s)) * passes + w
                                win = iota_f[:, bass.ds(w * WIN, WIN)]
                                if weights is None:
                                    off = dst_rel[:, bass.ds((turn * SLOTS + s) * GROUP, GROUP)].rearrange("p (j o) -> p j o", o=1)
                                    hot = nc.vector.tensor_tensor(onehot[:, :, :],
                                                                  win.rearrange("p (o c) -> p o c", o=1).broadcast_to([P, GROUP, WIN]),
                                                                  off.broadcast_to([P, GROUP, WIN]), ALU.is_equal)
                                else:
                                    for j in range(GROUP):
                                        edge = bass.ds((turn * SLOTS + s) * GROUP + j, 1)
                                        hot = nc.vector.tensor_scalar(onehot[:, j, :], win, dst_rel[:, edge], weights[:, edge],
                                                                      ALU.is_equal, ALU.mult)
                                hot.then_inc(onehot_ready.sem, 1)
                                dve.wait_ge(scattered.sem, n + 1)
                                dve.reg_alu(column, base + w * WIN, NODES, ALU.min)
                                col = dve.snap(column, min_val=0, max_val=NODES)
                                into = agg[:, 0:planes, bass.ds(col, WIN)]
                                nc.vector.tensor_tensor(into, into, sums, ALU.add).then_inc(summed.sem, 1)
                            nc.vector.tensor_copy(cur_idx[:, s, :], indices[:, bass.ds((turn * SLOTS + s + SLOTS) * GROUP, GROUP)]
                                                  ).then_inc(idx_ready.sem, 1)
                            if filters:
                                softplus((s + 1) % 2, turn * SLOTS + (s + 2))
            if filters:
                prepared.passed(N_GROUPS + 1)

        def identity_plus(bias_col):
            def takes(bank, c, n):
                return nc.scalar.activation(agg[:, 0, c:c + n], bank, ACT.Identity, bias=vecs[:, bias_col:bias_col + 1])
            return takes

        def mean_columns():
            with nc.Block() as block:
                @block.vector
                def _(dve):
                    nc.vector.tensor_tensor(m_cols[:, :], agg[:, 0, 0:NODES], agg[:, 1, 0:NODES], ALU.mult)

        def count_inverses():
            with nc.Block() as block:
                @block.vector
                def _(dve):
                    link(nc.vector.tensor_scalar(agg[:, 1, :], agg[:, 1, :], 1.0, None, ALU.max), chain_v, dve)
                    nc.vector.reciprocal(agg[:, 1, :], agg[:, 1, :])

        def clear_agg():
            with nc.Block() as block:
                @block.gpsimd
                def _(pool):
                    nc.gpsimd.memset(agg[:, 0, :], 0.0)

        def sage_hidden():
            stage = h_rows[:, :, :].rearrange("p t f -> p (t f)")

            def block_products(c, source_cols, takes):
                by_columns([w1lr[:, 0, c * D:(c + 1) * D], w1lr[:, 1, c * D:(c + 1) * D]], [m_cols, source_cols], takes)

            h_in = h_cols[:, 0, :]
            block_products(1, h_in, lambda bank, c, n: nc.scalar.activation(
                h_cols[:, 1, c:c + n], bank, ACT.Identity, bias=bn_vec[:, 0, 1:2]))
            block_products(0, h_in, lambda bank, c, n: nc.scalar.activation(
                stage[:, c:c + n], bank, ACT.Identity, bias=bn_vec[:, 0, 0:1]))
            pieces = [(c, min(BANK, N_NODES - c)) for c in range(0, N_NODES, BANK)]
            with nc.Block() as block:
                @block.vector
                def _(dve):
                    for f, src in ((0, stage), (1, h_cols[:, 1, :])):
                        for i, (c, n) in enumerate(pieces):
                            last = nc.vector.bn_stats(stats[:, f * len(pieces) + i, :], src[:, c:c + n])
                    link(last, chain_v, dve)
                    for f in range(H2):
                        last = nc.vector.bn_aggr(mean_var[:, f, :], stats[:, f * len(pieces):(f + 1) * len(pieces), :]
                                                 .rearrange("p s k -> p (s k)"))
                    last.then_inc(input_v.sem, 1)
                    dve.wait_ge(prepared.sem, prepared.at(1))
                    link(nc.vector.reciprocal(ln_scale[:, 0:H2], ln_std[:, 0:H2]), chain_v, dve)
                    link(nc.vector.tensor_tensor(ln_scale[:, 0:H2], ln_scale[:, 0:H2], bn_vec[:, 1, :], ALU.mult), chain_v, dve)
                    link(nc.vector.tensor_tensor(ln_shift[:, 0:H2], mean_var[:, 0:H2, 0], ln_scale[:, 0:H2], ALU.mult), chain_v, dve)
                    nc.vector.tensor_tensor(ln_shift[:, 0:H2], bn_vec[:, 2, :], ln_shift[:, 0:H2], ALU.subtract).then_inc(input_v.sem, 1)

                @block.scalar
                def _(act):
                    act.wait_ge(input_v.sem, input_v.at(1))
                    nc.scalar.activation(ln_std[:, 0:H2], mean_var[:, 0:H2, 1], ACT.Sqrt, bias=eps_t[:, :]).then_inc(prepared.sem, 1)
                    act.wait_ge(input_v.sem, input_v.at(2))
                    for f, src in ((0, stage), (1, h_cols[:, 1, :])):
                        nc.scalar.activation(h_cols[:, f, :], src[:, 0:NODES], ACT.Relu, bias=ln_shift[:, f:f + 1],
                                             scale=ln_scale[:, f:f + 1])
            input_v.passed(2)
            prepared.passed(1)

        def relu_columns(into):
            with nc.Block() as block:
                @block.vector
                def _(dve):
                    nc.vector.tensor_scalar(into[:, 0:NODES], agg[:, 0, 0:NODES], 0.0, None, ALU.max)

        def selu_columns():
            with nc.Block() as block:
                @block.vector
                def _(dve):
                    nc.vector.tensor_scalar(m_cols[:, :], agg[:, 0, 0:NODES], 0.0, None, ALU.min).then_inc(input_v.sem, 1)
                    dve.wait_ge(prepared.sem, prepared.at(1))
                    link(nc.vector.tensor_scalar(m_cols[:, :], m_cols[:, :], SELU_SCALE * SELU_ALPHA, -SELU_SCALE * SELU_ALPHA,
                                                 ALU.mult, ALU.add), chain_v, dve)
                    link(nc.vector.tensor_scalar(agg[:, 0, 0:NODES], agg[:, 0, 0:NODES], 0.0, SELU_SCALE, ALU.max, ALU.mult),
                         chain_v, dve)
                    nc.vector.tensor_tensor(m_cols[:, :], m_cols[:, :], agg[:, 0, 0:NODES], ALU.add)

                @block.scalar
                def _(act):
                    act.wait_ge(input_v.sem, input_v.at(1))
                    nc.scalar.activation(m_cols[:, :], m_cols[:, :], ACT.Exp).then_inc(prepared.sem, 1)
            input_v.passed(1)
            prepared.passed(1)

        def shifted_softplus():
            by_columns([sq_w[:, LIN2, :]], [agg[:, 0, :]], lambda bank, c, n: nc.scalar.activation(
                h_cols[:, 0, c:c + n], bank, ACT.Identity, bias=vecs[:, LIN2_B:LIN2_B + 1]))
            with nc.Block() as block:
                @block.vector
                def _(dve):
                    nc.vector.tensor_scalar(m_cols[:, :], h_cols[:, 0, :], EXP_CAP, None, ALU.min).then_inc(input_v.sem, 1)
                    dve.wait_ge(prepared.sem, prepared.at(2))
                    nc.vector.tensor_tensor(m_cols[:, :], m_cols[:, :], h_cols[:, 0, :], ALU.max)

                @block.scalar
                def _(act):
                    act.wait_ge(input_v.sem, input_v.at(1))
                    nc.scalar.activation(m_cols[:, :], m_cols[:, :], ACT.Exp).then_inc(prepared.sem, 1)
                    act.wait_ge(prepared.sem, prepared.at(1))
                    nc.scalar.activation(m_cols[:, :], m_cols[:, :], ACT.Ln, bias=ones[:, 0:1]).then_inc(prepared.sem, 1)
            input_v.passed(1)
            prepared.passed(2)

        def project_residual():
            with nc.Block() as block:
                @block.tensor
                def _(pe):
                    for g, (t, n) in enumerate(QUADS):
                        if g >= 4:
                            pe.wait_ge(taken_v.sem, taken_v.at(g - 3))
                        for i in range(n):
                            last = nc.tensor.matmul(ps[g % 4][:, i * P:(i + 1) * P], m_cols[:, (t + i) * P:(t + i + 1) * P],
                                                    sq_w[:, LIN, :], start=True, stop=True)
                        last.then_inc(made_t.sem, 1)

                @block.vector
                def _(dve):
                    for g, (t, n) in enumerate(QUADS):
                        dve.wait_ge(made_t.sem, made_t.at(g + 1))
                        xs = x_rows[:, t:t + n, :].rearrange("p t f -> p (t f)")
                        nc.vector.tensor_tensor(xs, xs, ps[g % 4][:, 0:n * P], ALU.add).then_inc(taken_v.sem, 1)
            for t in (made_t, taken_v):
                t.passed(len(QUADS))

        prepare()
        fold_biases()
        normalise(to_table=True)
        edge_round(table, src_idx, counts=True, add_rows=L0_B2)
        count_inverses()
        mean_columns()
        clear_agg()
        sage_hidden()
        project([h_cols[:, 0, :], h_cols[:, 1, :]], [w2lr[:, 0, 0:D], w2lr[:, 1, 0:D]],
                residual=[w2lr[:, 0, D:2 * D], w2lr[:, 1, D:2 * D]])
        edge_round(table, src_idx)
        mean_columns()
        clear_agg()
        add_transposed()

        normalise()
        project([h_cols[:, 0, :]], [sq_w[:, LIN1, :]])
        edge_round(table, src_idx, weights=e_cut, filters=True, add_rows=LIN_B)
        shifted_softplus()
        project_residual()

        normalise()
        by_columns([sq_w[:, SL1, :]], [h_cols[:, 0, :]], identity_plus(R_B1))
        project_relations(0)
        edge_round(rel_table, rel_idx)
        relu_columns(h_cols[:, 0, :])
        by_columns([sq_w[:, SL2, :]], [h_cols[:, 0, :]], identity_plus(R_B2))
        project_relations(1)
        edge_round(rel_table, rel_idx)
        relu_columns(m_cols)
        add_transposed()

        normalise()
        by_columns([sq_w[:, KER, :]], [h_cols[:, 0, :]], lambda bank, c, n: nc.scalar.activation(
            agg[:, 0, c:c + n], bank, ACT.Identity, bias=vecs[:, BIAS:BIAS + 1], scale=vecs[:, SKIP:SKIP + 1]))
        project([h_cols[:, 0, :]], [sq_w[:, KER, :]])
        edge_round(table, src_idx, weights=e_weight)
        selu_columns()
        add_transposed(to_out=True)


_DIRECT = ['L0_gnn_W1l', 'L0_gnn_b1', 'L0_gnn_W1r', 'L0_gnn_gamma', 'L0_gnn_beta', 'L0_gnn_W2l', 'L0_gnn_b2', 'L0_gnn_W2r',
           'L1_gnn_mlp_w1', 'L1_gnn_mlp_b1', 'L1_gnn_mlp_w2', 'L1_gnn_mlp_b2', 'L1_gnn_lin1_w', 'L1_gnn_lin2_w', 'L1_gnn_lin2_b',
           'L1_gnn_lin_w', 'L1_gnn_lin_b', 'L2_gnn_w1', 'L2_gnn_sl1', 'L2_gnn_b1', 'L2_gnn_w2', 'L2_gnn_sl2', 'L2_gnn_b2',
           'L3_gnn_kernel', 'L3_gnn_bias', 'L3_gnn_skip_weight']


def kernel(**inputs):
    import numpy as _np
    import concourse.bacc as _bacc
    from concourse import mybir as _mybir
    from concourse.bass_utils import run_bass_kernel_spmd as _run

    def padded(name, n, fill):
        v = _np.asarray(inputs[name])
        return _np.concatenate([v, _np.full((n - v.shape[0],) + v.shape[1:], fill, v.dtype)])

    def edge_columns(name, groups, fill):
        return _np.ascontiguousarray(padded(name, groups * G_EDGES, fill).reshape(-1, P).T)

    arrays = {
        "x": padded("x", NODES, 0),
        "dst": padded("dst", EDGES, -1),
        "dst_cols": edge_columns("dst", N_GROUPS, -1),
        "src_cols": edge_columns("src", AHEAD, 0),
        "type_cols": edge_columns("edge_type_8", AHEAD, 0),
        "weight_cols": edge_columns("edge_weight", N_GROUPS, 0),
        "attr_cols": _np.ascontiguousarray(padded("edge_attr_50", EDGES + G_EDGES, 0).T),
    }
    for name in _DIRECT:
        arrays[name] = _np.ascontiguousarray(inputs[name])
    nc = _bacc.Bacc("TRN2", target_bir_lowering=False, num_devices=1)
    aps = {name: nc.dram_tensor(f"in_{name}", v.shape, _mybir.dt.from_np(v.dtype), kind="ExternalInput").ap()
           for name, v in arrays.items()}
    out = nc.dram_tensor("out_x", (N_NODES, D), _mybir.dt.float32, kind="ExternalOutput").ap()
    build_gnn(nc, aps, out)
    r = _run(nc, [{f"in_{name}": v for name, v in arrays.items()}], core_ids=[0])
    return r.results[0]["out_x"]
```

```python
import concourse.bass as bass
from concourse import mybir
from contextlib import ExitStack
import numpy as np

fp32 = mybir.dt.float32
bf16 = mybir.dt.bfloat16
i32 = mybir.dt.int32
ALU = mybir.AluOpType
ACT = mybir.ActivationFunctionType
AX = mybir.AxisListType

N_NODES = 3125
N_EDGES = 100000
D = 128
H2 = 2
N_GAUSS = 50
N_REL = 8
P = 128
N_TILES = -(-N_NODES // P)
NODES = N_TILES * P
CHUNK = P
GROUP = 4
G_EDGES = CHUNK * GROUP
SLOTS = 4
N_GROUPS = -(-N_EDGES // G_EDGES)
TURNS = N_GROUPS // SLOTS
EDGES = N_GROUPS * G_EDGES
AHEAD = N_GROUPS + SLOTS
HOT_AHEAD = N_GROUPS + 2
ATTR_TURNS = TURNS + 2
WIN = 64
A_GROUPS = 76
A_TURNS = A_GROUPS // SLOTS
A_WIN = 20
A_COLS = 512
A_PER_TURN = 3
A_MADE = TURNS * A_PER_TURN
AGG = NODES + WIN
BANK = 512
COLS = [(c, min(BANK, NODES - c)) for c in range(0, NODES, BANK)]
QUADS = [(t, min(4, N_TILES - t)) for t in range(0, N_TILES, 4)]
MIN_ROWS = N_GROUPS // 2
LN_EPS = 1e-5
LN2 = float(np.log(2.0))
EXP_CAP = 30.0
SELU_SCALE = 1.0507009873554805
SELU_ALPHA = 1.6732632423543772
assert N_GROUPS % SLOTS == 0 and N_GROUPS % 2 == 0 and A_GROUPS % SLOTS == 0
assert (TURNS - A_TURNS) * A_PER_TURN >= A_GROUPS and 2 * TURNS >= A_GROUPS and A_MADE >= 2 * TURNS
assert N_TILES * A_WIN <= BANK and A_COLS <= BANK and A_WIN <= WIN


class Tally:

    def __init__(self, sem):
        self.sem, self.value = sem, 0

    def at(self, n):
        return self.value + n

    def passed(self, n):
        self.value += n


def build_gnn(nc, a, out):
    with ExitStack() as ctx:
        def sb(name, shape, dt=fp32):
            return ctx.enter_context(nc.sbuf_tensor(name, shape, dt))

        def tally(name):
            return Tally(ctx.enter_context(nc.semaphore(name)))

        def scratch(name, shape, dt=fp32):
            return nc.dram_tensor(name, shape, dt, kind="Internal").ap()

        table = scratch("table", (NODES, D))
        rel_table = scratch("rel_table", (NODES * N_REL, D))
        min_dram = scratch("min_dram", (2, N_GROUPS))

        x_rows = sb("x_rows", [P, N_TILES, D])
        h_rows = sb("h_rows", [P, N_TILES, D])
        h_cols = sb("h_cols", [P, H2, NODES])
        m_cols = sb("m_cols", [P, NODES])
        agg = sb("agg", [P, 2, AGG])
        src_idx = sb("src_idx", [P, AHEAD * GROUP], i32)
        rel_idx = sb("rel_idx", [P, AHEAD * GROUP], i32)
        dst_rel = sb("dst_rel", [P, HOT_AHEAD * GROUP])
        e_weight = sb("e_weight", [P, HOT_AHEAD * GROUP])
        e_cut = sb("e_cut", [P, HOT_AHEAD * GROUP])
        base_row = sb("base_row", [P, N_GROUPS])
        base_i = sb("base_i", [1, N_GROUPS], i32)
        more_i = sb("more_i", [1, 1], i32)
        turns_i = sb("turns_i", [1, 2], i32)
        iota_f = sb("iota_f", [P, P])
        further_rel = sb("further_rel", [P, GROUP])
        adj_mem = sb("adj_mem", [P, N_TILES * A_COLS])
        adj = adj_mem[:, :].rearrange("p (t d) -> p t d", d=A_COLS)
        a_src_tile = sb("a_src_tile", [P, A_MADE * GROUP], bf16)
        a_src_part = sb("a_src_part", [P, A_MADE * GROUP], bf16)
        a_dst_rel = sb("a_dst_rel", [P, A_MADE * GROUP], bf16)
        a_weight = sb("a_weight", [P, 3, A_MADE * GROUP], bf16)
        a_base_i = sb("a_base_i", [1, N_GROUPS], i32)
        iota_b = sb("iota_b", [P, P], bf16)
        ones_b = sb("ones_b", [P, P], bf16)
        tile_hot = sb("tile_hot", [P, 2, GROUP, N_TILES], bf16)
        dst_hot = sb("dst_hot", [P, 2, GROUP, A_WIN], bf16)
        pair_size = GROUP * N_TILES * A_WIN // 2
        pair_hot = [m_cols[:, b * pair_size:(b + 1) * pair_size].bitcast(bf16).rearrange("p (j t w) -> p j t w", t=N_TILES, w=A_WIN)
                    for b in range(2)]
        part_hot = [m_cols[:, 2 * pair_size + b * GROUP * D // 2:2 * pair_size + (b + 1) * GROUP * D // 2].bitcast(bf16)
                    .rearrange("p (j q) -> p j q", q=P) for b in range(2)]
        weight_hot = m_cols[:, pair_size:pair_size + 3 * GROUP * D // 2].bitcast(bf16).rearrange("p (k j q) -> p k j q", k=3, q=P)
        cur_idx = sb("cur_idx", [P, SLOTS, GROUP], i32)
        rows = sb("rows", [P, SLOTS, GROUP, D])
        onehot = sb("onehot", [P, 2, GROUP, WIN])
        hot_more = sb("hot_more", [P, GROUP, WIN])
        attr = adj_mem[0:N_GAUSS, 0:SLOTS * G_EDGES].rearrange("p (s e) -> p s e", s=SLOTS)
        soft = adj_mem[:, SLOTS * G_EDGES:(SLOTS + 2) * G_EDGES].rearrange("p (s e) -> p s e", s=2)
        filt = adj_mem[:, (SLOTS + 2) * G_EDGES:(2 * SLOTS + 2) * G_EDGES].rearrange("p (s e) -> p s e", s=SLOTS)
        ident = sb("ident", [P, P])
        ones = sb("ones", [P, P])
        eps_t = sb("eps_t", [P, 1])
        w1lr = sb("w1lr", [P, 2, H2 * D])
        w2lr = sb("w2lr", [P, H2, 2 * D])
        bn_vec = sb("bn_vec", [P, 3, H2])
        mlp_w1 = sb("mlp_w1", [N_GAUSS, D])
        sq_w = sb("sq_w", [P, 7, D])
        MLP2, LIN1, LIN2, LIN, SL1, SL2, KER = range(7)
        rel_w = sb("rel_w", [P, 2, N_REL * D])
        vecs = sb("vecs", [P, 6])
        MLP_B1, LIN2_B, R_B1, R_B2, BIAS, SKIP = range(6)
        row_vecs = sb("row_vecs", [P, 3, D])
        L0_B2, LIN_B, MLP_B2 = range(3)
        b2_parts = sb("b2_parts", [P, 3, D])
        b2_left = sb("b2_left", [P, 2, D])
        b2_split = sb("b2_split", [P, GROUP, D], bf16)
        three_ones = sb("three_ones", [P, P], bf16)
        stats = sb("stats", [P, N_TILES, 6])
        mean_var = sb("mean_var", [P, N_TILES, 2])
        ln_std = sb("ln_std", [P, N_TILES])
        inv_count = sb("inv_count", [P, N_TILES])
        ln_scale = sb("ln_scale", [P, N_TILES])
        ln_shift = sb("ln_shift", [P, N_TILES])
        dst_raw = agg[:, 0, 0:N_GROUPS * GROUP].bitcast(i32)
        dst_f = agg[:, 1, 0:N_GROUPS * GROUP]
        dst_groups_i = m_cols[0:MIN_ROWS, 0:2 * G_EDGES].rearrange("p (j e) -> p j e", j=2).bitcast(i32)
        dst_groups = m_cols[0:MIN_ROWS, 2 * G_EDGES:4 * G_EDGES].rearrange("p (j e) -> p j e", j=2)
        dst_lift = h_cols[0:MIN_ROWS, 0, 0:2 * G_EDGES].rearrange("p (j e) -> p j e", j=2)
        span = sb("span", [MIN_ROWS, 2, 2])
        span_row = h_cols[:, 0, 2048:2048 + N_GROUPS]
        max_row = h_cols[:, 0, 2304:2304 + N_GROUPS]
        span_max = sb("span_max", [P, 3])
        fits = sb("fits", [P, 3])
        src_part_i = h_cols[:, 1, 2048:2048 + A_MADE * GROUP].bitcast(i32)
        a_rel = h_cols[:, 1, 2048:2048 + A_GROUPS * GROUP]
        weight_rest = m_cols[:, 2048:2048 + A_MADE * GROUP]
        type_i = h_cols[:, 0, 1024:1024 + AHEAD * GROUP].bitcast(i32)
        cyc = h_cols[:, 1, 0:HOT_AHEAD * GROUP]
        cyc_round = h_cols[:, 1, 1024:1024 + HOT_AHEAD * GROUP]
        iota_i = h_rows[:, 0, :].bitcast(i32)

        ps = [ctx.enter_context(nc.psum_tensor(f"ps{i}", [P, BANK], fp32)) for i in range(8)]

        loaded = tally("loaded")
        edges_in = tally("edges_in")
        chain_v = tally("chain_v")
        chain_s = tally("chain_s")
        chain_g = tally("chain_g")
        made_t = tally("made_t")
        taken_v = tally("taken_v")
        taken_s = tally("taken_s")
        rows_done = tally("rows_done")
        stored = tally("stored")
        stage_out = [tally(f"stage_out{i}") for i in range(3)]
        prepared = tally("prepared")
        wanted = tally("wanted")
        input_v = tally("input_v")
        m_ready = tally("m_ready")
        z_made = tally("z_made")
        capped_z = tally("capped_z")
        logs_made = tally("logs_made")
        add_made = tally("add_made")
        x_ready = tally("x_ready")
        scale_ready = tally("scale_ready")
        shift_ready = tally("shift_ready")
        turned = tally("turned")
        cols_ready = tally("cols_ready")
        idx_ready = tally("idx_ready")
        turn_begun = tally("turn_begun")
        gathered = [tally(f"gathered{i}") for i in range(SLOTS)]
        onehot_ready = tally("onehot_ready")
        scattered = tally("scattered")
        more_hot = tally("more_hot")
        more_rel = tally("more_rel")
        more_sums = tally("more_sums")
        more_summed = tally("more_summed")
        summed = tally("summed")
        pairs_ready = [tally(f"pairs_ready{i}") for i in range(2)]
        hots_linked = [tally(f"hots_linked{i}") for i in range(2)]
        adj_made = [tally(f"adj_made{i}") for i in range(2)]
        adj_added = [tally(f"adj_added{i}") for i in range(2)]
        product_made = tally("product_made")
        attr_in = [tally(f"attr_in{i}") for i in range(SLOTS)]
        exp_ready = tally("exp_ready")
        z_ready = tally("z_ready")
        z_capped = tally("z_capped")
        ln_ready = tally("ln_ready")
        filt_ready = tally("filt_ready")
        w_ready = tally("w_ready")
        weighed = tally("weighed")

        def link(ins, t, eng):
            ins.then_inc(t.sem, 1)
            t.passed(1)
            eng.wait_ge(t.sem, t.value)

        def prepare():
            with nc.Block() as block:
                @block.sync
                def _(sp):
                    sp.dma_start(dst_groups_i, a["dst"].rearrange("(p j e) -> p j e", j=2, e=G_EDGES)).then_inc(edges_in.sem, 16)
                    sp.dma_start(dst_raw, a["dst_cols"]).then_inc(edges_in.sem, 16)
                    sp.dma_start(x_rows[:, :, :], a["x"].rearrange("(t p) f -> p t f", p=P)).then_inc(loaded.sem, 16)
                    sp.dma_start(src_idx[:, :], a["src_cols"]).then_inc(edges_in.sem, 16)
                    sp.dma_start(type_i, a["type_cols"]).then_inc(edges_in.sem, 16)
                    sp.dma_start(e_weight[:, :], a["weight_cols"]).then_inc(edges_in.sem, 16)
                    n = 1
                    for dst, src in (
                        (w1lr[:, 0, :], a["L0_gnn_W1l"]), (w1lr[:, 1, :], a["L0_gnn_W1r"]),
                        (w2lr[:, :, 0:D], a["L0_gnn_W2l"].rearrange("(c p) m -> p c m", p=P)),
                        (w2lr[:, :, D:2 * D], a["L0_gnn_W2r"].rearrange("(c p) m -> p c m", p=P)),
                        (mlp_w1[:, :], a["L1_gnn_mlp_w1"]), (sq_w[:, MLP2, :], a["L1_gnn_mlp_w2"]),
                        (sq_w[:, LIN1, :], a["L1_gnn_lin1_w"]), (sq_w[:, LIN2, :], a["L1_gnn_lin2_w"]),
                        (sq_w[:, LIN, :], a["L1_gnn_lin_w"]), (sq_w[:, SL1, :], a["L2_gnn_sl1"]),
                        (sq_w[:, SL2, :], a["L2_gnn_sl2"]), (sq_w[:, KER, :], a["L3_gnn_kernel"]),
                        (rel_w[:, 0, :].rearrange("p (r m) -> p r m", r=N_REL), a["L2_gnn_w1"].rearrange("r p m -> p r m")),
                        (rel_w[:, 1, :].rearrange("p (r m) -> p r m", r=N_REL), a["L2_gnn_w2"].rearrange("r p m -> p r m")),
                        (vecs[:, MLP_B1:MLP_B1 + 1], a["L1_gnn_mlp_b1"][:, None]),
                        (vecs[:, LIN2_B:LIN2_B + 1], a["L1_gnn_lin2_b"][:, None]),
                        (vecs[:, R_B1:R_B1 + 1], a["L2_gnn_b1"][:, None]), (vecs[:, R_B2:R_B2 + 1], a["L2_gnn_b2"][:, None]),
                        (vecs[:, BIAS:BIAS + 1], a["L3_gnn_bias"][:, None]), (vecs[:, SKIP:SKIP + 1], a["L3_gnn_skip_weight"][:, None]),
                        (row_vecs[:, L0_B2, :], a["L0_gnn_b2"][None, :].broadcast_to([P, D])),
                        (row_vecs[:, LIN_B, :], a["L1_gnn_lin_b"][None, :].broadcast_to([P, D])),
                        (row_vecs[:, MLP_B2, :], a["L1_gnn_mlp_b2"][None, :].broadcast_to([P, D])),
                    ):
                        sp.dma_start(dst, src).then_inc(loaded.sem, 16)
                        n += 1
                    for i, name in enumerate(("L0_gnn_b1", "L0_gnn_gamma", "L0_gnn_beta")):
                        for c in range(H2):
                            sp.dma_start(bn_vec[:, i, c:c + 1], a[name][c * P:(c + 1) * P, None]).then_inc(loaded.sem, 16)
                            n += 1
                    sp.wait_ge(prepared.sem, 1)
                    sp.dma_start(min_dram[0, :].rearrange("(p j) -> p j", j=2), span[:, 0, :]).then_inc(stored.sem, 16)
                    sp.dma_start(min_dram[1, :].rearrange("(p j) -> p j", j=2), span[:, 1, :]).then_inc(stored.sem, 16)
                    sp.wait_ge(stored.sem, 32)
                    sp.dma_start(base_row[:, :], min_dram[0:1, :].broadcast_to([P, N_GROUPS])).then_inc(stage_out[0].sem, 16)
                    sp.dma_start(max_row, min_dram[1:2, :].broadcast_to([P, N_GROUPS])).then_inc(stage_out[0].sem, 16)
                    sp.wait_ge(loaded.sem, 16 * n)
                    loaded.passed(16 * n)

                @block.gpsimd
                def _(pool):
                    link(nc.gpsimd.memset(ident[:, :], 0.0), chain_g, pool)
                    link(nc.gpsimd.affine_select(out=ident[:, :], in_=ident[:, :], compare_op=ALU.not_equal, fill=1.0,
                                                 base=0, pattern=[[-1, P]], channel_multiplier=1), chain_g, pool)
                    link(nc.gpsimd.memset(ones[:, :], 1.0), chain_g, pool)
                    link(nc.gpsimd.memset(eps_t[:, :], LN_EPS), chain_g, pool)
                    link(nc.gpsimd.memset(b2_split[:, :, :], 0.0), chain_g, pool)
                    link(nc.gpsimd.memset(three_ones[:, :], 1.0), chain_g, pool)
                    link(nc.gpsimd.affine_select(out=three_ones[:, :], in_=three_ones[:, :], compare_op=ALU.is_gt, fill=0.0,
                                                 base=3, pattern=[[0, P]], channel_multiplier=-1), chain_g, pool)
                    nc.gpsimd.memset(ones_b[:, :], 1.0)
                    nc.gpsimd.iota(iota_i, pattern=[[1, P]], base=0, channel_multiplier=0).then_inc(wanted.sem, 1)
                    nc.gpsimd.memset(adj_mem[:, :], 0.0)

                @block.scalar
                def _(act):
                    act.wait_ge(input_v.sem, 1)
                    nc.scalar.activation(cyc, cyc, ACT.Sin, scale=float(np.pi)).then_inc(taken_s.sem, 1)

                @block.vector
                def _(dve):
                    dve.wait_ge(edges_in.sem, 80)
                    link(nc.vector.tensor_copy(dst_groups, dst_groups_i), chain_v, dve)
                    link(nc.vector.tensor_scalar(dst_lift, dst_groups, 0.0, float(NODES), ALU.is_lt, ALU.mult), chain_v, dve)
                    link(nc.vector.tensor_tensor(dst_lift, dst_lift, dst_groups, ALU.add), chain_v, dve)
                    link(nc.vector.tensor_reduce(span[:, 0, :], dst_lift, AX.X, ALU.min), chain_v, dve)
                    nc.vector.tensor_reduce(span[:, 1, :], dst_groups, AX.X, ALU.max).then_inc(prepared.sem, 1)
                    link(nc.vector.tensor_scalar(cyc, e_weight[:, :], 1.0 / 20.0, None, ALU.mult), chain_v, dve)
                    link(nc.vector.tensor_scalar(cyc_round, cyc, 12582912.0, None, ALU.add), chain_v, dve)
                    link(nc.vector.tensor_scalar(cyc_round, cyc_round, 12582912.0, None, ALU.subtract), chain_v, dve)
                    nc.vector.tensor_tensor(cyc, cyc, cyc_round, ALU.subtract).then_inc(input_v.sem, 1)
                    link(nc.vector.tensor_scalar(rel_idx[:, :], src_idx[:, :], float(N_REL), None, ALU.mult), chain_v, dve)
                    link(nc.vector.tensor_tensor(rel_idx[:, :], rel_idx[:, :], type_i, ALU.add), chain_v, dve)
                    link(nc.vector.tensor_copy(dst_f, dst_raw), chain_v, dve)
                    dve.wait_ge(wanted.sem, 1)
                    link(nc.vector.tensor_copy(iota_f[:, :], iota_i), chain_v, dve)
                    link(nc.vector.tensor_copy(iota_b[:, :], iota_i), chain_v, dve)
                    srcs = src_idx[:, 0:A_MADE * GROUP]
                    link(nc.vector.tensor_scalar(src_part_i, srcs, P - 1, None, ALU.bitwise_and), chain_v, dve)
                    link(nc.vector.tensor_copy(a_src_part[:, :], src_part_i), chain_v, dve)
                    link(nc.vector.tensor_scalar(src_part_i, srcs, P.bit_length() - 1, None, ALU.arith_shift_right), chain_v, dve)
                    link(nc.vector.tensor_copy(a_src_tile[:, :], src_part_i), chain_v, dve)
                    rest = e_weight[:, 0:A_MADE * GROUP]
                    for k in range(3):
                        link(nc.vector.tensor_copy(a_weight[:, k, :], rest), chain_v, dve)
                        if k < 2:
                            link(nc.vector.tensor_tensor(weight_rest, rest, a_weight[:, k, :], ALU.subtract), chain_v, dve)
                            rest = weight_rest
                    nc.vector.memset(a_dst_rel[:, A_GROUPS * GROUP:], -1.0).then_inc(adj_added[0].sem, 1)
                    nc.vector.memset(fits[:, :], 0.0).then_inc(adj_added[1].sem, 1)
                    nc.vector.memset(dst_rel[:, N_GROUPS * GROUP:], -1.0).then_inc(summed.sem, 1)
                    dve.wait_ge(taken_s.sem, 1)
                    link(nc.vector.tensor_tensor(cyc, cyc, cyc, ALU.mult), chain_v, dve)
                    link(nc.vector.tensor_scalar(e_cut[:, :], cyc, -1.0, 1.0, ALU.mult, ALU.add), chain_v, dve)
                    dve.wait_ge(stage_out[0].sem, 32)
                    link(nc.vector.tensor_tensor(dst_rel[:, 0:N_GROUPS * GROUP].rearrange("p (g j) -> p g j", j=GROUP),
                                                 dst_f.rearrange("p (g j) -> p g j", j=GROUP),
                                                 base_row[:, :].rearrange("p (g o) -> p g o", o=1).broadcast_to([P, N_GROUPS, GROUP]),
                                                 ALU.subtract), chain_v, dve)
                    link(nc.vector.tensor_copy(base_i[:, :], base_row[0:1, :]), chain_v, dve)
                    link(nc.vector.tensor_tensor(span_row, max_row, base_row[:, :], ALU.subtract), chain_v, dve)
                    nc.vector.tensor_reduce(span_max[:, 0:1], span_row, AX.X, ALU.max)
                    nc.vector.tensor_reduce(span_max[:, 1:2], span_row[:, 0:A_GROUPS], AX.X, ALU.max)
                    link(nc.vector.tensor_reduce(span_max[:, 2:3], base_row[:, 0:A_GROUPS], AX.X, ALU.max), chain_v, dve)
                    link(nc.vector.tensor_copy(more_i[:, :], span_max[0:1, 0:1]), chain_v, dve)
                    link(nc.vector.tensor_scalar(more_i[:, :], more_i[:, :], WIN.bit_length() - 1, None,
                                                 ALU.arith_shift_right), chain_v, dve)
                    nc.vector.tensor_scalar(fits[:, 0:1], span_max[:, 0:1], float(WIN), None, ALU.is_lt)
                    nc.vector.tensor_scalar(fits[:, 1:2], span_max[:, 1:2], float(A_WIN), None, ALU.is_lt)
                    link(nc.vector.tensor_scalar(fits[:, 2:3], span_max[:, 2:3], float(A_COLS - A_WIN), None, ALU.is_le), chain_v, dve)
                    link(nc.vector.tensor_tensor(fits[:, 0:1], fits[:, 0:1], fits[:, 1:2], ALU.mult), chain_v, dve)
                    link(nc.vector.tensor_tensor(fits[:, 0:1], fits[:, 0:1], fits[:, 2:3], ALU.mult), chain_v, dve)
                    link(nc.vector.tensor_scalar(a_rel, dst_rel[:, 0:A_GROUPS * GROUP], 1.0, fits[:, 0:1], ALU.add, ALU.mult), chain_v, dve)
                    link(nc.vector.tensor_scalar(a_dst_rel[:, 0:A_GROUPS * GROUP], a_rel, -1.0, None, ALU.add), chain_v, dve)
                    link(nc.vector.tensor_scalar(span_row, base_row[:, :], float(A_COLS - A_WIN), None, ALU.min), chain_v, dve)
                    link(nc.vector.tensor_copy(a_base_i[:, :], span_row[0:1, :]), chain_v, dve)
                    link(nc.vector.tensor_scalar(turns_i[:, 0:1], fits[0:1, 0:1], float(A_TURNS), None, ALU.mult), chain_v, dve)
                    link(nc.vector.tensor_scalar(turns_i[:, 1:2], fits[0:1, 0:1], -float(A_TURNS), float(TURNS), ALU.mult, ALU.add),
                         chain_v, dve)

            for i in range(2):
                adj_added[i].passed(1)
            for t, n in ((edges_in, 80), (prepared, 1), (wanted, 1), (input_v, 1), (taken_s, 1), (stored, 32), (stage_out[0], 32)):
                t.passed(n)

        def fold_biases():
            with nc.Block() as block:
                @block.tensor
                def _(pe):
                    nc.tensor.matmul(ps[0][:, 0:D], ones[:, :], sq_w[:, MLP2, :], start=True, stop=True)
                    nc.tensor.matmul(ps[0][:, D:2 * D], ones[:, :], sq_w[:, LIN, :], start=True, stop=True).then_inc(made_t.sem, 1)

                @block.gpsimd
                def _(pool):
                    nc.gpsimd.memset(agg[:, :, :], 0.0)

                @block.vector
                def _(dve):
                    dve.wait_ge(made_t.sem, made_t.at(1))
                    link(nc.vector.scalar_tensor_tensor(row_vecs[:, MLP_B2, :], ps[0][:, 0:D], -LN2, row_vecs[:, MLP_B2, :],
                                                        ALU.mult, ALU.add), chain_v, dve)
                    link(nc.vector.scalar_tensor_tensor(row_vecs[:, LIN_B, :], ps[0][:, D:2 * D], -LN2, row_vecs[:, LIN_B, :],
                                                        ALU.mult, ALU.add), chain_v, dve)
                    rest = row_vecs[:, MLP_B2, :]
                    for k in range(3):
                        link(nc.vector.tensor_copy(b2_split[:, k, :], rest), chain_v, dve)
                        link(nc.vector.tensor_copy(b2_parts[:, k, :], b2_split[:, k, :]), chain_v, dve)
                        if k < 2:
                            link(nc.vector.tensor_tensor(b2_left[:, k, :], rest, b2_parts[:, k, :], ALU.subtract), chain_v, dve)
                            rest = b2_left[:, k, :]
                    link(nc.vector.tensor_scalar(b2_left[:, 0, :], b2_parts[:, 0, :], ident[:, 0:1], None, ALU.mult), chain_v, dve)
                    for k in (1, 2):
                        link(nc.vector.scalar_tensor_tensor(b2_left[:, k % 2, :], b2_parts[:, k, :], ident[:, k:k + 1],
                                                            b2_left[:, (k - 1) % 2, :], ALU.mult, ALU.add), chain_v, dve)
                    for j in range(GROUP):
                        last = nc.vector.tensor_copy(b2_split[:, j, :], b2_left[:, 0, :])
                    link(last, chain_v, dve)
            made_t.passed(1)

        def node_phase(front=None, residual=None, norm=True, weight=None, layer=None, h_table=False, to_out=False,
                       clear=False, clear_adjacency=False):
            lag = 1 if front == "softplus" else 0
            n_quads = len(QUADS)
            steps = n_quads + 3 + lag
            stage = h_rows[:, :, :].rearrange("p t f -> p (t f)")
            rel_stage = m_cols[:, :]
            if layer is not None and residual is not None:
                rel_stage = h_cols[:, 1, :]
            half = N_REL * D // 2
            Z, ADD, TURNED, PROD = ps[0], (ps[1], ps[2]), ps[3], ps[4:8]
            full_tiles = N_NODES // P

            def quad(q):
                t, n = QUADS[q]
                return t, n, slice(t * P, (t + n) * P)

            def in_range(q):
                return 0 <= q < n_quads

            with nc.Block() as block:
                @block.tensor
                def _(pe):
                    def tail(q):
                        t, n, _ = quad(q)
                        pe.wait_ge(cols_ready.sem, cols_ready.at(q + 1))
                        if weight is not None:
                            if q >= 4:
                                pe.wait_ge(taken_s.sem, taken_s.at(q - 3))
                            for i in range(n):
                                last = nc.tensor.matmul(PROD[q % 4][:, i * P:(i + 1) * P], h_cols[:, 0, (t + i) * P:(t + i + 1) * P],
                                                        weight, start=True, stop=True)
                            last.then_inc(made_t.sem, 1)
                        if layer is not None:
                            for u in range(t, t + n):
                                if u >= 2:
                                    pe.wait_ge(taken_v.sem, taken_v.at(u - 1))
                                    pe.wait_ge(taken_s.sem, taken_s.at(u - 1))
                                for part in range(2):
                                    last = nc.tensor.matmul(PROD[2 * (u % 2) + part][:, :], h_cols[:, 0, u * P:(u + 1) * P],
                                                            rel_w[:, layer, part * half:(part + 1) * half], start=True, stop=True)
                                last.then_inc(made_t.sem, 1)

                    for step in range(steps):
                        if front == "softplus" and in_range(step):
                            t, n, cols = quad(step)
                            if step:
                                pe.wait_ge(m_ready.sem, m_ready.at(step))
                            nc.tensor.matmul(Z[:, 0:n * P], sq_w[:, LIN2, :], agg[:, 0, cols], start=True, stop=True
                                             ).then_inc(z_made.sem, 1)
                        q = step - lag
                        if residual is not None and in_range(q):
                            t, n, cols = quad(q)
                            if front != "mean":
                                pe.wait_ge(m_ready.sem, m_ready.at(q + 1))
                            if q >= 2:
                                pe.wait_ge(x_ready.sem, x_ready.at(q - 1))
                            for i in range(n):
                                m = (agg[:, 0, :] if front == "mean" else m_cols)[:, (t + i) * P:(t + i + 1) * P]
                                into = ADD[q % 2][:, i * P:(i + 1) * P]
                                if residual is ident:
                                    last = nc.tensor.transpose(into, m, ident[:, :])
                                else:
                                    last = nc.tensor.matmul(into, m, residual, start=True, stop=True)
                            last.then_inc(add_made.sem, 1)
                        if in_range(q - 2) and (weight is not None or layer is not None):
                            tail(q - 2)
                        if norm and in_range(q - 1):
                            t, n, cols = quad(q - 1)
                            pe.wait_ge(rows_done.sem, rows_done.at(q))
                            if q >= 2:
                                pe.wait_ge(cols_ready.sem, cols_ready.at(q - 1))
                            for i in range(n):
                                last = nc.tensor.transpose(TURNED[:, i * P:(i + 1) * P], h_rows[:, t + i, :], ident[:, :])
                            last.then_inc(turned.sem, 1)

                @block.scalar
                def _(act):
                    nc.scalar.preload_act_table_set("natural_log_exp_and_others")

                    def tail(q):
                        t, n, cols = quad(q)
                        if weight is not None:
                            act.wait_ge(made_t.sem, made_t.at(q + 1))
                            nc.scalar.copy(stage[:, cols], PROD[q % 4][:, 0:n * P]).then_inc(taken_s.sem, 1)
                        if layer is not None:
                            for u in range(t, t + n):
                                if u >= 3:
                                    act.wait_ge(stage_out[u % 3].sem, stage_out[u % 3].at(16 * (u // 3)))
                                act.wait_ge(made_t.sem, made_t.at(u + 1))
                                o = (u % 3) * N_REL * D + half
                                nc.scalar.copy(rel_stage[:, o:o + half], PROD[2 * (u % 2) + 1][:, :]).then_inc(taken_s.sem, 1)

                    for step in range(steps):
                        q = step - lag - 1
                        if front in ("softplus", "selu") and in_range(step):
                            t, n, cols = quad(step)
                            act.wait_ge(capped_z.sem, capped_z.at(step + 1))
                            nc.scalar.activation(m_cols[:, cols], m_cols[:, cols], ACT.Exp).then_inc(prepared.sem, 1)
                            if front == "softplus":
                                act.wait_ge(prepared.sem, prepared.at(step + 1))
                                nc.scalar.activation(m_cols[:, cols], m_cols[:, cols], ACT.Ln, bias=ones[:, 0:1]).then_inc(logs_made.sem, 1)
                        if norm and in_range(q):
                            t, n, cols = quad(q)
                            act.wait_ge(x_ready.sem, x_ready.at(q + 1))
                            nc.scalar.activation(ln_std[:, t:t + n], mean_var[:, t:t + n, 1], ACT.Ln, bias=eps_t[:, :]
                                                 ).then_inc(chain_s.sem, 1)
                            act.wait_ge(chain_s.sem, chain_s.at(q + 1))
                            nc.scalar.activation(ln_scale[:, t:t + n], ln_std[:, t:t + n], ACT.Exp, scale=-0.5).then_inc(scale_ready.sem, 1)
                            act.wait_ge(shift_ready.sem, shift_ready.at(q + 1))
                            for u in range(t, t + n):
                                last = nc.scalar.activation(h_rows[:, u, :], x_rows[:, u, :], ACT.Relu, bias=ln_shift[:, u:u + 1],
                                                            scale=ln_scale[:, u:u + 1])
                            last.then_inc(rows_done.sem, 1)
                        if in_range(q - 1) and (weight is not None or layer is not None):
                            tail(q - 1)

                @block.vector
                def _(dve):
                    def tail(q):
                        t, n, cols = quad(q)
                        for u in range(t, t + n):
                            if u >= 3:
                                dve.wait_ge(stage_out[u % 3].sem, stage_out[u % 3].at(16 * (u // 3)))
                            dve.wait_ge(made_t.sem, made_t.at(u + 1))
                            o = (u % 3) * N_REL * D
                            nc.vector.tensor_copy(rel_stage[:, o:o + half], PROD[2 * (u % 2)][:, :]).then_inc(taken_v.sem, 1)

                    for step in range(steps):
                        q = step - lag - 1
                        if in_range(step):
                            t, n, cols = quad(step)
                            src, into = agg[:, 0, cols], m_cols[:, cols]
                            if front == "relu":
                                if norm:
                                    nc.vector.tensor_scalar(into, src, 0.0, None, ALU.max).then_inc(m_ready.sem, 1)
                                else:
                                    nc.vector.tensor_scalar(h_cols[:, 0, cols], src, 0.0, None, ALU.max).then_inc(cols_ready.sem, 1)
                            if front == "selu":
                                nc.vector.tensor_scalar(into, src, 0.0, None, ALU.min).then_inc(capped_z.sem, 1)
                                nc.vector.tensor_scalar(src, src, 0.0, SELU_SCALE, ALU.max, ALU.mult).then_inc(logs_made.sem, 1)
                            if front == "softplus":
                                dve.wait_ge(z_made.sem, z_made.at(step + 1))
                                nc.vector.tensor_scalar(into, Z[:, 0:n * P], vecs[:, LIN2_B:LIN2_B + 1], EXP_CAP, ALU.add, ALU.min
                                                        ).then_inc(capped_z.sem, 1)
                        if in_range(q):
                            t, n, cols = quad(q)
                            if residual is not None:
                                dve.wait_ge(add_made.sem, add_made.at(q + 1))
                                xs = x_rows[:, t:t + n, :].rearrange("p t f -> p (t f)")
                                if front == "mean":
                                    for i in range(n):
                                        last = nc.vector.scalar_tensor_tensor(x_rows[:, t + i, :], ADD[q % 2][:, i * P:(i + 1) * P],
                                                                              inv_count[:, t + i:t + i + 1], x_rows[:, t + i, :],
                                                                              ALU.mult, ALU.add)
                                else:
                                    last = nc.vector.tensor_tensor(xs, xs, ADD[q % 2][:, 0:n * P], ALU.add)
                                if norm:
                                    last.then_inc(chain_v.sem, 1)
                                    dve.wait_ge(chain_v.sem, chain_v.at(2 * q + 1))
                                else:
                                    last.then_inc(x_ready.sem, 1)
                            if norm:
                                for u in range(t, t + n):
                                    last = nc.vector.bn_stats(stats[:, u, :], x_rows[:, u, :])
                                last.then_inc(chain_v.sem, 1)
                                dve.wait_ge(chain_v.sem, chain_v.at((2 if residual is not None else 1) * (q + 1)))
                                for u in range(t, t + n):
                                    last = nc.vector.bn_aggr(mean_var[:, u, :], stats[:, u, :])
                                last.then_inc(x_ready.sem, 1)
                        if norm and in_range(q - 1):
                            t, n, cols = quad(q - 1)
                            dve.wait_ge(turned.sem, turned.at(q))
                            nc.vector.tensor_copy(h_cols[:, 0, cols], TURNED[:, 0:n * P]).then_inc(cols_ready.sem, 1)
                        if norm and in_range(q):
                            t, n, cols = quad(q)
                            dve.wait_ge(scale_ready.sem, scale_ready.at(q + 1))
                            nc.vector.scalar_tensor_tensor(ln_shift[:, t:t + n], mean_var[:, t:t + n, 0], -1.0, ln_scale[:, t:t + n],
                                                           ALU.mult, ALU.mult).then_inc(shift_ready.sem, 1)
                        if in_range(step):
                            t, n, cols = quad(step)
                            into = m_cols[:, cols]
                            if front == "softplus":
                                dve.wait_ge(logs_made.sem, logs_made.at(step + 1))
                                nc.vector.scalar_tensor_tensor(into, Z[:, 0:n * P], vecs[:, LIN2_B:LIN2_B + 1], into,
                                                               ALU.add, ALU.max).then_inc(m_ready.sem, 1)
                            if front == "selu":
                                dve.wait_ge(prepared.sem, prepared.at(step + 1))
                                nc.vector.tensor_scalar(into, into, SELU_SCALE * SELU_ALPHA, -SELU_SCALE * SELU_ALPHA,
                                                        ALU.mult, ALU.add).then_inc(logs_made.sem, 1)
                                dve.wait_ge(logs_made.sem, logs_made.at(2 * (step + 1)))
                                nc.vector.tensor_tensor(into, into, agg[:, 0, cols], ALU.add).then_inc(m_ready.sem, 1)
                        if layer is not None and in_range(q - 1):
                            tail(q - 1)

                @block.gpsimd
                def _(pool):
                    if clear_adjacency:
                        nc.gpsimd.memset(adj_mem[:, :], 0.0)
                    if clear:
                        pool.wait_ge(add_made.sem, add_made.at(n_quads))
                        nc.gpsimd.memset(agg[:, 0, :], 0.0)

                @block.sync
                def _(sp):
                    rows_out = table.rearrange("(t p) f -> p t f", p=P)
                    if h_table or weight is not None:
                        for q0, q1 in ((0, 3), (3, 6), (6, 7)):
                            t0, t1 = QUADS[q0][0], QUADS[q1 - 1][0] + QUADS[q1 - 1][1]
                            if h_table:
                                sp.wait_ge(rows_done.sem, rows_done.at(q1))
                            else:
                                sp.wait_ge(taken_s.sem, taken_s.at(q1))
                            sp.dma_start(rows_out[:, t0:t1, :], h_rows[:, t0:t1, :]).then_inc(stored.sem, 16)
                        sp.wait_ge(stored.sem, stored.at(48))
                    if layer is not None:
                        for t in range(N_TILES):
                            sp.wait_ge(taken_v.sem, taken_v.at(t + 1))
                            sp.wait_ge(taken_s.sem, taken_s.at(t + 1))
                            o = (t % 3) * N_REL * D
                            sp.dma_start(rel_table[t * P * N_REL:(t + 1) * P * N_REL, :].rearrange("(p r) f -> p (r f)", r=N_REL),
                                         rel_stage[:, o:o + N_REL * D]).then_inc(stage_out[t % 3].sem, 16)
                        for i in range(3):
                            sp.wait_ge(stage_out[i].sem, stage_out[i].at(16 * len(range(i, N_TILES, 3))))
                    if to_out:
                        for q in range(n_quads):
                            t, n, _ = quad(q)
                            sp.wait_ge(x_ready.sem, x_ready.at(q + 1))
                            full = min(t + n, full_tiles) - t
                            if full:
                                sp.dma_start(out[t * P:(t + full) * P, :].rearrange("(t p) f -> p t f", p=P),
                                             x_rows[:, t:t + full, :]).then_inc(stored.sem, 16)
                            else:
                                sp.dma_start(out[t * P:N_NODES, :], x_rows[0:N_NODES - t * P, t, :]).then_inc(stored.sem, 16)
                        sp.wait_ge(stored.sem, stored.at(16 * n_quads))

            def count(t, n):
                if n:
                    t.passed(n)

            count(m_ready, n_quads if front in ("softplus", "selu") or (front == "relu" and norm) else 0)
            count(z_made, n_quads if front == "softplus" else 0)
            count(capped_z, n_quads if front in ("softplus", "selu") else 0)
            count(prepared, n_quads if front in ("softplus", "selu") else 0)
            count(logs_made, {"softplus": 1, "selu": 2}.get(front, 0) * n_quads)
            count(add_made, n_quads if residual is not None else 0)
            count(x_ready, n_quads if norm or residual is not None else 0)
            count(chain_v, ((2 if residual is not None else 1) * n_quads) if norm else 0)
            for t in (chain_s, scale_ready, shift_ready, rows_done, turned):
                count(t, n_quads if norm else 0)
            count(cols_ready, n_quads if norm or layer is not None else 0)
            count(made_t, n_quads if weight is not None else N_TILES if layer is not None else 0)
            count(taken_s, n_quads if weight is not None else N_TILES if layer is not None else 0)
            count(taken_v, N_TILES if layer is not None else 0)
            count(stored, 48 if h_table or weight is not None else 16 * n_quads if to_out else 0)
            if layer is not None:
                for i in range(3):
                    stage_out[i].passed(16 * len(range(i, N_TILES, 3)))

        def sage_hidden():
            n_quads = len(QUADS)
            before = h_rows[:, :, :].rearrange("p t f -> p (t f)"), h_cols[:, 1, :]
            pieces = [(c, min(BANK, N_NODES - c)) for c in range(0, N_NODES, BANK)]
            with nc.Block() as block:
                @block.tensor
                def _(pe):
                    for t in range(N_TILES):
                        last = nc.tensor.matmul(ps[7][:, t:t + 1], agg[:, 1, t * P:(t + 1) * P], ident[:, 0:1], start=True, stop=True)
                    last.then_inc(add_made.sem, 1)

                    def inverses(q):
                        t, n = QUADS[q]
                        pe.wait_ge(capped_z.sem, capped_z.at(q + 1))
                        if q >= 2:
                            pe.wait_ge(m_ready.sem, m_ready.at(q - 1))
                        nc.tensor.matmul(ps[6 + q % 2][:, 0:n * P], ones[:, :], h_cols[:, 1, t * P:(t + n) * P], start=True, stop=True
                                         ).then_inc(z_made.sem, 1)

                    inverses(0)
                    inverses(1)
                    for q, (t, n) in enumerate(QUADS):
                        cols = slice(t * P, (t + n) * P)
                        pe.wait_ge(m_ready.sem, m_ready.at(q + 1))
                        for f in range(H2):
                            k = q * H2 + f
                            if k >= 6:
                                pe.wait_ge(taken_s.sem, taken_s.at(k - 5))
                            nc.tensor.matmul(ps[k % 6][:, 0:n * P], w1lr[:, 0, f * D:(f + 1) * D], m_cols[:, cols], start=True, stop=False)
                            nc.tensor.matmul(ps[k % 6][:, 0:n * P], w1lr[:, 1, f * D:(f + 1) * D], h_cols[:, 0, cols],
                                             start=False, stop=True).then_inc(made_t.sem, 1)
                        if q + 2 < n_quads:
                            inverses(q + 2)
                    for q, (t, n) in enumerate(QUADS):
                        pe.wait_ge(cols_ready.sem, cols_ready.at(H2 * (q + 1)))
                        if q >= 4:
                            pe.wait_ge(taken_v.sem, taken_v.at(q - 3))
                        for i in range(n):
                            for f in range(H2):
                                last = nc.tensor.matmul(ps[q % 4][:, i * P:(i + 1) * P], h_cols[:, f, (t + i) * P:(t + i + 1) * P],
                                                        w2lr[:, f, 0:D], start=(f == 0), stop=(f == H2 - 1))
                        last.then_inc(turned.sem, 1)

                @block.scalar
                def _(act):
                    nc.scalar.preload_act_table_set("natural_log_exp_and_others")
                    for q, (t, n) in enumerate(QUADS):
                        for f in range(H2):
                            k = q * H2 + f
                            act.wait_ge(made_t.sem, made_t.at(k + 1))
                            nc.scalar.activation(before[f][:, t * P:(t + n) * P], ps[k % 6][:, 0:n * P], ACT.Identity,
                                                 bias=bn_vec[:, 0, f:f + 1]).then_inc(taken_s.sem, 1)
                    act.wait_ge(x_ready.sem, x_ready.at(1))
                    nc.scalar.activation(ln_std[:, 0:H2], mean_var[:, 0:H2, 1], ACT.Ln, bias=eps_t[:, :]).then_inc(chain_s.sem, 1)
                    act.wait_ge(chain_s.sem, chain_s.at(1))
                    nc.scalar.activation(ln_std[:, 0:H2], ln_std[:, 0:H2], ACT.Exp, scale=-0.5).then_inc(scale_ready.sem, 1)
                    act.wait_ge(shift_ready.sem, shift_ready.at(1))
                    for q, (t, n) in enumerate(QUADS):
                        cols = slice(t * P, (t + n) * P)
                        for f in range(H2):
                            nc.scalar.activation(h_cols[:, f, cols], before[f][:, cols], ACT.Relu, bias=ln_shift[:, f:f + 1],
                                                 scale=ln_scale[:, f:f + 1]).then_inc(cols_ready.sem, 1)

                @block.vector
                def _(dve):
                    def means(q):
                        t, n = QUADS[q]
                        cols = slice(t * P, (t + n) * P)
                        dve.wait_ge(z_made.sem, z_made.at(q + 1))
                        nc.vector.tensor_tensor(m_cols[:, cols], agg[:, 0, cols], ps[6 + q % 2][:, 0:n * P], ALU.mult
                                                ).then_inc(m_ready.sem, 1)

                    dve.wait_ge(add_made.sem, add_made.at(1))
                    link(nc.vector.tensor_scalar(inv_count[:, :], ps[7][:, 0:N_TILES], 1.0, None, ALU.max), chain_v, dve)
                    link(nc.vector.reciprocal(inv_count[:, :], inv_count[:, :]), chain_v, dve)
                    for q, (t, n) in enumerate(QUADS):
                        eye = ident[:, :].rearrange("p (o c) -> p o c", o=1).broadcast_to([P, n, P])
                        inv = inv_count[:, t:t + n].rearrange("p (t o) -> p t o", o=1).broadcast_to([P, n, P])
                        nc.vector.tensor_tensor(h_cols[:, 1, t * P:(t + n) * P].rearrange("p (t c) -> p t c", c=P), eye, inv, ALU.mult
                                                ).then_inc(capped_z.sem, 1)
                        if q >= 1:
                            means(q - 1)
                    means(n_quads - 1)
                    for i, (c, n) in enumerate(pieces):
                        for f in range(H2):
                            dve.wait_ge(taken_s.sem, taken_s.at(i * H2 + f + 1))
                            last = nc.vector.bn_stats(stats[:, f * len(pieces) + i, :], before[f][:, c:c + n])
                    link(last, chain_v, dve)
                    for f in range(H2):
                        last = nc.vector.bn_aggr(mean_var[:, f, :], stats[:, f * len(pieces):(f + 1) * len(pieces), :]
                                                 .rearrange("p s k -> p (s k)"))
                    last.then_inc(x_ready.sem, 1)
                    dve.wait_ge(scale_ready.sem, scale_ready.at(1))
                    link(nc.vector.tensor_tensor(ln_scale[:, 0:H2], ln_std[:, 0:H2], bn_vec[:, 1, :], ALU.mult), chain_v, dve)
                    link(nc.vector.tensor_tensor(ln_shift[:, 0:H2], mean_var[:, 0:H2, 0], ln_scale[:, 0:H2], ALU.mult), chain_v, dve)
                    nc.vector.tensor_tensor(ln_shift[:, 0:H2], bn_vec[:, 2, :], ln_shift[:, 0:H2], ALU.subtract).then_inc(shift_ready.sem, 1)
                    for q, (t, n) in enumerate(QUADS):
                        cols = slice(t * P, (t + n) * P)
                        dve.wait_ge(turned.sem, turned.at(q + 1))
                        nc.vector.tensor_copy(before[0][:, cols], ps[q % 4][:, 0:n * P]).then_inc(taken_v.sem, 1)

                @block.gpsimd
                def _(pool):
                    pool.wait_ge(m_ready.sem, m_ready.at(n_quads))
                    nc.gpsimd.memset(agg[:, 0, :], 0.0)

                @block.sync
                def _(sp):
                    rows_out = table.rearrange("(t p) f -> p t f", p=P)
                    for q0, q1 in ((0, 3), (3, 6), (6, 7)):
                        t0, t1 = QUADS[q0][0], QUADS[q1 - 1][0] + QUADS[q1 - 1][1]
                        sp.wait_ge(taken_v.sem, taken_v.at(q1))
                        sp.dma_start(rows_out[:, t0:t1, :], h_rows[:, t0:t1, :]).then_inc(stored.sem, 16)
                    sp.wait_ge(stored.sem, stored.at(48))
            for t, n in ((m_ready, n_quads), (made_t, H2 * n_quads), (taken_s, H2 * n_quads), (cols_ready, H2 * n_quads),
                         (turned, n_quads), (taken_v, n_quads), (chain_s, 1), (x_ready, 1), (scale_ready, 1), (shift_ready, 1),
                         (stored, 48), (z_made, n_quads), (capped_z, n_quads), (add_made, 1)):
                t.passed(n)

        rounds, spared, hots_ahead = [0], [0], [0]
        columns = [nc.vector.alloc_register(f"column{s}") for s in range(SLOTS)]
        further = nc.vector.alloc_register("further")
        turn_register = nc.vector.alloc_register("turn_register")
        a_columns = [nc.vector.alloc_register(f"a_column{m}") for m in range(A_PER_TURN)]

        def edge_round(source, indices, weights=None, counts=False, filters=False, add_rows=None, start=None, residual=False,
                       by_adjacency=False, first_product=False, build=None):
            r, before = rounds[0], spared[0]
            rounds[0] += 1
            spared[0] += by_adjacency
            hots_before = hots_ahead[0]
            hots_ahead[0] += 2 if filters else 1
            SUMS, W_BANK, Z_BANK = (ps[0], ps[1]), (ps[2], ps[3]), ps[4:8]
            ADJ, A_COUNTS, PRODUCT = (ps[2], ps[3]), (ps[4], ps[5]), ps[5]
            planes = 2 if counts else 1
            kind, per_turn, a_first = build if build else (0, 0, 0)
            a_adds = 2 if counts else 1
            a_pairs, a_made, a_added = pairs_ready[kind], adj_made[kind], adj_added[kind]

            def more_windows(eng):
                return eng.value_load(more_i[0:1, 0:1], min_val=0, max_val=NODES // WIN)

            def turns_of(eng):
                skip = eng.value_load(turns_i[0:1, 0:1], min_val=0, max_val=A_TURNS)
                left = eng.value_load(turns_i[0:1, 1:2], min_val=TURNS - A_TURNS, max_val=TURNS)
                done = left * (SLOTS * before) + (r - before) * N_GROUPS
                return (skip, left, done) if by_adjacency else (0, TURNS, done)

            def sum_of(bank):
                return bank[:, 0:planes * WIN].rearrange("p (a w) -> p a w", w=WIN)

            with nc.Block() as block:
                @block.gpsimd
                def _(pool):
                    skip, left, done = turns_of(pool)
                    with pool.Fori(0, left) as turn:
                        for s in range(SLOTS):
                            pool.wait_ge(idx_ready.sem, turn * SLOTS + done + (r * SLOTS + s + 1))
                            pool.sem_inc(turn_begun.sem, 1)
                            for j in range(GROUP):
                                nc.gpsimd.indirect_dma_start(rows[:, s, j, :], None, source,
                                                             bass.IndirectOffsetOnAxis(ap=cur_idx[:, s, j:j + 1], axis=0)
                                                             ).then_inc(gathered[s].sem, 16)

                if filters:
                    @block.sync
                    def _(sp):
                        cols = a["attr_cols"]
                        for s in range(SLOTS):
                            sp.dma_start(attr[:, s, :], cols[:, s * G_EDGES:(s + 1) * G_EDGES]).then_inc(attr_in[s].sem, 16)
                        with sp.Fori(1, ATTR_TURNS) as turn:
                            for s in range(SLOTS):
                                sp.wait_ge(z_ready.sem, turn * SLOTS + (s + 1 - SLOTS))
                                sp.dma_start(attr[:, s, :], cols[:, bass.ds(turn * (SLOTS * G_EDGES) + s * G_EDGES, G_EDGES)]
                                             ).then_inc(attr_in[s].sem, 16)
                        for s in range(SLOTS):
                            sp.wait_ge(attr_in[s].sem, 16 * ATTR_TURNS)

                @block.tensor
                def _(pe):
                    more = more_windows(pe)
                    skip, left, done = turns_of(pe)
                    if start:
                        for q, (t, n) in enumerate(QUADS):
                            if q >= 2:
                                pe.wait_ge(taken_s.sem, taken_s.at(q - 1))
                            nc.tensor.matmul(ps[6 + q % 2][:, 0:n * P], start[0], h_cols[:, 0, t * P:(t + n) * P], start=True, stop=True
                                             ).then_inc(made_t.sem, 1)
                    if residual:
                        for q, (t, n) in enumerate(QUADS):
                            if q >= 2:
                                pe.wait_ge(taken_v.sem, taken_v.at(q - 1))
                            for i in range(n):
                                for f in range(H2):
                                    last = nc.tensor.matmul(ps[6 + q % 2][:, i * P:(i + 1) * P], h_cols[:, f, (t + i) * P:(t + i + 1) * P],
                                                            w2lr[:, f, D:2 * D], start=(f == 0), stop=(f == H2 - 1))
                            last.then_inc(made_t.sem, 1)

                    def first_layer(slot, load):
                        pe.wait_ge(attr_in[slot].sem, load * 16)
                        nc.tensor.matmul(Z_BANK[slot][:, :], mlp_w1[:, :], attr[:, slot, :], start=True, stop=True
                                         ).then_inc(z_ready.sem, 1)

                    def second_layer(slot, filt_count):
                        pe.wait_ge(filt_ready.sem, filt_count)
                        for j in range(GROUP):
                            wj = W_BANK[slot % 2][:, j * D:(j + 1) * D]
                            nc.tensor.matmul(wj, filt[:, slot, j * P:(j + 1) * P], sq_w[:, MLP2, :], start=True, stop=False)
                            last = nc.tensor.matmul(wj, three_ones[:, :], b2_split[:, j, :], start=False, stop=True)
                        last.then_inc(w_ready.sem, 1)

                    def sums(s, hot, into, done):
                        for j in range(GROUP):
                            last = nc.tensor.matmul(into[:, 0:WIN], rows[:, s, j, :], hot[:, j, :], start=(j == 0), stop=(j == GROUP - 1))
                        if counts:
                            for j in range(GROUP):
                                last = nc.tensor.matmul(into[:, WIN:2 * WIN], ones[:, :], hot[:, j, :], start=(j == 0), stop=(j == GROUP - 1))
                        last.then_inc(done.sem, 1)

                    def scatter(turn, s):
                        if filters:
                            pe.wait_ge(weighed.sem, turn * SLOTS + (s + 1))
                        else:
                            pe.wait_ge(gathered[s].sem, (turn * SLOTS + done) * 16 + 16 * GROUP)
                        pe.wait_ge(onehot_ready.sem, turn * SLOTS + done + (hots_before + s + 1))
                        sums(s, onehot[:, s % 2, :, :], SUMS[s % 2], scattered)
                        with pe.If(more > 0):
                            with pe.Fori(0, more) as w:
                                n = (turn * SLOTS + done + s) * more + w
                                pe.wait_ge(more_hot.sem, n + 1)
                                sums(s, hot_more[:, :, :], SUMS[s % 2], more_sums)

                    def join_pairs(turn, m):
                        pe.wait_ge(a_pairs.sem, turn * per_turn + (a_pairs.value + m + 1))
                        for j in range(GROUP):
                            pairs = pair_hot[m % 2][:, j, :, :].rearrange("p t w -> p (t w)")
                            for k in range(3 if kind else 1):
                                part = weight_hot[:, k, j, :] if kind else part_hot[m % 2][:, j, :]
                                last = nc.tensor.matmul(ADJ[m % 2][:, 0:N_TILES * A_WIN], part, pairs, start=(j == 0 and k == 0),
                                                        stop=(j == GROUP - 1 and k == (2 if kind else 0)))
                        if counts:
                            for j in range(GROUP):
                                last = nc.tensor.matmul(A_COUNTS[m % 2][:, 0:A_WIN], ones_b[:, :], dst_hot[:, m % 2, j, :],
                                                        start=(j == 0), stop=(j == GROUP - 1))
                        last.then_inc(a_made.sem, 1)

                    def product():
                        for t in range(N_TILES):
                            last = nc.tensor.matmul(PRODUCT[:, 0:A_COLS], h_rows[:, t, :], adj[:, t, :], start=(t == 0),
                                                    stop=(t == N_TILES - 1))
                        last.then_inc(product_made.sem, 1)

                    if by_adjacency and first_product:
                        product()
                    if filters:
                        for s in range(SLOTS):
                            first_layer(s, 1)
                        for s in range(2):
                            second_layer(s, s + 1)
                            first_layer(s, 2)
                    with pe.Fori(0, left) as turn:
                        for pair in range(0, SLOTS, 2):
                            for s in (pair, pair + 1):
                                scatter(turn, s)
                                if 1 <= s <= per_turn:
                                    join_pairs(turn, s - 1)
                            if filters:
                                for s in (pair + 2, pair + 3):
                                    second_layer(s % SLOTS, turn * SLOTS + (s + 1))
                                for s in (pair + 2, pair + 3):
                                    first_layer(s % SLOTS, turn + (2 if s < SLOTS else 3))
                    if by_adjacency and not first_product:
                        pe.wait_ge(a_added.sem, left * (per_turn * a_adds) + a_added.value)
                        product()

                if start:
                    @block.scalar
                    def _(act):
                        for q, (t, n) in enumerate(QUADS):
                            act.wait_ge(made_t.sem, made_t.at(q + 1))
                            nc.scalar.activation(agg[:, 0, t * P:(t + n) * P], ps[6 + q % 2][:, 0:n * P], ACT.Identity,
                                                 bias=start[1], scale=start[2]).then_inc(taken_s.sem, 1)

                if filters:
                    @block.scalar
                    def _(act):
                        nc.scalar.preload_act_table_set("natural_log_exp_and_others")

                        def logs(parity, count):
                            act.wait_ge(z_capped.sem, count)
                            nc.scalar.activation(soft[:, parity, :], soft[:, parity, :], ACT.Exp).then_inc(exp_ready.sem, 1)
                            act.wait_ge(exp_ready.sem, count)
                            nc.scalar.activation(soft[:, parity, :], soft[:, parity, :], ACT.Ln, bias=ones[:, 0:1]
                                                 ).then_inc(ln_ready.sem, 1)

                        for s in range(SLOTS):
                            logs(s % 2, s + 1)
                        with act.Fori(1, TURNS + 1) as turn:
                            for s in range(SLOTS):
                                logs(s % 2, turn * SLOTS + (s + 1))

                @block.vector
                def _(dve):
                    more = more_windows(dve)
                    skip, left, done = turns_of(dve)
                    for s in range(SLOTS):
                        nc.vector.tensor_copy(cur_idx[:, s, :], indices[:, bass.ds(skip * (SLOTS * GROUP) + s * GROUP, GROUP)]
                                              ).then_inc(idx_ready.sem, 1)
                    if add_rows is not None:
                        row = row_vecs[:, add_rows, :].rearrange("p (o f) -> p o f", o=1).broadcast_to([P, N_TILES, D])
                        nc.vector.tensor_tensor(x_rows[:, :, :], x_rows[:, :, :], row, ALU.add)
                    if residual:
                        for q, (t, n) in enumerate(QUADS):
                            dve.wait_ge(made_t.sem, made_t.at(q + 1))
                            xs = x_rows[:, t:t + n, :].rearrange("p t f -> p (t f)")
                            nc.vector.tensor_tensor(xs, xs, ps[6 + q % 2][:, 0:n * P], ALU.add).then_inc(taken_v.sem, 1)

                    def one_hots(hot, window, edges, group, weight_group=None):
                        if weights is None:
                            off = edges[:, bass.ds(group * GROUP, GROUP)].rearrange("p (j o) -> p j o", o=1)
                            last = nc.vector.tensor_tensor(hot, window.rearrange("p (o c) -> p o c", o=1).broadcast_to([P, GROUP, WIN]),
                                                           off.broadcast_to([P, GROUP, WIN]), ALU.is_equal)
                        else:
                            weight_at = (group if weight_group is None else weight_group) * GROUP
                            for j in range(GROUP):
                                edge = bass.ds(group * GROUP + j, 1)
                                last = nc.vector.tensor_scalar(hot[:, j, :], window, edges[:, edge], weights[:, bass.ds(weight_at + j, 1)],
                                                               ALU.is_equal, ALU.mult)
                        return last

                    def cap(slot, count, first=False):
                        dve.wait_ge(z_ready.sem, count)
                        if not first:
                            dve.wait_ge(filt_ready.sem, count - 2)
                        nc.vector.tensor_scalar(soft[:, slot % 2, :], Z_BANK[slot][:, :], vecs[:, MLP_B1:MLP_B1 + 1], EXP_CAP,
                                                ALU.add, ALU.min).then_inc(z_capped.sem, 1)

                    def softplus(slot, count):
                        dve.wait_ge(ln_ready.sem, count)
                        nc.vector.scalar_tensor_tensor(filt[:, slot, :], Z_BANK[slot][:, :], vecs[:, MLP_B1:MLP_B1 + 1],
                                                       soft[:, slot % 2, :], ALU.add, ALU.max).then_inc(filt_ready.sem, 1)

                    def weigh(turn, s):
                        dve.wait_ge(w_ready.sem, turn * SLOTS + (s + 1))
                        dve.wait_ge(gathered[s].sem, (turn * SLOTS + done) * 16 + 16 * GROUP)
                        msg = rows[:, s, :, :].rearrange("p j f -> p (j f)")
                        nc.vector.tensor_tensor(msg, msg, W_BANK[s % 2][:, :], ALU.mult).then_inc(weighed.sem, 1)

                    def next_one_hots(turn, at_turn, s):
                        one_hots(onehot[:, s % 2, :, :], iota_f[:, 0:WIN], dst_rel, at_turn * SLOTS + s).then_inc(onehot_ready.sem, 1)

                    def add_sums(turn, at_turn, s):
                        column = dve.snap(columns[s], min_val=0, max_val=NODES)
                        dve.wait_ge(scattered.sem, turn * SLOTS + done + (s + 1))
                        dve.wait_ge(summed.sem, turn * SLOTS + done + (s + 1))
                        if build and counts:
                            dve.wait_ge(a_added.sem, (turn * per_turn + min(max(s - 1, 0), per_turn)) * a_adds + a_added.value)
                        into = agg[:, 0:planes, bass.ds(column, WIN)]
                        nc.vector.tensor_tensor(into, into, sum_of(SUMS[s % 2]), ALU.add).then_inc(summed.sem, 1)
                        with dve.If(more > 0):
                            first_more = (turn * SLOTS + done + s) * more
                            first_rel = (turn * SLOTS + done + s) * (more + 1)
                            nc.vector.tensor_scalar(further_rel[:, :], dst_rel[:, bass.ds(at_turn * (SLOTS * GROUP) + s * GROUP, GROUP)],
                                                    float(WIN), None, ALU.subtract).then_inc(more_rel.sem, 1)
                            with dve.Fori(0, more) as w:
                                dve.wait_ge(more_rel.sem, first_rel + w + 1)
                                one_hots(hot_more[:, :, :], iota_f[:, 0:WIN], further_rel, 0,
                                         at_turn * SLOTS + s).then_inc(more_hot.sem, 1)
                                dve.reg_alu(further, columns[s], (w + 1) * WIN, ALU.add)
                                dve.reg_alu(further, further, NODES, ALU.min)
                                column = dve.snap(further, min_val=0, max_val=NODES)
                                dve.wait_ge(more_sums.sem, first_more + w + 1)
                                into = agg[:, 0:planes, bass.ds(column, WIN)]
                                nc.vector.tensor_tensor(into, into, sum_of(SUMS[s % 2]), ALU.add).then_inc(more_summed.sem, 1)
                                nc.vector.tensor_scalar(further_rel[:, :], further_rel[:, :], float(WIN), None, ALU.subtract
                                                        ).then_inc(more_rel.sem, 1)
                                dve.wait_ge(more_summed.sem, first_more + w + 1)
                                dve.wait_ge(more_rel.sem, first_rel + w + 2)
                        nc.vector.tensor_copy(cur_idx[:, s, :], indices[:, bass.ds(at_turn * (SLOTS * GROUP) + (s + SLOTS) * GROUP, GROUP)]
                                              ).then_inc(idx_ready.sem, 1)

                    def pair_one_hots(turn, m):
                        at = bass.ds((turn * per_turn + (a_first + m)) * GROUP, GROUP)

                        def hot(into, edges, n):
                            off = edges.rearrange("p (j o) -> p j o", o=1).broadcast_to([P, GROUP, n])
                            return nc.vector.tensor_tensor(into, iota_b[:, 0:n].rearrange("p (o c) -> p o c", o=1).broadcast_to([P, GROUP, n]),
                                                           off, ALU.is_equal)

                        n_hots = turn * (2 * per_turn) + (hots_linked[kind].value + 2 * m)
                        hot(tile_hot[:, m % 2, :, :], a_src_tile[:, at], N_TILES)
                        hot(dst_hot[:, m % 2, :, :], a_dst_rel[:, at], A_WIN).then_inc(hots_linked[kind].sem, 1)
                        hot(part_hot[m % 2], a_src_part[:, at], P).then_inc(hots_linked[kind].sem, 1)
                        dve.wait_ge(hots_linked[kind].sem, n_hots + 1)
                        pairs = nc.vector.tensor_tensor(
                            pair_hot[m % 2],
                            tile_hot[:, m % 2, :, :].rearrange("p j (t o) -> p j t o", o=1).broadcast_to([P, GROUP, N_TILES, A_WIN]),
                            dst_hot[:, m % 2, :, :].rearrange("p j (o w) -> p j o w", o=1).broadcast_to([P, GROUP, N_TILES, A_WIN]), ALU.mult)
                        if kind:
                            dve.wait_ge(hots_linked[kind].sem, n_hots + 2)
                            for k in range(3):
                                w = a_weight[:, k, at].rearrange("p (j o) -> p j o", o=1).broadcast_to([P, GROUP, P])
                                pairs = nc.vector.tensor_tensor(weight_hot[:, k, :, :], part_hot[m % 2], w, ALU.mult)
                        pairs.then_inc(a_pairs.sem, 1)

                    def add_pairs(turn, m):
                        column = dve.snap(a_columns[m], min_val=0, max_val=A_COLS - A_WIN)
                        dve.wait_ge(a_made.sem, turn * per_turn + (a_made.value + m + 1))
                        dve.wait_ge(a_added.sem, (turn * per_turn + m) * a_adds + a_added.value)
                        into = adj[:, :, bass.ds(column, A_WIN)]
                        nc.vector.tensor_tensor(into, into, ADJ[m % 2][:, 0:N_TILES * A_WIN].rearrange("p (t w) -> p t w", w=A_WIN), ALU.add
                                                ).then_inc(a_added.sem, 1)
                        if counts:
                            dve.wait_ge(summed.sem, turn * SLOTS + done + (m + 3))
                            into = agg[:, 1, bass.ds(column, A_WIN)]
                            nc.vector.tensor_tensor(into, into, A_COUNTS[m % 2][:, 0:A_WIN], ALU.add).then_inc(a_added.sem, 1)

                    def add_product():
                        dve.wait_ge(product_made.sem, product_made.at(1))
                        into = agg[:, 0, 0:A_COLS]
                        link(nc.vector.tensor_tensor(into, into, PRODUCT[:, 0:A_COLS], ALU.add), chain_v, dve)

                    if filters:
                        cap(0, 1, first=True)
                        cap(1, 2, first=True)
                        softplus(0, 1)
                        cap(2, 3)
                        softplus(1, 2)
                        cap(3, 4)
                        softplus(2, 3)
                        softplus(3, 4)
                        for s in range(2):
                            next_one_hots(0, skip, s)
                    else:
                        next_one_hots(0, skip, 0)
                    if start:
                        dve.wait_ge(taken_s.sem, taken_s.at(len(QUADS)))
                    if by_adjacency and first_product:
                        add_product()
                    with dve.Fori(0, left) as turn:
                        at_turn = turn
                        if by_adjacency:
                            dve.reg_alu(turn_register, turn, skip, ALU.add)
                            at_turn = dve.snap(turn_register, min_val=0, max_val=TURNS - 1)
                        dve.load(columns, base_i[0:1, bass.ds(at_turn * SLOTS, SLOTS)])
                        if build:
                            dve.load(a_columns[0:per_turn], a_base_i[0:1, bass.ds(turn * per_turn + a_first, per_turn)])
                        for pair in range(0, SLOTS, 2):
                            if filters:
                                weigh(turn, pair)
                                weigh(turn, pair + 1)
                                cap(pair, turn * SLOTS + (pair + 1 + SLOTS))
                                cap(pair + 1, turn * SLOTS + (pair + 2 + SLOTS))
                                add_sums(turn, at_turn, pair)
                                next_one_hots(turn, at_turn, pair + 2)
                                add_sums(turn, at_turn, pair + 1)
                                next_one_hots(turn, at_turn, pair + 3)
                                softplus(pair, turn * SLOTS + (pair + 1 + SLOTS))
                                softplus(pair + 1, turn * SLOTS + (pair + 2 + SLOTS))
                            else:
                                for s in (pair, pair + 1):
                                    next_one_hots(turn, at_turn, s + 1)
                                    if 2 <= s <= per_turn + 1:
                                        add_pairs(turn, s - 2)
                                    add_sums(turn, at_turn, s)
                                    if s < per_turn:
                                        pair_one_hots(turn, s)
                        if per_turn == SLOTS - 1:
                            add_pairs(turn, per_turn - 1)
                    if by_adjacency and not first_product:
                        dve.wait_ge(summed.sem, left * SLOTS + done + 1)
                        add_product()
            product_made.passed(1 if by_adjacency else 0)
            if build and not by_adjacency:
                hots_linked[kind].passed(2 * per_turn * TURNS)
                a_pairs.passed(per_turn * TURNS)
                a_made.passed(per_turn * TURNS)
                a_added.passed(per_turn * TURNS * a_adds)
            made_t.passed(len(QUADS) if start or residual else 0)
            taken_s.passed(len(QUADS) if start else 0)
            taken_v.passed(len(QUADS) if residual else 0)

        prepare()
        fold_biases()
        node_phase(h_table=True)
        edge_round(table, src_idx, counts=True, add_rows=L0_B2, by_adjacency=True, build=(0, A_PER_TURN, 0))
        sage_hidden()
        edge_round(table, src_idx, residual=True, by_adjacency=True, first_product=True)
        node_phase(front="mean", residual=ident, weight=sq_w[:, LIN1, :], clear=True)
        edge_round(table, src_idx, weights=e_cut, filters=True, add_rows=LIN_B)
        node_phase(front="softplus", residual=sq_w[:, LIN, :], layer=0, clear_adjacency=True)
        edge_round(rel_table, rel_idx, start=(sq_w[:, SL1, :], vecs[:, R_B1:R_B1 + 1], 1.0), build=(1, 1, 0))
        node_phase(front="relu", norm=False, layer=1)
        edge_round(rel_table, rel_idx, start=(sq_w[:, SL2, :], vecs[:, R_B2:R_B2 + 1], 1.0), build=(1, 1, TURNS))
        node_phase(front="relu", residual=ident, weight=sq_w[:, KER, :])
        edge_round(table, src_idx, weights=e_weight, start=(sq_w[:, KER, :], vecs[:, BIAS:BIAS + 1], vecs[:, SKIP:SKIP + 1]), by_adjacency=True,
                   first_product=True)
        node_phase(front="selu", residual=ident, norm=False, to_out=True)


_DIRECT = ['L0_gnn_W1l', 'L0_gnn_b1', 'L0_gnn_W1r', 'L0_gnn_gamma', 'L0_gnn_beta', 'L0_gnn_W2l', 'L0_gnn_b2', 'L0_gnn_W2r',
           'L1_gnn_mlp_w1', 'L1_gnn_mlp_b1', 'L1_gnn_mlp_w2', 'L1_gnn_mlp_b2', 'L1_gnn_lin1_w', 'L1_gnn_lin2_w', 'L1_gnn_lin2_b',
           'L1_gnn_lin_w', 'L1_gnn_lin_b', 'L2_gnn_w1', 'L2_gnn_sl1', 'L2_gnn_b1', 'L2_gnn_w2', 'L2_gnn_sl2', 'L2_gnn_b2',
           'L3_gnn_kernel', 'L3_gnn_bias', 'L3_gnn_skip_weight']


def kernel(**inputs):
    import numpy as _np
    import concourse.bacc as _bacc
    from concourse import mybir as _mybir
    from concourse.bass_utils import run_bass_kernel_spmd as _run

    def padded(name, n, fill):
        v = _np.asarray(inputs[name])
        return _np.concatenate([v, _np.full((n - v.shape[0],) + v.shape[1:], fill, v.dtype)])

    def edge_columns(name, groups, fill):
        return _np.ascontiguousarray(padded(name, groups * G_EDGES, fill).reshape(-1, P).T)

    arrays = {
        "x": padded("x", NODES, 0),
        "dst": padded("dst", EDGES, -1),
        "dst_cols": edge_columns("dst", N_GROUPS, -1),
        "src_cols": edge_columns("src", AHEAD, 0),
        "type_cols": edge_columns("edge_type_8", AHEAD, 0),
        "weight_cols": edge_columns("edge_weight", HOT_AHEAD, 0),
        "attr_cols": _np.ascontiguousarray(padded("edge_attr_50", ATTR_TURNS * SLOTS * G_EDGES, 0).T),
    }
    for name in _DIRECT:
        arrays[name] = _np.ascontiguousarray(inputs[name])
    nc = _bacc.Bacc("TRN2", target_bir_lowering=False, num_devices=1)
    aps = {name: nc.dram_tensor(f"in_{name}", v.shape, _mybir.dt.from_np(v.dtype), kind="ExternalInput").ap()
           for name, v in arrays.items()}
    out = nc.dram_tensor("out_x", (N_NODES, D), _mybir.dt.float32, kind="ExternalOutput").ap()
    build_gnn(nc, aps, out)
    r = _run(nc, [{f"in_{name}": v for name, v in arrays.items()}], core_ids=[0])
    return r.results[0]["out_x"]
```

```python
import concourse.bass as bass
from concourse import mybir
from contextlib import ExitStack
import numpy as np

fp32 = mybir.dt.float32
bf16 = mybir.dt.bfloat16
i32 = mybir.dt.int32
ALU = mybir.AluOpType
ACT = mybir.ActivationFunctionType
AX = mybir.AxisListType

N_NODES = 3125
N_EDGES = 100000
D = 128
H2 = 2
N_GAUSS = 50
N_REL = 8
P = 128
N_TILES = -(-N_NODES // P)
NODES = N_TILES * P
CHUNK = P
GROUP = 4
G_EDGES = CHUNK * GROUP
SLOTS = 4
N_GROUPS = -(-N_EDGES // G_EDGES)
TURNS = N_GROUPS // SLOTS
EDGES = N_GROUPS * G_EDGES
AHEAD = N_GROUPS + SLOTS
HOT_AHEAD = N_GROUPS + 2
ATTR_TURNS = TURNS + 2
WIN = 64
A_GROUPS = 76
A_TURNS = A_GROUPS // SLOTS
A_WIN = 20
A_COLS = 512
A_PER_TURN = 3
A_TAIL = 4
A_MADE = (TURNS - A_TAIL) * A_PER_TURN
B_GROUPS = 28
B_TURNS = B_GROUPS // SLOTS
B_FIRST = 432
B_HEAD = 5
B_MADE = TURNS - B_HEAD
AGG = NODES + WIN
BANK = 512
COLS = [(c, min(BANK, NODES - c)) for c in range(0, NODES, BANK)]
QUADS = [(t, min(4, N_TILES - t)) for t in range(0, N_TILES, 4)]
MIN_ROWS = N_GROUPS // 2
LN_EPS = 1e-5
LN2 = float(np.log(2.0))
EXP_CAP = 30.0
SELU_SCALE = 1.0507009873554805
SELU_ALPHA = 1.6732632423543772
assert N_GROUPS % SLOTS == 0 and N_GROUPS % 2 == 0 and A_GROUPS % SLOTS == 0
assert (TURNS - A_TURNS - A_TAIL) * A_PER_TURN >= A_GROUPS and A_MADE >= 2 * TURNS >= A_GROUPS
assert B_MADE >= B_GROUPS and B_GROUPS % SLOTS == 0 and A_GROUPS + B_MADE <= N_GROUPS
assert N_TILES * A_WIN <= BANK and A_COLS <= BANK and A_WIN <= WIN


class Tally:

    def __init__(self, sem):
        self.sem, self.value = sem, 0

    def at(self, n):
        return self.value + n

    def passed(self, n):
        self.value += n


def build_gnn(nc, a, out):
    with ExitStack() as ctx:
        def sb(name, shape, dt=fp32):
            return ctx.enter_context(nc.sbuf_tensor(name, shape, dt))

        def tally(name):
            return Tally(ctx.enter_context(nc.semaphore(name)))

        def scratch(name, shape, dt=fp32):
            return nc.dram_tensor(name, shape, dt, kind="Internal").ap()

        table = scratch("table", (NODES, D))
        rel_table = scratch("rel_table", (NODES * N_REL, D))
        adj_dram = scratch("adj_dram", (P, N_TILES * A_COLS))
        min_dram = scratch("min_dram", (2, N_GROUPS))

        x_rows = sb("x_rows", [P, N_TILES, D])
        h_rows = sb("h_rows", [P, N_TILES, D])
        h_cols = sb("h_cols", [P, H2, NODES])
        m_cols = sb("m_cols", [P, NODES])
        agg = sb("agg", [P, 2, AGG])
        src_idx = sb("src_idx", [P, AHEAD * GROUP], i32)
        rel_idx = sb("rel_idx", [P, AHEAD * GROUP], i32)
        dst_rel = sb("dst_rel", [P, HOT_AHEAD * GROUP])
        e_weight = sb("e_weight", [P, HOT_AHEAD * GROUP])
        e_cut = sb("e_cut", [P, HOT_AHEAD * GROUP])
        base_row = sb("base_row", [P, N_GROUPS])
        base_i = sb("base_i", [1, N_GROUPS], i32)
        more_i = sb("more_i", [1, 1], i32)
        turns_i = sb("turns_i", [1, 4], i32)
        iota_f = sb("iota_f", [P, P])
        further_rel = sb("further_rel", [P, GROUP])
        adj_mem = sb("adj_mem", [P, N_TILES * A_COLS])
        adj = adj_mem[:, :].rearrange("p (t d) -> p t d", d=A_COLS)
        a_src_tile = sb("a_src_tile", [P, (A_MADE + B_MADE) * GROUP], bf16)
        a_src_part = sb("a_src_part", [P, (A_MADE + B_MADE) * GROUP], bf16)
        a_dst_rel = sb("a_dst_rel", [P, (A_MADE + B_MADE) * GROUP], bf16)
        a_weight = sb("a_weight", [P, 3, (A_GROUPS + B_MADE) * GROUP])
        a_weight_b = sb("a_weight_b", [P, (A_GROUPS + B_MADE) * GROUP], bf16)
        a_base_i = sb("a_base_i", [1, A_MADE + B_MADE], i32)
        iota_b = sb("iota_b", [P, P], bf16)
        ones_b = sb("ones_b", [P, P], bf16)
        tile_hot = sb("tile_hot", [P, 2, GROUP, N_TILES], bf16)
        dst_hot = sb("dst_hot", [P, 2, GROUP, A_WIN], bf16)
        pair_size = GROUP * N_TILES * A_WIN // 2
        pair_hot = [m_cols[:, b * pair_size:(b + 1) * pair_size].bitcast(bf16).rearrange("p (j t w) -> p j t w", t=N_TILES, w=A_WIN)
                    for b in range(2)]
        part_hot = [m_cols[:, 2 * pair_size + b * GROUP * D // 2:2 * pair_size + (b + 1) * GROUP * D // 2].bitcast(bf16)
                    .rearrange("p (j q) -> p j q", q=P) for b in range(2)]
        weight_hot = [h_cols[:, 1, b * 3 * GROUP * P // 2:(b + 1) * 3 * GROUP * P // 2].bitcast(bf16)
                      .rearrange("p (k j q) -> p k j q", k=3, q=P) for b in range(2)]
        cur_idx = sb("cur_idx", [P, SLOTS, GROUP], i32)
        rows = sb("rows", [P, SLOTS, GROUP, D])
        onehot = sb("onehot", [P, 2, GROUP, WIN])
        onehot_b = sb("onehot_b", [P, 2, GROUP, WIN], bf16)
        hot_more = sb("hot_more", [P, GROUP, WIN])
        attr = adj_mem[0:N_GAUSS, 0:SLOTS * G_EDGES].rearrange("p (s e) -> p s e", s=SLOTS)
        soft = adj_mem[:, SLOTS * G_EDGES:(SLOTS + 2) * G_EDGES].rearrange("p (s e) -> p s e", s=2)
        filt = adj_mem[:, (SLOTS + 2) * G_EDGES:(2 * SLOTS + 2) * G_EDGES].rearrange("p (s e) -> p s e", s=SLOTS)
        ident = sb("ident", [P, P])
        ones = sb("ones", [P, P])
        eps_t = sb("eps_t", [P, 1])
        w1lr = sb("w1lr", [P, 2, H2 * D])
        w2lr = sb("w2lr", [P, H2, 2 * D])
        bn_vec = sb("bn_vec", [P, 3, H2])
        mlp_w1 = sb("mlp_w1", [N_GAUSS, D])
        sq_w = sb("sq_w", [P, 7, D])
        MLP2, LIN1, LIN2, LIN, SL1, SL2, KER = range(7)
        rel_w = sb("rel_w", [P, 2, N_REL * D])
        vecs = sb("vecs", [P, 6])
        MLP_B1, LIN2_B, R_B1, R_B2, BIAS, SKIP = range(6)
        row_vecs = sb("row_vecs", [P, 3, D])
        L0_B2, LIN_B, MLP_B2 = range(3)
        b2_parts = sb("b2_parts", [P, 3, D])
        b2_left = sb("b2_left", [P, 2, D])
        b2_split = sb("b2_split", [P, GROUP, D], bf16)
        three_ones = sb("three_ones", [P, P], bf16)
        stats = sb("stats", [P, N_TILES, 6])
        mean_var = sb("mean_var", [P, N_TILES, 2])
        ln_std = sb("ln_std", [P, N_TILES])
        inv_count = sb("inv_count", [P, N_TILES])
        ln_scale = sb("ln_scale", [P, N_TILES])
        ln_shift = sb("ln_shift", [P, N_TILES])
        dst_raw = agg[:, 0, 0:N_GROUPS * GROUP].bitcast(i32)
        dst_f = agg[:, 1, 0:N_GROUPS * GROUP]
        dst_groups_i = m_cols[0:MIN_ROWS, 0:2 * G_EDGES].rearrange("p (j e) -> p j e", j=2).bitcast(i32)
        dst_groups = m_cols[0:MIN_ROWS, 2 * G_EDGES:4 * G_EDGES].rearrange("p (j e) -> p j e", j=2)
        dst_lift = h_cols[0:MIN_ROWS, 0, 0:2 * G_EDGES].rearrange("p (j e) -> p j e", j=2)
        span = sb("span", [MIN_ROWS, 2, 2])
        span_row = h_cols[:, 0, 2048:2048 + N_GROUPS]
        max_row = h_cols[:, 0, 2304:2304 + N_GROUPS]
        span_max = sb("span_max", [P, 6])
        fits = sb("fits", [P, 6])
        turns_f = sb("turns_f", [1, 4])
        zero_t = sb("zero_t", [P, 1])
        a_temp = h_cols[:, 1, 2048:2048 + A_MADE * GROUP]
        type_i = m_cols[:, 0:AHEAD * GROUP].bitcast(i32)
        cyc = h_cols[:, 1, 0:HOT_AHEAD * GROUP]
        cyc_round = h_cols[:, 1, 1024:1024 + HOT_AHEAD * GROUP]
        iota_i = h_rows[:, 0, :].bitcast(i32)

        ps = [ctx.enter_context(nc.psum_tensor(f"ps{i}", [P, BANK], fp32)) for i in range(8)]

        loaded = tally("loaded")
        dst_in = tally("dst_in")
        edges_in = tally("edges_in")
        chain_v = tally("chain_v")
        chain_s = tally("chain_s")
        chain_g = tally("chain_g")
        made_t = tally("made_t")
        taken_v = tally("taken_v")
        taken_s = tally("taken_s")
        rows_done = tally("rows_done")
        stored = tally("stored")
        stage_out = [tally(f"stage_out{i}") for i in range(3)]
        prepared = tally("prepared")
        wanted = tally("wanted")
        input_v = tally("input_v")
        m_ready = tally("m_ready")
        z_made = tally("z_made")
        capped_z = tally("capped_z")
        logs_made = tally("logs_made")
        add_made = tally("add_made")
        x_ready = tally("x_ready")
        scale_ready = tally("scale_ready")
        shift_ready = tally("shift_ready")
        turned = tally("turned")
        cols_ready = tally("cols_ready")
        idx_ready = tally("idx_ready")
        turn_begun = tally("turn_begun")
        gathered = [tally(f"gathered{i}") for i in range(SLOTS)]
        onehot_ready = tally("onehot_ready")
        onehot_b_ready = tally("onehot_b_ready")
        scattered = tally("scattered")
        more_hot = tally("more_hot")
        more_rel = tally("more_rel")
        more_sums = tally("more_sums")
        more_summed = tally("more_summed")
        summed = tally("summed")
        pairs_ready = [tally(f"pairs_ready{i}") for i in range(2)]
        hots_linked = [tally(f"hots_linked{i}") for i in range(2)]
        weights_hot = tally("weights_hot")
        adj_made = [tally(f"adj_made{i}") for i in range(2)]
        adj_added = [tally(f"adj_added{i}") for i in range(2)]
        product_made = tally("product_made")
        product_added = tally("product_added")
        adj_saved = tally("adj_saved")
        adj_cleared = tally("adj_cleared")
        adj_back = tally("adj_back")
        attr_in = [tally(f"attr_in{i}") for i in range(SLOTS)]
        exp_ready = tally("exp_ready")
        z_ready = tally("z_ready")
        z_capped = tally("z_capped")
        ln_ready = tally("ln_ready")
        filt_ready = tally("filt_ready")
        w_ready = tally("w_ready")
        weighed = tally("weighed")

        def link(ins, t, eng):
            ins.then_inc(t.sem, 1)
            t.passed(1)
            eng.wait_ge(t.sem, t.value)

        def prepare():
            with nc.Block() as block:
                @block.sync
                def _(sp):
                    sp.dma_start(dst_groups_i, a["dst"].rearrange("(p j e) -> p j e", j=2, e=G_EDGES)).then_inc(dst_in.sem, 16)
                    sp.dma_start(dst_raw, a["dst_cols"]).then_inc(edges_in.sem, 16)
                    sp.dma_start(x_rows[:, :, :], a["x"].rearrange("(t p) f -> p t f", p=P)).then_inc(loaded.sem, 16)
                    sp.dma_start(src_idx[:, :], a["src_cols"]).then_inc(edges_in.sem, 16)
                    sp.dma_start(e_weight[:, :], a["weight_cols"]).then_inc(edges_in.sem, 16)
                    n = 1
                    for dst, src in (
                        (w1lr[:, 0, :], a["L0_gnn_W1l"]), (w1lr[:, 1, :], a["L0_gnn_W1r"]),
                        (w2lr[:, :, 0:D], a["L0_gnn_W2l"].rearrange("(c p) m -> p c m", p=P)),
                        (w2lr[:, :, D:2 * D], a["L0_gnn_W2r"].rearrange("(c p) m -> p c m", p=P)),
                        (mlp_w1[:, :], a["L1_gnn_mlp_w1"]), (sq_w[:, MLP2, :], a["L1_gnn_mlp_w2"]),
                        (sq_w[:, LIN1, :], a["L1_gnn_lin1_w"]), (sq_w[:, LIN2, :], a["L1_gnn_lin2_w"]),
                        (sq_w[:, LIN, :], a["L1_gnn_lin_w"]), (sq_w[:, SL1, :], a["L2_gnn_sl1"]),
                        (sq_w[:, SL2, :], a["L2_gnn_sl2"]), (sq_w[:, KER, :], a["L3_gnn_kernel"]),
                        (rel_w[:, 0, :].rearrange("p (r m) -> p r m", r=N_REL), a["L2_gnn_w1"].rearrange("r p m -> p r m")),
                        (rel_w[:, 1, :].rearrange("p (r m) -> p r m", r=N_REL), a["L2_gnn_w2"].rearrange("r p m -> p r m")),
                        (vecs[:, MLP_B1:MLP_B1 + 1], a["L1_gnn_mlp_b1"][:, None]),
                        (vecs[:, LIN2_B:LIN2_B + 1], a["L1_gnn_lin2_b"][:, None]),
                        (vecs[:, R_B1:R_B1 + 1], a["L2_gnn_b1"][:, None]), (vecs[:, R_B2:R_B2 + 1], a["L2_gnn_b2"][:, None]),
                        (vecs[:, BIAS:BIAS + 1], a["L3_gnn_bias"][:, None]), (vecs[:, SKIP:SKIP + 1], a["L3_gnn_skip_weight"][:, None]),
                        (row_vecs[:, L0_B2, :], a["L0_gnn_b2"][None, :].broadcast_to([P, D])),
                        (row_vecs[:, LIN_B, :], a["L1_gnn_lin_b"][None, :].broadcast_to([P, D])),
                        (row_vecs[:, MLP_B2, :], a["L1_gnn_mlp_b2"][None, :].broadcast_to([P, D])),
                    ):
                        sp.dma_start(dst, src).then_inc(loaded.sem, 16)
                        n += 1
                    for i, name in enumerate(("L0_gnn_b1", "L0_gnn_gamma", "L0_gnn_beta")):
                        for c in range(H2):
                            sp.dma_start(bn_vec[:, i, c:c + 1], a[name][c * P:(c + 1) * P, None]).then_inc(loaded.sem, 16)
                            n += 1
                    sp.wait_ge(prepared.sem, 1)
                    sp.dma_start(min_dram[0, :].rearrange("(p j) -> p j", j=2), span[:, 0, :]).then_inc(stored.sem, 16)
                    sp.dma_start(min_dram[1, :].rearrange("(p j) -> p j", j=2), span[:, 1, :]).then_inc(stored.sem, 16)
                    sp.wait_ge(stored.sem, 32)
                    sp.dma_start(base_row[:, :], min_dram[0:1, :].broadcast_to([P, N_GROUPS])).then_inc(stage_out[0].sem, 16)
                    sp.dma_start(max_row, min_dram[1:2, :].broadcast_to([P, N_GROUPS])).then_inc(stage_out[0].sem, 16)
                    sp.wait_ge(loaded.sem, 16 * n)
                    loaded.passed(16 * n)

                @block.gpsimd
                def _(pool):
                    link(nc.gpsimd.memset(ident[:, :], 0.0), chain_g, pool)
                    link(nc.gpsimd.affine_select(out=ident[:, :], in_=ident[:, :], compare_op=ALU.not_equal, fill=1.0,
                                                 base=0, pattern=[[-1, P]], channel_multiplier=1), chain_g, pool)
                    link(nc.gpsimd.memset(ones[:, :], 1.0), chain_g, pool)
                    link(nc.gpsimd.memset(eps_t[:, :], LN_EPS), chain_g, pool)
                    link(nc.gpsimd.memset(b2_split[:, :, :], 0.0), chain_g, pool)
                    link(nc.gpsimd.memset(three_ones[:, :], 1.0), chain_g, pool)
                    link(nc.gpsimd.affine_select(out=three_ones[:, :], in_=three_ones[:, :], compare_op=ALU.is_gt, fill=0.0,
                                                 base=3, pattern=[[0, P]], channel_multiplier=-1), chain_g, pool)
                    nc.gpsimd.memset(ones_b[:, :], 1.0)
                    nc.gpsimd.iota(iota_i, pattern=[[1, P]], base=0, channel_multiplier=0).then_inc(wanted.sem, 1)
                    nc.gpsimd.memset(adj_mem[:, :], 0.0)

                @block.vector
                def _(dve):
                    dve.wait_ge(dst_in.sem, 16)
                    link(nc.vector.tensor_copy(dst_groups, dst_groups_i), chain_v, dve)
                    link(nc.vector.tensor_scalar(dst_lift, dst_groups, 0.0, float(NODES), ALU.is_lt, ALU.mult), chain_v, dve)
                    link(nc.vector.tensor_tensor(dst_lift, dst_lift, dst_groups, ALU.add), chain_v, dve)
                    link(nc.vector.tensor_reduce(span[:, 0, :], dst_lift, AX.X, ALU.min), chain_v, dve)
                    nc.vector.tensor_reduce(span[:, 1, :], dst_groups, AX.X, ALU.max).then_inc(prepared.sem, 1)
                    dve.wait_ge(edges_in.sem, 48)
                    link(nc.vector.tensor_copy(dst_f, dst_raw), chain_v, dve)
                    dve.wait_ge(wanted.sem, 1)
                    link(nc.vector.tensor_copy(iota_f[:, :], iota_i), chain_v, dve)
                    link(nc.vector.tensor_copy(iota_b[:, :], iota_i), chain_v, dve)
                    for first, to, n in ((0, 0, A_MADE), (A_GROUPS, A_MADE, B_MADE)):
                        edges = slice(first * GROUP, (first + n) * GROUP)
                        into = slice(to * GROUP, (to + n) * GROUP)
                        temp = a_temp[:, 0:n * GROUP]
                        temp_i = temp.bitcast(i32)
                        link(nc.vector.tensor_scalar(temp_i, src_idx[:, edges], P - 1, None, ALU.bitwise_and), chain_v, dve)
                        link(nc.vector.tensor_copy(a_src_part[:, into], temp_i), chain_v, dve)
                        link(nc.vector.tensor_scalar(temp_i, src_idx[:, edges], P.bit_length() - 1, None, ALU.arith_shift_right), chain_v, dve)
                        link(nc.vector.tensor_copy(a_src_tile[:, into], temp_i), chain_v, dve)
                    nc.vector.memset(zero_t[:, :], 0.0)
                    nc.vector.memset(a_dst_rel[:, (A_MADE + B_GROUPS) * GROUP:], -1.0)
                    nc.vector.memset(a_dst_rel[:, A_GROUPS * GROUP:A_MADE * GROUP], -1.0).then_inc(adj_added[0].sem, 1)
                    nc.vector.memset(fits[:, :], 0.0).then_inc(adj_added[1].sem, 1)
                    nc.vector.memset(dst_rel[:, N_GROUPS * GROUP:], -1.0).then_inc(summed.sem, 1)
                    dve.wait_ge(stage_out[0].sem, 32)
                    link(nc.vector.tensor_tensor(dst_rel[:, 0:N_GROUPS * GROUP].rearrange("p (g j) -> p g j", j=GROUP),
                                                 dst_f.rearrange("p (g j) -> p g j", j=GROUP),
                                                 base_row[:, :].rearrange("p (g o) -> p g o", o=1).broadcast_to([P, N_GROUPS, GROUP]),
                                                 ALU.subtract), chain_v, dve)
                    link(nc.vector.tensor_copy(base_i[:, :], base_row[0:1, :]), chain_v, dve)
                    link(nc.vector.tensor_tensor(span_row, max_row, base_row[:, :], ALU.subtract), chain_v, dve)
                    nc.vector.tensor_reduce(span_max[:, 0:1], span_row, AX.X, ALU.max)
                    ab = A_GROUPS + B_GROUPS
                    nc.vector.tensor_reduce(span_max[:, 1:2], span_row[:, 0:A_GROUPS], AX.X, ALU.max)
                    nc.vector.tensor_reduce(span_max[:, 2:3], base_row[:, 0:A_GROUPS], AX.X, ALU.max)
                    nc.vector.tensor_reduce(span_max[:, 3:4], span_row[:, A_GROUPS:ab], AX.X, ALU.max)
                    nc.vector.tensor_reduce(span_max[:, 4:5], base_row[:, A_GROUPS:ab], AX.X, ALU.max)
                    link(nc.vector.tensor_reduce(span_max[:, 5:6], base_row[:, A_GROUPS:ab], AX.X, ALU.min), chain_v, dve)
                    link(nc.vector.tensor_copy(more_i[:, :], span_max[0:1, 0:1]), chain_v, dve)
                    link(nc.vector.tensor_scalar(more_i[:, :], more_i[:, :], WIN.bit_length() - 1, None,
                                                 ALU.arith_shift_right), chain_v, dve)
                    last_a, last_b = float(A_COLS - A_WIN), float(B_FIRST + A_COLS - A_WIN)
                    for k, (bound, is_so) in enumerate(((float(WIN), ALU.is_lt), (float(A_WIN), ALU.is_lt), (last_a, ALU.is_le),
                                                        (float(A_WIN), ALU.is_lt), (last_b, ALU.is_le), (float(B_FIRST), ALU.is_ge))):
                        last = nc.vector.tensor_scalar(fits[:, k:k + 1], span_max[:, k:k + 1], bound, None, is_so)
                    link(last, chain_v, dve)
                    for k in range(1, 6):
                        link(nc.vector.tensor_tensor(fits[:, k:k + 1], fits[:, k:k + 1], fits[:, k - 1:k], ALU.mult), chain_v, dve)
                    for first, to, n, fit in ((0, 0, A_GROUPS, 2), (A_GROUPS, A_MADE, B_GROUPS, 5)):
                        temp = a_temp[:, 0:n * GROUP]
                        link(nc.vector.tensor_scalar(temp, dst_rel[:, first * GROUP:(first + n) * GROUP], 1.0, fits[:, fit:fit + 1],
                                                     ALU.add, ALU.mult), chain_v, dve)
                        link(nc.vector.tensor_scalar(a_dst_rel[:, to * GROUP:(to + n) * GROUP], temp, -1.0, None, ALU.add), chain_v, dve)
                    link(nc.vector.tensor_scalar(span_row[:, 0:A_MADE], base_row[:, 0:A_MADE], last_a, None, ALU.min), chain_v, dve)
                    link(nc.vector.tensor_copy(a_base_i[:, 0:A_MADE], span_row[0:1, 0:A_MADE]), chain_v, dve)
                    link(nc.vector.tensor_scalar(span_row[:, 0:B_MADE], base_row[:, A_GROUPS:A_GROUPS + B_MADE], last_b, float(B_FIRST),
                                                 ALU.min, ALU.max), chain_v, dve)
                    link(nc.vector.tensor_scalar(span_row[:, 0:B_MADE], span_row[:, 0:B_MADE], float(B_FIRST), None, ALU.subtract), chain_v, dve)
                    link(nc.vector.tensor_copy(a_base_i[:, A_MADE:], span_row[0:1, 0:B_MADE]), chain_v, dve)
                    a_fit, b_fit = fits[0:1, 2:3], fits[0:1, 5:6]
                    link(nc.vector.tensor_scalar(turns_f[:, 0:1], a_fit, float(A_TURNS), None, ALU.mult), chain_v, dve)
                    link(nc.vector.scalar_tensor_tensor(turns_f[:, 2:3], b_fit, float(B_TURNS), turns_f[:, 0:1], ALU.mult, ALU.add), chain_v, dve)
                    for k, less in ((0, A_TAIL), (2, 0)):
                        link(nc.vector.tensor_scalar(turns_f[:, k + 1:k + 2], turns_f[:, k:k + 1], -1.0, float(TURNS - less),
                                                     ALU.mult, ALU.add), chain_v, dve)
                    link(nc.vector.tensor_copy(turns_i[:, :], turns_f[:, :]), chain_v, dve)

            for i in range(2):
                adj_added[i].passed(1)
            for t, n in ((dst_in, 16), (edges_in, 48), (prepared, 1), (wanted, 1), (stored, 32), (stage_out[0], 32)):
                t.passed(n)

        def node_phase(front=None, residual=None, norm=True, weight=None, layer=None, h_table=False, to_out=False,
                       clear=False, clear_first=False, clear_adjacency=False):
            n_quads = len(QUADS)
            lag = 2 if not norm else 5 if layer is not None else 3
            steps = n_quads + lag + 1
            stage = h_rows[:, :, :].rearrange("p t f -> p (t f)")
            rel_stage = m_cols[:, :]
            if layer is not None and residual is not None:
                rel_stage = h_cols[:, 1, :]
            half = N_REL * D // 2
            ADD, TURNED, PROD = (ps[1], ps[2]), ps[3], ps[4:8]
            full_tiles = N_NODES // P

            def quad(q):
                t, n = QUADS[q]
                return t, n, slice(t * P, (t + n) * P)

            def in_range(q):
                return 0 <= q < n_quads

            with nc.Block() as block:
                @block.tensor
                def _(pe):
                    def tail(q):
                        t, n, _ = quad(q)
                        pe.wait_ge(cols_ready.sem, cols_ready.at(q + 1))
                        if weight is not None:
                            if q >= 4:
                                pe.wait_ge(taken_s.sem, taken_s.at(q - 3))
                            for i in range(n):
                                last = nc.tensor.matmul(PROD[q % 4][:, i * P:(i + 1) * P], h_cols[:, 0, (t + i) * P:(t + i + 1) * P],
                                                        weight, start=True, stop=True)
                            last.then_inc(made_t.sem, 1)
                        if layer is not None:
                            for u in range(t, t + n):
                                if u >= 2:
                                    pe.wait_ge(taken_v.sem, taken_v.at(u - 1))
                                    pe.wait_ge(taken_s.sem, taken_s.at(u - 1))
                                for part in range(2):
                                    last = nc.tensor.matmul(PROD[2 * (u % 2) + part][:, :], h_cols[:, 0, u * P:(u + 1) * P],
                                                            rel_w[:, layer, part * half:(part + 1) * half], start=True, stop=True)
                                last.then_inc(made_t.sem, 1)

                    if front == "softplus":
                        for q in range(n_quads):
                            t, n, cols = quad(q)
                            if q >= 4:
                                pe.wait_ge(m_ready.sem, m_ready.at(q - 3))
                            nc.tensor.matmul(PROD[q % 4][:, 0:n * P], sq_w[:, LIN2, :], agg[:, 0, cols], start=True, stop=True
                                             ).then_inc(z_made.sem, 1)
                    for step in range(steps):
                        q = step
                        if residual is not None and in_range(q):
                            t, n, cols = quad(q)
                            if front != "mean":
                                pe.wait_ge(m_ready.sem, m_ready.at(q + 1))
                            if q >= 2:
                                pe.wait_ge(x_ready.sem, x_ready.at(q - 1))
                            for i in range(n):
                                m = (agg[:, 0, :] if front == "mean" else m_cols)[:, (t + i) * P:(t + i + 1) * P]
                                into = ADD[q % 2][:, i * P:(i + 1) * P]
                                if residual is ident:
                                    last = nc.tensor.transpose(into, m, ident[:, :])
                                else:
                                    last = nc.tensor.matmul(into, m, residual, start=True, stop=True)
                            last.then_inc(add_made.sem, 1)
                        if in_range(q - lag) and (weight is not None or layer is not None):
                            if front == "softplus" and q == lag:
                                pe.wait_ge(m_ready.sem, m_ready.at(n_quads))
                            tail(q - lag)
                        if norm and in_range(q - 2):
                            t, n, cols = quad(q - 2)
                            pe.wait_ge(rows_done.sem, rows_done.at(q - 1))
                            if q >= 3:
                                pe.wait_ge(cols_ready.sem, cols_ready.at(q - 2))
                            for i in range(n):
                                last = nc.tensor.transpose(TURNED[:, i * P:(i + 1) * P], h_rows[:, t + i, :], ident[:, :])
                            last.then_inc(turned.sem, 1)

                @block.scalar
                def _(act):
                    nc.scalar.preload_act_table_set("natural_log_exp_and_others")

                    def tail(q):
                        t, n, cols = quad(q)
                        if weight is not None:
                            act.wait_ge(made_t.sem, made_t.at(q + 1))
                            nc.scalar.copy(stage[:, cols], PROD[q % 4][:, 0:n * P]).then_inc(taken_s.sem, 1)
                        if layer is not None:
                            for u in range(t, t + n):
                                if u >= 3:
                                    act.wait_ge(stage_out[u % 3].sem, stage_out[u % 3].at(16 * (u // 3)))
                                act.wait_ge(made_t.sem, made_t.at(u + 1))
                                o = (u % 3) * N_REL * D + half
                                nc.scalar.copy(rel_stage[:, o:o + half], PROD[2 * (u % 2) + 1][:, :]).then_inc(taken_s.sem, 1)

                    def exponential(q):
                        t, n, cols = quad(q)
                        act.wait_ge(capped_z.sem, capped_z.at(q + 1))
                        nc.scalar.activation(m_cols[:, cols], m_cols[:, cols], ACT.Exp).then_inc(prepared.sem, 1)

                    if front == "softplus":
                        for q in range(n_quads):
                            t, n, cols = quad(q)
                            exponential(q)
                            act.wait_ge(prepared.sem, prepared.at(q + 1))
                            nc.scalar.activation(m_cols[:, cols], m_cols[:, cols], ACT.Ln, bias=ones[:, 0:1]).then_inc(logs_made.sem, 1)
                    for step in range(steps):
                        q = step - 1
                        if front == "selu" and in_range(step):
                            exponential(step)
                        if norm and in_range(q):
                            t, n, cols = quad(q)
                            act.wait_ge(x_ready.sem, x_ready.at(q + 1))
                            nc.scalar.activation(ln_std[:, t:t + n], mean_var[:, t:t + n, 1], ACT.Ln, bias=eps_t[:, :]
                                                 ).then_inc(chain_s.sem, 1)
                            act.wait_ge(chain_s.sem, chain_s.at(q + 1))
                            nc.scalar.activation(ln_scale[:, t:t + n], ln_std[:, t:t + n], ACT.Exp, scale=-0.5).then_inc(scale_ready.sem, 1)
                        if norm and in_range(q - 1):
                            t, n, cols = quad(q - 1)
                            act.wait_ge(shift_ready.sem, shift_ready.at(q))
                            for u in range(t, t + n):
                                last = nc.scalar.activation(h_rows[:, u, :], x_rows[:, u, :], ACT.Relu, bias=ln_shift[:, u:u + 1],
                                                            scale=ln_scale[:, u:u + 1])
                            last.then_inc(rows_done.sem, 1)
                        if in_range(q + 1 - lag) and (weight is not None or layer is not None):
                            tail(q + 1 - lag)

                @block.vector
                def _(dve):
                    def tail(q):
                        t, n, cols = quad(q)
                        for u in range(t, t + n):
                            if u >= 3:
                                dve.wait_ge(stage_out[u % 3].sem, stage_out[u % 3].at(16 * (u // 3)))
                            dve.wait_ge(made_t.sem, made_t.at(u + 1))
                            o = (u % 3) * N_REL * D
                            nc.vector.tensor_copy(rel_stage[:, o:o + half], PROD[2 * (u % 2)][:, :]).then_inc(taken_v.sem, 1)

                    if front == "softplus":
                        for step in range(n_quads + 1):
                            if step < n_quads:
                                t, n, cols = quad(step)
                                dve.wait_ge(z_made.sem, z_made.at(step + 1))
                                nc.vector.tensor_scalar(m_cols[:, cols], PROD[step % 4][:, 0:n * P], vecs[:, LIN2_B:LIN2_B + 1], EXP_CAP,
                                                        ALU.add, ALU.min).then_inc(capped_z.sem, 1)
                            if step:
                                t, n, cols = quad(step - 1)
                                dve.wait_ge(logs_made.sem, logs_made.at(step))
                                nc.vector.scalar_tensor_tensor(m_cols[:, cols], PROD[(step - 1) % 4][:, 0:n * P], vecs[:, LIN2_B:LIN2_B + 1],
                                                               m_cols[:, cols], ALU.add, ALU.max).then_inc(m_ready.sem, 1)
                    for step in range(steps):
                        q = step - 1
                        if in_range(step):
                            t, n, cols = quad(step)
                            src, into = agg[:, 0, cols], m_cols[:, cols]
                            if front == "relu":
                                if norm:
                                    nc.vector.tensor_scalar(into, src, 0.0, None, ALU.max).then_inc(m_ready.sem, 1)
                                else:
                                    nc.vector.tensor_scalar(h_cols[:, 0, cols], src, 0.0, None, ALU.max).then_inc(cols_ready.sem, 1)
                            if front == "selu":
                                nc.vector.tensor_scalar(into, src, 0.0, None, ALU.min).then_inc(capped_z.sem, 1)
                                nc.vector.tensor_scalar(src, src, 0.0, SELU_SCALE, ALU.max, ALU.mult).then_inc(logs_made.sem, 1)
                        if in_range(q):
                            t, n, cols = quad(q)
                            if residual is not None:
                                dve.wait_ge(add_made.sem, add_made.at(q + 1))
                                xs = x_rows[:, t:t + n, :].rearrange("p t f -> p (t f)")
                                if front == "mean":
                                    for i in range(n):
                                        last = nc.vector.scalar_tensor_tensor(x_rows[:, t + i, :], ADD[q % 2][:, i * P:(i + 1) * P],
                                                                              inv_count[:, t + i:t + i + 1], x_rows[:, t + i, :],
                                                                              ALU.mult, ALU.add)
                                else:
                                    last = nc.vector.tensor_tensor(xs, xs, ADD[q % 2][:, 0:n * P], ALU.add)
                                if norm:
                                    last.then_inc(chain_v.sem, 1)
                                    dve.wait_ge(chain_v.sem, chain_v.at(2 * q + 1))
                                else:
                                    last.then_inc(x_ready.sem, 1)
                            if norm:
                                for u in range(t, t + n):
                                    last = nc.vector.bn_stats(stats[:, u, :], x_rows[:, u, :])
                                last.then_inc(chain_v.sem, 1)
                                dve.wait_ge(chain_v.sem, chain_v.at((2 if residual is not None else 1) * (q + 1)))
                                for u in range(t, t + n):
                                    last = nc.vector.bn_aggr(mean_var[:, u, :], stats[:, u, :])
                                last.then_inc(x_ready.sem, 1)
                        if norm and in_range(q - 1):
                            t, n, cols = quad(q - 1)
                            dve.wait_ge(scale_ready.sem, scale_ready.at(q))
                            nc.vector.scalar_tensor_tensor(ln_shift[:, t:t + n], mean_var[:, t:t + n, 0], -1.0, ln_scale[:, t:t + n],
                                                           ALU.mult, ALU.mult).then_inc(shift_ready.sem, 1)
                        if norm and in_range(q - 2):
                            t, n, cols = quad(q - 2)
                            dve.wait_ge(turned.sem, turned.at(q - 1))
                            nc.vector.tensor_copy(h_cols[:, 0, cols], TURNED[:, 0:n * P]).then_inc(cols_ready.sem, 1)
                        if in_range(step):
                            t, n, cols = quad(step)
                            into = m_cols[:, cols]
                            if front == "selu":
                                dve.wait_ge(prepared.sem, prepared.at(step + 1))
                                nc.vector.tensor_scalar(into, into, SELU_SCALE * SELU_ALPHA, -SELU_SCALE * SELU_ALPHA,
                                                        ALU.mult, ALU.add).then_inc(logs_made.sem, 1)
                                dve.wait_ge(logs_made.sem, logs_made.at(2 * (step + 1)))
                                nc.vector.tensor_tensor(into, into, agg[:, 0, cols], ALU.add).then_inc(m_ready.sem, 1)
                        if layer is not None and in_range(q + 1 - lag):
                            tail(q + 1 - lag)

                @block.gpsimd
                def _(pool):
                    if clear_first:
                        nc.gpsimd.memset(agg[:, :, :], 0.0)
                    if clear_adjacency:
                        nc.gpsimd.memset(adj_mem[:, :], 0.0)
                    if clear:
                        pool.wait_ge(add_made.sem, add_made.at(n_quads))
                        nc.gpsimd.memset(agg[:, 0, :], 0.0)

                @block.sync
                def _(sp):
                    rows_out = table.rearrange("(t p) f -> p t f", p=P)
                    if h_table or weight is not None:
                        for q0, q1 in ((0, 3), (3, 6), (6, 7)):
                            t0, t1 = QUADS[q0][0], QUADS[q1 - 1][0] + QUADS[q1 - 1][1]
                            if h_table:
                                sp.wait_ge(rows_done.sem, rows_done.at(q1))
                            else:
                                sp.wait_ge(taken_s.sem, taken_s.at(q1))
                            sp.dma_start(rows_out[:, t0:t1, :], h_rows[:, t0:t1, :]).then_inc(stored.sem, 16)
                        sp.wait_ge(stored.sem, stored.at(48))
                    if layer is not None:
                        for t in range(N_TILES):
                            sp.wait_ge(taken_v.sem, taken_v.at(t + 1))
                            sp.wait_ge(taken_s.sem, taken_s.at(t + 1))
                            o = (t % 3) * N_REL * D
                            sp.dma_start(rel_table[t * P * N_REL:(t + 1) * P * N_REL, :].rearrange("(p r) f -> p (r f)", r=N_REL),
                                         rel_stage[:, o:o + N_REL * D]).then_inc(stage_out[t % 3].sem, 16)
                        for i in range(3):
                            sp.wait_ge(stage_out[i].sem, stage_out[i].at(16 * len(range(i, N_TILES, 3))))
                    if to_out:
                        for q in range(n_quads):
                            t, n, _ = quad(q)
                            sp.wait_ge(x_ready.sem, x_ready.at(q + 1))
                            full = min(t + n, full_tiles) - t
                            if full:
                                sp.dma_start(out[t * P:(t + full) * P, :].rearrange("(t p) f -> p t f", p=P),
                                             x_rows[:, t:t + full, :]).then_inc(stored.sem, 16)
                            else:
                                sp.dma_start(out[t * P:N_NODES, :], x_rows[0:N_NODES - t * P, t, :]).then_inc(stored.sem, 16)
                        sp.wait_ge(stored.sem, stored.at(16 * n_quads))

            def count(t, n):
                if n:
                    t.passed(n)

            count(m_ready, n_quads if front in ("softplus", "selu") or (front == "relu" and norm) else 0)
            count(z_made, n_quads if front == "softplus" else 0)
            count(capped_z, n_quads if front in ("softplus", "selu") else 0)
            count(prepared, n_quads if front in ("softplus", "selu") else 0)
            count(logs_made, {"softplus": 1, "selu": 2}.get(front, 0) * n_quads)
            count(add_made, n_quads if residual is not None else 0)
            count(x_ready, n_quads if norm or residual is not None else 0)
            count(chain_v, ((2 if residual is not None else 1) * n_quads) if norm else 0)
            for t in (chain_s, scale_ready, shift_ready, rows_done, turned):
                count(t, n_quads if norm else 0)
            count(cols_ready, n_quads if norm or layer is not None else 0)
            count(made_t, n_quads if weight is not None else N_TILES if layer is not None else 0)
            count(taken_s, n_quads if weight is not None else N_TILES if layer is not None else 0)
            count(taken_v, N_TILES if layer is not None else 0)
            count(stored, 48 if h_table or weight is not None else 16 * n_quads if to_out else 0)
            if layer is not None:
                for i in range(3):
                    stage_out[i].passed(16 * len(range(i, N_TILES, 3)))

        def sage_hidden():
            n_quads = len(QUADS)
            before = h_rows[:, :, :].rearrange("p t f -> p (t f)"), h_cols[:, 1, :]
            pieces = [(c, min(BANK, N_NODES - c)) for c in range(0, N_NODES, BANK)]
            with nc.Block() as block:
                @block.tensor
                def _(pe):
                    for t in range(N_TILES):
                        last = nc.tensor.matmul(ps[7][:, t:t + 1], agg[:, 1, t * P:(t + 1) * P], ident[:, 0:1], start=True, stop=True)
                    last.then_inc(add_made.sem, 1)

                    def inverses(q):
                        t, n = QUADS[q]
                        pe.wait_ge(capped_z.sem, capped_z.at(q + 1))
                        if q >= 2:
                            pe.wait_ge(m_ready.sem, m_ready.at(q - 1))
                        nc.tensor.matmul(ps[6 + q % 2][:, 0:n * P], ones[:, :], h_cols[:, 1, t * P:(t + n) * P], start=True, stop=True
                                         ).then_inc(z_made.sem, 1)

                    inverses(0)
                    inverses(1)
                    for q, (t, n) in enumerate(QUADS):
                        cols = slice(t * P, (t + n) * P)
                        pe.wait_ge(m_ready.sem, m_ready.at(q + 1))
                        for f in range(H2):
                            k = q * H2 + f
                            if k >= 6:
                                pe.wait_ge(taken_s.sem, taken_s.at(k - 5))
                            nc.tensor.matmul(ps[k % 6][:, 0:n * P], w1lr[:, 0, f * D:(f + 1) * D], m_cols[:, cols], start=True, stop=False)
                            nc.tensor.matmul(ps[k % 6][:, 0:n * P], w1lr[:, 1, f * D:(f + 1) * D], h_cols[:, 0, cols],
                                             start=False, stop=True).then_inc(made_t.sem, 1)
                        if q + 2 < n_quads:
                            inverses(q + 2)
                    for q, (t, n) in enumerate(QUADS):
                        pe.wait_ge(cols_ready.sem, cols_ready.at(H2 * (q + 1)))
                        if q >= 4:
                            pe.wait_ge(taken_v.sem, taken_v.at(q - 3))
                        for i in range(n):
                            for f in range(H2):
                                last = nc.tensor.matmul(ps[q % 4][:, i * P:(i + 1) * P], h_cols[:, f, (t + i) * P:(t + i + 1) * P],
                                                        w2lr[:, f, 0:D], start=(f == 0), stop=(f == H2 - 1))
                        last.then_inc(turned.sem, 1)

                @block.scalar
                def _(act):
                    nc.scalar.preload_act_table_set("natural_log_exp_and_others")
                    for q, (t, n) in enumerate(QUADS):
                        for f in range(H2):
                            k = q * H2 + f
                            act.wait_ge(made_t.sem, made_t.at(k + 1))
                            nc.scalar.activation(before[f][:, t * P:(t + n) * P], ps[k % 6][:, 0:n * P], ACT.Identity,
                                                 bias=bn_vec[:, 0, f:f + 1]).then_inc(taken_s.sem, 1)
                    act.wait_ge(x_ready.sem, x_ready.at(1))
                    nc.scalar.activation(ln_std[:, 0:H2], mean_var[:, 0:H2, 1], ACT.Ln, bias=eps_t[:, :]).then_inc(chain_s.sem, 1)
                    act.wait_ge(chain_s.sem, chain_s.at(1))
                    nc.scalar.activation(ln_std[:, 0:H2], ln_std[:, 0:H2], ACT.Exp, scale=-0.5).then_inc(scale_ready.sem, 1)
                    act.wait_ge(shift_ready.sem, shift_ready.at(1))
                    for q, (t, n) in enumerate(QUADS):
                        cols = slice(t * P, (t + n) * P)
                        for f in range(H2):
                            nc.scalar.activation(h_cols[:, f, cols], before[f][:, cols], ACT.Relu, bias=ln_shift[:, f:f + 1],
                                                 scale=ln_scale[:, f:f + 1]).then_inc(cols_ready.sem, 1)

                @block.vector
                def _(dve):
                    def means(q):
                        t, n = QUADS[q]
                        cols = slice(t * P, (t + n) * P)
                        dve.wait_ge(z_made.sem, z_made.at(q + 1))
                        nc.vector.tensor_tensor(m_cols[:, cols], agg[:, 0, cols], ps[6 + q % 2][:, 0:n * P], ALU.mult
                                                ).then_inc(m_ready.sem, 1)

                    dve.wait_ge(add_made.sem, add_made.at(1))
                    link(nc.vector.tensor_scalar(inv_count[:, :], ps[7][:, 0:N_TILES], 1.0, None, ALU.max), chain_v, dve)
                    link(nc.vector.reciprocal(inv_count[:, :], inv_count[:, :]), chain_v, dve)
                    for q, (t, n) in enumerate(QUADS):
                        eye = ident[:, :].rearrange("p (o c) -> p o c", o=1).broadcast_to([P, n, P])
                        inv = inv_count[:, t:t + n].rearrange("p (t o) -> p t o", o=1).broadcast_to([P, n, P])
                        nc.vector.tensor_tensor(h_cols[:, 1, t * P:(t + n) * P].rearrange("p (t c) -> p t c", c=P), eye, inv, ALU.mult
                                                ).then_inc(capped_z.sem, 1)
                        if q >= 1:
                            means(q - 1)
                    means(n_quads - 1)
                    for i, (c, n) in enumerate(pieces):
                        for f in range(H2):
                            dve.wait_ge(taken_s.sem, taken_s.at(i * H2 + f + 1))
                            last = nc.vector.bn_stats(stats[:, f * len(pieces) + i, :], before[f][:, c:c + n])
                    link(last, chain_v, dve)
                    for f in range(H2):
                        last = nc.vector.bn_aggr(mean_var[:, f, :], stats[:, f * len(pieces):(f + 1) * len(pieces), :]
                                                 .rearrange("p s k -> p (s k)"))
                    last.then_inc(x_ready.sem, 1)
                    dve.wait_ge(scale_ready.sem, scale_ready.at(1))
                    link(nc.vector.tensor_tensor(ln_scale[:, 0:H2], ln_std[:, 0:H2], bn_vec[:, 1, :], ALU.mult), chain_v, dve)
                    link(nc.vector.tensor_tensor(ln_shift[:, 0:H2], mean_var[:, 0:H2, 0], ln_scale[:, 0:H2], ALU.mult), chain_v, dve)
                    nc.vector.tensor_tensor(ln_shift[:, 0:H2], bn_vec[:, 2, :], ln_shift[:, 0:H2], ALU.subtract).then_inc(shift_ready.sem, 1)
                    for q, (t, n) in enumerate(QUADS):
                        cols = slice(t * P, (t + n) * P)
                        dve.wait_ge(turned.sem, turned.at(q + 1))
                        nc.vector.tensor_copy(before[0][:, cols], ps[q % 4][:, 0:n * P]).then_inc(taken_v.sem, 1)

                @block.gpsimd
                def _(pool):
                    pool.wait_ge(m_ready.sem, m_ready.at(n_quads))
                    nc.gpsimd.memset(agg[:, 0, :], 0.0)

                @block.sync
                def _(sp):
                    rows_out = table.rearrange("(t p) f -> p t f", p=P)
                    for q0, q1 in ((0, 3), (3, 6), (6, 7)):
                        t0, t1 = QUADS[q0][0], QUADS[q1 - 1][0] + QUADS[q1 - 1][1]
                        sp.wait_ge(taken_v.sem, taken_v.at(q1))
                        sp.dma_start(rows_out[:, t0:t1, :], h_rows[:, t0:t1, :]).then_inc(stored.sem, 16)
                    sp.wait_ge(stored.sem, stored.at(48))
            for t, n in ((m_ready, n_quads), (made_t, H2 * n_quads), (taken_s, H2 * n_quads), (cols_ready, H2 * n_quads),
                         (turned, n_quads), (taken_v, n_quads), (chain_s, 1), (x_ready, 1), (scale_ready, 1), (shift_ready, 1),
                         (stored, 48), (z_made, n_quads), (capped_z, n_quads), (add_made, 1)):
                t.passed(n)

        def aside_vector(dve):
            link(nc.vector.tensor_scalar(cyc, e_weight[:, :], 1.0 / 20.0, None, ALU.mult), chain_v, dve)
            link(nc.vector.tensor_scalar(cyc_round, cyc, 12582912.0, None, ALU.add), chain_v, dve)
            link(nc.vector.tensor_scalar(cyc_round, cyc_round, 12582912.0, None, ALU.subtract), chain_v, dve)
            nc.vector.tensor_tensor(cyc, cyc, cyc_round, ALU.subtract).then_inc(input_v.sem, 1)
            dve.wait_ge(edges_in.sem, edges_in.at(16))
            link(nc.vector.tensor_scalar(rel_idx[:, :], src_idx[:, :], float(N_REL), None, ALU.mult), chain_v, dve)
            link(nc.vector.tensor_tensor(rel_idx[:, :], rel_idx[:, :], type_i, ALU.add), chain_v, dve)
            rest = e_weight[:, 0:(A_GROUPS + B_MADE) * GROUP]
            for k in range(3):
                link(nc.vector.tensor_copy(a_weight_b[:, :], rest), chain_v, dve)
                link(nc.vector.tensor_copy(a_weight[:, k, :], a_weight_b[:, :]), chain_v, dve)
                if k < 2:
                    temp = a_temp[:, 0:(A_GROUPS + B_MADE) * GROUP]
                    link(nc.vector.tensor_tensor(temp, rest, a_weight[:, k, :], ALU.subtract), chain_v, dve)
                    rest = temp
            dve.wait_ge(taken_s.sem, taken_s.at(1))
            link(nc.vector.tensor_tensor(cyc, cyc, cyc, ALU.mult), chain_v, dve)
            link(nc.vector.tensor_scalar(e_cut[:, :], cyc, -1.0, 1.0, ALU.mult, ALU.add), chain_v, dve)
            dve.wait_ge(made_t.sem, made_t.at(len(QUADS) + 1))
            link(nc.vector.scalar_tensor_tensor(row_vecs[:, MLP_B2, :], ps[7][:, 0:D], -LN2, row_vecs[:, MLP_B2, :],
                                                ALU.mult, ALU.add), chain_v, dve)
            link(nc.vector.scalar_tensor_tensor(row_vecs[:, LIN_B, :], ps[7][:, D:2 * D], -LN2, row_vecs[:, LIN_B, :],
                                                ALU.mult, ALU.add), chain_v, dve)
            rest = row_vecs[:, MLP_B2, :]
            for k in range(3):
                link(nc.vector.tensor_copy(b2_split[:, k, :], rest), chain_v, dve)
                link(nc.vector.tensor_copy(b2_parts[:, k, :], b2_split[:, k, :]), chain_v, dve)
                if k < 2:
                    link(nc.vector.tensor_tensor(b2_left[:, k, :], rest, b2_parts[:, k, :], ALU.subtract), chain_v, dve)
                    rest = b2_left[:, k, :]
            link(nc.vector.tensor_scalar(b2_left[:, 0, :], b2_parts[:, 0, :], ident[:, 0:1], None, ALU.mult), chain_v, dve)
            for k in (1, 2):
                link(nc.vector.scalar_tensor_tensor(b2_left[:, k % 2, :], b2_parts[:, k, :], ident[:, k:k + 1],
                                                    b2_left[:, (k - 1) % 2, :], ALU.mult, ALU.add), chain_v, dve)
            for j in range(GROUP):
                last = nc.vector.tensor_copy(b2_split[:, j, :], b2_left[:, 0, :])
            link(last, chain_v, dve)

        def aside_scalar(act):
            act.wait_ge(input_v.sem, input_v.at(1))
            nc.scalar.activation(cyc, cyc, ACT.Sin, scale=float(np.pi)).then_inc(taken_s.sem, 1)

        def aside_tensor(pe):
            pe.wait_ge(taken_v.sem, taken_v.at(len(QUADS)))
            nc.tensor.matmul(ps[7][:, 0:D], ones[:, :], sq_w[:, MLP2, :], start=True, stop=True)
            nc.tensor.matmul(ps[7][:, D:2 * D], ones[:, :], sq_w[:, LIN, :], start=True, stop=True).then_inc(made_t.sem, 1)

        rounds, spared, hots_ahead = [0], [0], [0]
        columns = [nc.vector.alloc_register(f"column{s}") for s in range(SLOTS)]
        further = nc.vector.alloc_register("further")
        turn_register = nc.vector.alloc_register("turn_register")
        a_columns = [nc.vector.alloc_register(f"a_column{m}") for m in range(A_PER_TURN)]

        def edge_round(source, indices, weights=None, counts=False, filters=False, add_rows=None, start=None, residual=False,
                       by_adjacency=0, build=None, sections=((None, True, None),), save_adjacency=False, load_before=None):
            r, before = rounds[0], spared[0]
            rounds[0] += 1
            spared[0] += by_adjacency > 0
            hots_before = hots_ahead[0]
            hots_ahead[0] += 2 if filters else 1
            SUMS, W_BANK, Z_BANK = (ps[0], ps[1]), (ps[2], ps[3]), ps[4:8]
            ADJ, A_COUNTS, PRODUCT = (ps[2], ps[3]), (ps[4], ps[5]), (ps[4], ps[5])
            planes = 2 if counts else 1
            kind, per_turn, a_first = build if build else (0, 0, 0)
            w_first = a_first if a_first < A_MADE else A_GROUPS + a_first - A_MADE
            a_adds = 2 if counts else 1
            a_pairs, a_made, a_added, a_links = pairs_ready[kind], adj_made[kind], adj_added[kind], hots_linked[kind]
            a_turn = 0 if sections[0][1] else sections[0][0]
            aside = any(after == "aside" for _, _, after in sections)
            products = [after for _, _, after in sections if after and after != "aside"]
            half = A_COLS // 2

            def more_windows(eng):
                return eng.value_load(more_i[0:1, 0:1], min_val=0, max_val=NODES // WIN)

            def turns_of(eng):
                left = eng.value_load(turns_i[0:1, 1:2], min_val=TURNS - A_TURNS - A_TAIL, max_val=TURNS - A_TAIL) + A_TAIL
                done = left * (SLOTS * before) + (r - before) * N_GROUPS
                if not by_adjacency:
                    return 0, TURNS, done
                most = A_TURNS
                if by_adjacency == 2:
                    most += B_TURNS
                    left = eng.value_load(turns_i[0:1, 3:4], min_val=TURNS - most, max_val=TURNS)
                k = 2 * (by_adjacency - 1)
                skip = eng.value_load(turns_i[0:1, k:k + 1], min_val=0, max_val=most)
                return skip, left, done

            def parts(left):
                at, from_end = 0, False
                for end, puts, after in sections:
                    if end is None:
                        end = 0
                        to_end = True
                    else:
                        to_end = end < 0
                    first = left + at if from_end else at
                    n = end - at if to_end == from_end else left + (end - at)
                    yield first, n, puts, after
                    at, from_end = end, to_end

            def sum_of(bank):
                return bank[:, 0:planes * WIN].rearrange("p (a w) -> p a w", w=WIN)

            with nc.Block() as block:
                @block.gpsimd
                def _(pool):
                    skip, left, done = turns_of(pool)
                    with pool.Fori(0, left) as turn:
                        for s in range(SLOTS):
                            pool.wait_ge(idx_ready.sem, turn * SLOTS + done + (r * SLOTS + s + 1))
                            pool.sem_inc(turn_begun.sem, 1)
                            for j in range(GROUP):
                                nc.gpsimd.indirect_dma_start(rows[:, s, j, :], None, source,
                                                             bass.IndirectOffsetOnAxis(ap=cur_idx[:, s, j:j + 1], axis=0)
                                                             ).then_inc(gathered[s].sem, 16)

                if filters:
                    @block.sync
                    def _(sp):
                        cols = a["attr_cols"]
                        for s in range(SLOTS):
                            sp.dma_start(attr[:, s, :], cols[:, s * G_EDGES:(s + 1) * G_EDGES]).then_inc(attr_in[s].sem, 16)
                        with sp.Fori(1, ATTR_TURNS) as turn:
                            for s in range(SLOTS):
                                sp.wait_ge(z_ready.sem, turn * SLOTS + (s + 1 - SLOTS))
                                sp.dma_start(attr[:, s, :], cols[:, bass.ds(turn * (SLOTS * G_EDGES) + s * G_EDGES, G_EDGES)]
                                             ).then_inc(attr_in[s].sem, 16)
                        for s in range(SLOTS):
                            sp.wait_ge(attr_in[s].sem, 16 * ATTR_TURNS)

                @block.tensor
                def _(pe):
                    more = more_windows(pe)
                    skip, left, done = turns_of(pe)
                    if start:
                        for q, (t, n) in enumerate(QUADS):
                            if q >= 2:
                                pe.wait_ge(taken_s.sem, taken_s.at(q - 1))
                            nc.tensor.matmul(ps[6 + q % 2][:, 0:n * P], start[0], h_cols[:, 0, t * P:(t + n) * P], start=True, stop=True
                                             ).then_inc(made_t.sem, 1)
                    if residual:
                        for q, (t, n) in enumerate(QUADS):
                            if q >= 2:
                                pe.wait_ge(taken_v.sem, taken_v.at(q - 1))
                            for i in range(n):
                                for f in range(H2):
                                    last = nc.tensor.matmul(ps[6 + q % 2][:, i * P:(i + 1) * P], h_cols[:, f, (t + i) * P:(t + i + 1) * P],
                                                            w2lr[:, f, D:2 * D], start=(f == 0), stop=(f == H2 - 1))
                            last.then_inc(made_t.sem, 1)

                    def first_layer(slot, load):
                        pe.wait_ge(attr_in[slot].sem, load * 16)
                        nc.tensor.matmul(Z_BANK[slot][:, :], mlp_w1[:, :], attr[:, slot, :], start=True, stop=True
                                         ).then_inc(z_ready.sem, 1)

                    def second_layer(slot, filt_count):
                        pe.wait_ge(filt_ready.sem, filt_count)
                        for j in range(GROUP):
                            wj = W_BANK[slot % 2][:, j * D:(j + 1) * D]
                            nc.tensor.matmul(wj, filt[:, slot, j * P:(j + 1) * P], sq_w[:, MLP2, :], start=True, stop=False)
                            last = nc.tensor.matmul(wj, three_ones[:, :], b2_split[:, j, :], start=False, stop=True)
                        last.then_inc(w_ready.sem, 1)

                    def sums(s, hot, hot_for_counts, into, done):
                        for j in range(GROUP):
                            last = nc.tensor.matmul(into[:, 0:WIN], rows[:, s, j, :], hot[:, j, :], start=(j == 0), stop=(j == GROUP - 1))
                        if counts:
                            for j in range(GROUP):
                                last = nc.tensor.matmul(into[:, WIN:2 * WIN], hot_for_counts[0][:, :], hot_for_counts[1][:, j, :],
                                                        start=(j == 0), stop=(j == GROUP - 1))
                        last.then_inc(done.sem, 1)

                    def scatter(turn, s):
                        if filters:
                            pe.wait_ge(weighed.sem, turn * SLOTS + (s + 1))
                        else:
                            pe.wait_ge(gathered[s].sem, (turn * SLOTS + done) * 16 + 16 * GROUP)
                        pe.wait_ge(onehot_ready.sem, turn * SLOTS + done + (hots_before + s + 1))
                        if counts:
                            pe.wait_ge(onehot_b_ready.sem, turn * SLOTS + (s + 1))
                        sums(s, onehot[:, s % 2, :, :], (ones_b, onehot_b[:, s % 2, :, :]), SUMS[s % 2], scattered)
                        with pe.If(more > 0):
                            with pe.Fori(0, more) as w:
                                n = (turn * SLOTS + done + s) * more + w
                                pe.wait_ge(more_hot.sem, n + 1)
                                sums(s, hot_more[:, :, :], (ones, hot_more[:, :, :]), SUMS[s % 2], more_sums)

                    def join_pairs(turn, m):
                        if kind:
                            pe.wait_ge(weights_hot.sem, turn * per_turn + (weights_hot.value - a_turn * per_turn + m + 1))
                        pe.wait_ge(a_pairs.sem, turn * per_turn + (a_pairs.value - a_turn * per_turn + m + 1))
                        for j in range(GROUP):
                            pairs = pair_hot[m % 2][:, j, :, :].rearrange("p t w -> p (t w)")
                            for k in range(3 if kind else 1):
                                part = weight_hot[m][:, k, j, :] if kind else part_hot[m % 2][:, j, :]
                                last = nc.tensor.matmul(ADJ[m % 2][:, 0:N_TILES * A_WIN], part, pairs, start=(j == 0 and k == 0),
                                                        stop=(j == GROUP - 1 and k == (2 if kind else 0)))
                        if counts:
                            for j in range(GROUP):
                                last = nc.tensor.matmul(A_COUNTS[m % 2][:, 0:A_WIN], ones_b[:, :], dst_hot[:, m % 2, j, :],
                                                        start=(j == 0), stop=(j == GROUP - 1))
                        last.then_inc(a_made.sem, 1)

                    def product(k, which):
                        if k >= 2:
                            pe.wait_ge(product_added.sem, product_added.at(k - 1))
                        for t in range(N_TILES):
                            last = nc.tensor.matmul(PRODUCT[k % 2][:, 0:half], h_rows[:, t, :], adj[:, t, which * half:(which + 1) * half],
                                                    start=(t == 0), stop=(t == N_TILES - 1))
                        last.then_inc(product_made.sem, 1)

                    if filters:
                        for s in range(SLOTS):
                            first_layer(s, 1)
                        for s in range(2):
                            second_layer(s, s + 1)
                            first_layer(s, 2)
                    k = 0
                    for at, turns, puts, after in parts(left):
                        with pe.Fori(0, turns) as loop:
                            turn = loop + at
                            for pair in range(0, SLOTS, 2):
                                for s in (pair, pair + 1):
                                    scatter(turn, s)
                                    if build and puts and 1 <= s <= per_turn:
                                        join_pairs(turn, s - 1)
                                if filters:
                                    for s in (pair + 2, pair + 3):
                                        second_layer(s % SLOTS, turn * SLOTS + (s + 1))
                                    for s in (pair + 2, pair + 3):
                                        first_layer(s % SLOTS, turn + (2 if s < SLOTS else 3))
                        at = at + turns
                        if after == "aside":
                            aside_tensor(pe)
                        elif after:
                            if build and puts:
                                pe.wait_ge(a_added.sem, at * (per_turn * a_adds) + a_added.value)
                            if k == load_before:
                                pe.wait_ge(adj_back.sem, 16)
                            product(k, after[0])
                            k += 1

                if aside:
                    @block.sync
                    def _(sp):
                        sp.dma_start(type_i, a["type_cols"]).then_inc(edges_in.sem, 16)

                    @block.scalar
                    def _(act):
                        aside_scalar(act)

                if counts:
                    @block.scalar
                    def _(act):
                        skip, left, done = turns_of(act)
                        with act.Fori(0, left) as turn:
                            for s in range(SLOTS):
                                act.wait_ge(onehot_ready.sem, turn * SLOTS + (s + 1))
                                nc.scalar.copy(onehot_b[:, s % 2, :, :], onehot[:, s % 2, :, :]).then_inc(onehot_b_ready.sem, 1)

                if save_adjacency or load_before:
                    @block.sync
                    def _(sp):
                        if save_adjacency:
                            sp.dma_start(adj_dram[:, :], adj_mem[:, :]).then_inc(adj_saved.sem, 16)
                            sp.wait_ge(adj_saved.sem, 16)
                        if load_before:
                            sp.wait_ge(product_made.sem, product_made.at(load_before))
                            sp.dma_start(adj_mem[:, :], adj_dram[:, :]).then_inc(adj_back.sem, 16)
                            sp.wait_ge(adj_back.sem, 16)

                if start:
                    @block.scalar
                    def _(act):
                        for q, (t, n) in enumerate(QUADS):
                            act.wait_ge(made_t.sem, made_t.at(q + 1))
                            nc.scalar.activation(agg[:, 0, t * P:(t + n) * P], ps[6 + q % 2][:, 0:n * P], ACT.Identity,
                                                 bias=start[1], scale=start[2]).then_inc(taken_s.sem, 1)
                        if save_adjacency:
                            act.wait_ge(adj_saved.sem, 16)
                            nc.scalar.copy(adj_mem[:, :], zero_t[:, :].broadcast_to([P, N_TILES * A_COLS])).then_inc(adj_cleared.sem, 1)
                        if kind:
                            with act.Fori(0, TURNS - a_turn) as loop:
                                for m in range(per_turn):
                                    act.wait_ge(a_links.sem, loop * (2 * per_turn) + (a_links.value + 2 * m + 2))
                                    for k in range(3):
                                        for j in range(GROUP):
                                            edge = bass.ds((loop * per_turn + (w_first + m)) * GROUP + j, 1)
                                            last = nc.scalar.activation(weight_hot[m][:, k, j, :], part_hot[m % 2][:, j, :], ACT.Copy,
                                                                        scale=a_weight[:, k, edge])
                                    last.then_inc(weights_hot.sem, 1)

                if filters:
                    @block.scalar
                    def _(act):
                        nc.scalar.preload_act_table_set("natural_log_exp_and_others")

                        def logs(parity, count):
                            act.wait_ge(z_capped.sem, count)
                            nc.scalar.activation(soft[:, parity, :], soft[:, parity, :], ACT.Exp).then_inc(exp_ready.sem, 1)
                            act.wait_ge(exp_ready.sem, count)
                            nc.scalar.activation(soft[:, parity, :], soft[:, parity, :], ACT.Ln, bias=ones[:, 0:1]
                                                 ).then_inc(ln_ready.sem, 1)

                        for s in range(SLOTS):
                            logs(s % 2, s + 1)
                        with act.Fori(1, TURNS + 1) as turn:
                            for s in range(SLOTS):
                                logs(s % 2, turn * SLOTS + (s + 1))

                @block.vector
                def _(dve):
                    more = more_windows(dve)
                    skip, left, done = turns_of(dve)
                    for s in range(SLOTS):
                        nc.vector.tensor_copy(cur_idx[:, s, :], indices[:, bass.ds(skip * (SLOTS * GROUP) + s * GROUP, GROUP)]
                                              ).then_inc(idx_ready.sem, 1)
                    if add_rows is not None:
                        row = row_vecs[:, add_rows, :].rearrange("p (o f) -> p o f", o=1).broadcast_to([P, N_TILES, D])
                        nc.vector.tensor_tensor(x_rows[:, :, :], x_rows[:, :, :], row, ALU.add)
                    if residual:
                        for q, (t, n) in enumerate(QUADS):
                            dve.wait_ge(made_t.sem, made_t.at(q + 1))
                            xs = x_rows[:, t:t + n, :].rearrange("p t f -> p (t f)")
                            nc.vector.tensor_tensor(xs, xs, ps[6 + q % 2][:, 0:n * P], ALU.add).then_inc(taken_v.sem, 1)

                    def one_hots(hot, window, edges, group, weight_group=None):
                        if weights is None:
                            off = edges[:, bass.ds(group * GROUP, GROUP)].rearrange("p (j o) -> p j o", o=1)
                            last = nc.vector.tensor_tensor(hot, window.rearrange("p (o c) -> p o c", o=1).broadcast_to([P, GROUP, WIN]),
                                                           off.broadcast_to([P, GROUP, WIN]), ALU.is_equal)
                        else:
                            weight_at = (group if weight_group is None else weight_group) * GROUP
                            for j in range(GROUP):
                                edge = bass.ds(group * GROUP + j, 1)
                                last = nc.vector.tensor_scalar(hot[:, j, :], window, edges[:, edge], weights[:, bass.ds(weight_at + j, 1)],
                                                               ALU.is_equal, ALU.mult)
                        return last

                    def cap(slot, count, first=False):
                        dve.wait_ge(z_ready.sem, count)
                        if not first:
                            dve.wait_ge(filt_ready.sem, count - 2)
                        nc.vector.tensor_scalar(soft[:, slot % 2, :], Z_BANK[slot][:, :], vecs[:, MLP_B1:MLP_B1 + 1], EXP_CAP,
                                                ALU.add, ALU.min).then_inc(z_capped.sem, 1)

                    def softplus(slot, count):
                        dve.wait_ge(ln_ready.sem, count)
                        nc.vector.scalar_tensor_tensor(filt[:, slot, :], Z_BANK[slot][:, :], vecs[:, MLP_B1:MLP_B1 + 1],
                                                       soft[:, slot % 2, :], ALU.add, ALU.max).then_inc(filt_ready.sem, 1)

                    def weigh(turn, s):
                        dve.wait_ge(w_ready.sem, turn * SLOTS + (s + 1))
                        dve.wait_ge(gathered[s].sem, (turn * SLOTS + done) * 16 + 16 * GROUP)
                        msg = rows[:, s, :, :].rearrange("p j f -> p (j f)")
                        nc.vector.tensor_tensor(msg, msg, W_BANK[s % 2][:, :], ALU.mult).then_inc(weighed.sem, 1)

                    def next_one_hots(turn, at_turn, s):
                        one_hots(onehot[:, s % 2, :, :], iota_f[:, 0:WIN], dst_rel, at_turn * SLOTS + s).then_inc(onehot_ready.sem, 1)

                    def add_sums(turn, at_turn, s, putting=False):
                        column = dve.snap(columns[s], min_val=0, max_val=NODES)
                        dve.wait_ge(scattered.sem, turn * SLOTS + done + (s + 1))
                        dve.wait_ge(summed.sem, turn * SLOTS + done + (s + 1))
                        if putting and counts:
                            dve.wait_ge(a_added.sem, (turn * per_turn + max(s - 1, 0)) * a_adds + a_added.value)
                        into = agg[:, 0:planes, bass.ds(column, WIN)]
                        nc.vector.tensor_tensor(into, into, sum_of(SUMS[s % 2]), ALU.add).then_inc(summed.sem, 1)
                        with dve.If(more > 0):
                            first_more = (turn * SLOTS + done + s) * more
                            first_rel = (turn * SLOTS + done + s) * (more + 1)
                            nc.vector.tensor_scalar(further_rel[:, :], dst_rel[:, bass.ds(at_turn * (SLOTS * GROUP) + s * GROUP, GROUP)],
                                                    float(WIN), None, ALU.subtract).then_inc(more_rel.sem, 1)
                            with dve.Fori(0, more) as w:
                                dve.wait_ge(more_rel.sem, first_rel + w + 1)
                                one_hots(hot_more[:, :, :], iota_f[:, 0:WIN], further_rel, 0,
                                         at_turn * SLOTS + s).then_inc(more_hot.sem, 1)
                                dve.reg_alu(further, columns[s], (w + 1) * WIN, ALU.add)
                                dve.reg_alu(further, further, NODES, ALU.min)
                                column = dve.snap(further, min_val=0, max_val=NODES)
                                dve.wait_ge(more_sums.sem, first_more + w + 1)
                                into = agg[:, 0:planes, bass.ds(column, WIN)]
                                nc.vector.tensor_tensor(into, into, sum_of(SUMS[s % 2]), ALU.add).then_inc(more_summed.sem, 1)
                                nc.vector.tensor_scalar(further_rel[:, :], further_rel[:, :], float(WIN), None, ALU.subtract
                                                        ).then_inc(more_rel.sem, 1)
                                dve.wait_ge(more_summed.sem, first_more + w + 1)
                                dve.wait_ge(more_rel.sem, first_rel + w + 2)
                        nc.vector.tensor_copy(cur_idx[:, s, :], indices[:, bass.ds(at_turn * (SLOTS * GROUP) + (s + SLOTS) * GROUP, GROUP)]
                                              ).then_inc(idx_ready.sem, 1)

                    def pair_one_hots(turn, m):
                        at = bass.ds((loop * per_turn + (a_first + m)) * GROUP, GROUP)

                        def hot(into, edges, n):
                            off = edges.rearrange("p (j o) -> p j o", o=1).broadcast_to([P, GROUP, n])
                            return nc.vector.tensor_tensor(into, iota_b[:, 0:n].rearrange("p (o c) -> p o c", o=1).broadcast_to([P, GROUP, n]),
                                                           off, ALU.is_equal)

                        n_hots = turn * (2 * per_turn) + (a_links.value - a_turn * 2 * per_turn + 2 * m)
                        hot(tile_hot[:, m % 2, :, :], a_src_tile[:, at], N_TILES)
                        hot(dst_hot[:, m % 2, :, :], a_dst_rel[:, at], A_WIN).then_inc(a_links.sem, 1)
                        hot(part_hot[m % 2], a_src_part[:, at], P).then_inc(a_links.sem, 1)
                        dve.wait_ge(a_links.sem, n_hots + 1)
                        pairs = nc.vector.tensor_tensor(
                            pair_hot[m % 2],
                            tile_hot[:, m % 2, :, :].rearrange("p j (t o) -> p j t o", o=1).broadcast_to([P, GROUP, N_TILES, A_WIN]),
                            dst_hot[:, m % 2, :, :].rearrange("p j (o w) -> p j o w", o=1).broadcast_to([P, GROUP, N_TILES, A_WIN]), ALU.mult)
                        pairs.then_inc(a_pairs.sem, 1)

                    def add_pairs(turn, m):
                        column = dve.snap(a_columns[m], min_val=0, max_val=A_COLS - A_WIN)
                        dve.wait_ge(a_made.sem, turn * per_turn + (a_made.value - a_turn * per_turn + m + 1))
                        dve.wait_ge(a_added.sem, turn * (per_turn * a_adds) + (a_added.value + (m - a_turn * per_turn) * a_adds))
                        into = adj[:, :, bass.ds(column, A_WIN)]
                        nc.vector.tensor_tensor(into, into, ADJ[m % 2][:, 0:N_TILES * A_WIN].rearrange("p (t w) -> p t w", w=A_WIN), ALU.add
                                                ).then_inc(a_added.sem, 1)
                        if counts:
                            dve.wait_ge(summed.sem, turn * SLOTS + done + (m + 3))
                            into = agg[:, 1, bass.ds(column, A_WIN)]
                            nc.vector.tensor_tensor(into, into, A_COUNTS[m % 2][:, 0:A_WIN], ALU.add).then_inc(a_added.sem, 1)

                    def add_product(k, which, first):
                        dve.wait_ge(product_made.sem, product_made.at(k + 1))
                        into = agg[:, 0, first + which * half:first + (which + 1) * half]
                        nc.vector.tensor_tensor(into, into, PRODUCT[k % 2][:, 0:half], ALU.add).then_inc(product_added.sem, 1)
                        dve.wait_ge(product_added.sem, product_added.at(k + 1))

                    if filters:
                        cap(0, 1, first=True)
                        cap(1, 2, first=True)
                        softplus(0, 1)
                        cap(2, 3)
                        softplus(1, 2)
                        cap(3, 4)
                        softplus(2, 3)
                        softplus(3, 4)
                        for s in range(2):
                            next_one_hots(0, skip, s)
                    else:
                        next_one_hots(0, skip, 0)
                    if start:
                        dve.wait_ge(taken_s.sem, taken_s.at(len(QUADS)))
                    k = 0
                    for at, turns, puts, after in parts(left):
                        puts = puts and build
                        with dve.Fori(0, turns) as loop:
                            turn = loop + at
                            at_turn = turn
                            if by_adjacency:
                                dve.reg_alu(turn_register, turn, skip, ALU.add)
                                at_turn = dve.snap(turn_register, min_val=0, max_val=TURNS - 1)
                            dve.load(columns, base_i[0:1, bass.ds(at_turn * SLOTS, SLOTS)])
                            if puts:
                                dve.load(a_columns[0:per_turn], a_base_i[0:1, bass.ds(loop * per_turn + a_first, per_turn)])
                            for pair in range(0, SLOTS, 2):
                                if filters:
                                    weigh(turn, pair)
                                    weigh(turn, pair + 1)
                                    cap(pair, turn * SLOTS + (pair + 1 + SLOTS))
                                    cap(pair + 1, turn * SLOTS + (pair + 2 + SLOTS))
                                    add_sums(turn, at_turn, pair)
                                    next_one_hots(turn, at_turn, pair + 2)
                                    add_sums(turn, at_turn, pair + 1)
                                    next_one_hots(turn, at_turn, pair + 3)
                                    softplus(pair, turn * SLOTS + (pair + 1 + SLOTS))
                                    softplus(pair + 1, turn * SLOTS + (pair + 2 + SLOTS))
                                else:
                                    for s in (pair, pair + 1):
                                        next_one_hots(turn, at_turn, s + 1)
                                        if puts and 2 <= s <= per_turn + 1:
                                            add_pairs(turn, s - 2)
                                        add_sums(turn, at_turn, s, puts)
                                        if puts and s < per_turn:
                                            pair_one_hots(turn, s)
                            if puts and per_turn == SLOTS - 1:
                                add_pairs(turn, per_turn - 1)
                        at = at + turns
                        if puts and counts:
                            dve.wait_ge(a_added.sem, at * (per_turn * a_adds) + a_added.value)
                        if not puts and build and save_adjacency:
                            dve.wait_ge(adj_cleared.sem, 1)
                        if after == "aside":
                            aside_vector(dve)
                        elif after:
                            dve.wait_ge(summed.sem, at * SLOTS + done + 1)
                            add_product(k, *after)
                            k += 1
            product_made.passed(len(products))
            product_added.passed(len(products))
            if build and not by_adjacency:
                a_groups = per_turn * (TURNS - a_turn)
                a_links.passed(2 * a_groups)
                a_pairs.passed(a_groups)
                weights_hot.passed(a_groups if kind else 0)
                a_made.passed(a_groups)
                a_added.passed(a_groups * a_adds)
            made_t.passed(len(QUADS) if start or residual else 0)
            taken_s.passed(len(QUADS) if start else 0)
            taken_v.passed(len(QUADS) if residual else 0)
            if aside:
                for t, n in ((edges_in, 16), (input_v, 1), (taken_s, 1), (made_t, 1)):
                    t.passed(n)

        prepare()
        node_phase(h_table=True, clear_first=True)
        edge_round(table, src_idx, counts=True, add_rows=L0_B2, by_adjacency=1, build=(0, A_PER_TURN, 0),
                   sections=((-A_TAIL, True, (0, 0)), (-A_TAIL // 2, False, (1, 0)), (None, False, None)))
        sage_hidden()
        edge_round(table, src_idx, residual=True, by_adjacency=1,
                   sections=((2, False, (0, 0)), (4, False, (1, 0)), (8, False, "aside"), (None, False, None)))
        node_phase(front="mean", residual=ident, weight=sq_w[:, LIN1, :], clear=True)
        edge_round(table, src_idx, weights=e_cut, filters=True, add_rows=LIN_B)
        node_phase(front="softplus", residual=sq_w[:, LIN, :], layer=0, clear_adjacency=True)
        edge_round(rel_table, rel_idx, start=(sq_w[:, SL1, :], vecs[:, R_B1:R_B1 + 1], 1.0), build=(1, 2, 0))
        node_phase(front="relu", norm=False, layer=1)
        edge_round(rel_table, rel_idx, start=(sq_w[:, SL2, :], vecs[:, R_B2:R_B2 + 1], 1.0), build=(1, 1, A_MADE),
                   save_adjacency=True, sections=((B_HEAD, False, None), (None, True, None)))
        node_phase(front="relu", residual=ident, weight=sq_w[:, KER, :])
        edge_round(table, src_idx, weights=e_weight, start=(sq_w[:, KER, :], vecs[:, BIAS:BIAS + 1], vecs[:, SKIP:SKIP + 1]), by_adjacency=2,
                   load_before=2, sections=((2, False, (0, B_FIRST)), (4, False, (1, B_FIRST)), (8, False, (0, 0)), (10, False, (1, 0)),
                                            (None, False, None)))
        node_phase(front="selu", residual=ident, norm=False, to_out=True)


_DIRECT = ['L0_gnn_W1l', 'L0_gnn_b1', 'L0_gnn_W1r', 'L0_gnn_gamma', 'L0_gnn_beta', 'L0_gnn_W2l', 'L0_gnn_b2', 'L0_gnn_W2r',
           'L1_gnn_mlp_w1', 'L1_gnn_mlp_b1', 'L1_gnn_mlp_w2', 'L1_gnn_mlp_b2', 'L1_gnn_lin1_w', 'L1_gnn_lin2_w', 'L1_gnn_lin2_b',
           'L1_gnn_lin_w', 'L1_gnn_lin_b', 'L2_gnn_w1', 'L2_gnn_sl1', 'L2_gnn_b1', 'L2_gnn_w2', 'L2_gnn_sl2', 'L2_gnn_b2',
           'L3_gnn_kernel', 'L3_gnn_bias', 'L3_gnn_skip_weight']


def kernel(**inputs):
    import numpy as _np
    import concourse.bacc as _bacc
    from concourse import mybir as _mybir
    from concourse.bass_utils import run_bass_kernel_spmd as _run

    def padded(name, n, fill):
        v = _np.asarray(inputs[name])
        return _np.concatenate([v, _np.full((n - v.shape[0],) + v.shape[1:], fill, v.dtype)])

    def edge_columns(name, groups, fill):
        return _np.ascontiguousarray(padded(name, groups * G_EDGES, fill).reshape(-1, P).T)

    arrays = {
        "x": padded("x", NODES, 0),
        "dst": padded("dst", EDGES, -1),
        "dst_cols": edge_columns("dst", N_GROUPS, -1),
        "src_cols": edge_columns("src", AHEAD, 0),
        "type_cols": edge_columns("edge_type_8", AHEAD, 0),
        "weight_cols": edge_columns("edge_weight", HOT_AHEAD, 0),
        "attr_cols": _np.ascontiguousarray(padded("edge_attr_50", ATTR_TURNS * SLOTS * G_EDGES, 0).T),
    }
    for name in _DIRECT:
        arrays[name] = _np.ascontiguousarray(inputs[name])
    nc = _bacc.Bacc("TRN2", target_bir_lowering=False, num_devices=1)
    aps = {name: nc.dram_tensor(f"in_{name}", v.shape, _mybir.dt.from_np(v.dtype), kind="ExternalInput").ap()
           for name, v in arrays.items()}
    out = nc.dram_tensor("out_x", (N_NODES, D), _mybir.dt.float32, kind="ExternalOutput").ap()
    build_gnn(nc, aps, out)
    r = _run(nc, [{f"in_{name}": v for name, v in arrays.items()}], core_ids=[0])
    return r.results[0]["out_x"]
```
